# Optimizing a Trainium2 kernel written in Bass

```python
import numpy as np
import jax
import jax.numpy as jnp

def _softmax(x, axis=-1):
    return jax.nn.softmax(x, axis=axis)

def _gelu(x):
    return jax.nn.gelu(x, approximate=True)

def _silu(x):
    return jax.nn.silu(x)

def _sigmoid(x):
    return jax.nn.sigmoid(x)

def _layernorm(x, axis=-1, eps=1e-05):
    m = jnp.mean(x, axis=axis, keepdims=True)
    v = jnp.var(x, axis=axis, keepdims=True)
    return (x - m) / jnp.sqrt(v + eps)

def _scatter_add(tgt, idx, src, axis=0):
    return tgt.at[idx].add(src)

def _segment_sum(src, seg, n):
    return jax.ops.segment_sum(src, seg, n)
kernel_name = 'mk_recurrent_d2_jaxref_r8_65642d'

def setup_inputs(seed: int=0):
    np.random.seed(seed)
    _w = jnp.asarray

    def _L0_attn_setup():
        import jax, jax.numpy as jnp
        import numpy as np
        B, S, E, H = (2, 256, 512, 32)
        D = E // H
        ROPE_BASE = 10000.0
        MASK_VAL = -66504.0

        def _rope(x, cos, sin):
            x1, x2 = jnp.split(x, 2, axis=-1)
            return jnp.concatenate([x1 * cos - x2 * sin, x2 * cos + x1 * sin], axis=-1)
        key = jax.random.key(seed)
        k1, k2, k3, k4, k5 = jax.random.split(key, 5)
        return {'hidden_states': jax.random.normal(k1, (B, S, E), dtype=jnp.float32), 'qkv_w': jax.random.normal(k2, (E, 3 * E), dtype=jnp.float32) * 0.02, 'qkv_b': jax.random.normal(k3, (3 * E,), dtype=jnp.float32) * 0.02, 'out_w': jax.random.normal(k4, (E, E), dtype=jnp.float32) * 0.02, 'out_b': jax.random.normal(k5, (E,), dtype=jnp.float32) * 0.02}
    _L0_attn_in = _L0_attn_setup()

    def _L0_ffn_setup():
        import jax, jax.numpy as jnp
        import numpy as np
        D = 512
        F = 1376
        B, S = (4, 256)
        key = jax.random.key(seed)
        k_x, k_g, k_u, k_d = jax.random.split(key, 4)
        scale = 0.02
        return {'x': jax.random.normal(k_x, (B, S, D), dtype=jnp.float32), 'W_gate': jax.random.normal(k_g, (F, D), dtype=jnp.float32) * scale, 'W_up': jax.random.normal(k_u, (F, D), dtype=jnp.float32) * scale, 'W_down': jax.random.normal(k_d, (D, F), dtype=jnp.float32) * scale}
    _L0_ffn_in = _L0_ffn_setup()

    def _L1_attn_setup():
        import jax, jax.numpy as jnp
        import numpy as np
        DEPTH, DIM, DFF, VOCAB = (4, 64, 256, 512)
        EPS = 1e-05

        def layernorm(x, w, b):
            mu = jnp.mean(x, axis=-1, keepdims=True)
            var = jnp.mean((x - mu) ** 2, axis=-1, keepdims=True)
            return (x - mu) * jax.lax.rsqrt(var + EPS) * w + b

        def sconv(x, phazor_c, last_conv_c):
            B, L, D = x.shape
            r = jnp.abs(phazor_c)
            p = jnp.tanh(r) * jnp.exp(1j * jnp.angle(phazor_c))
            prog = p[None, :] ** jnp.arange(L, dtype=jnp.float32)[:, None]
            filt_fft = jnp.fft.fft(prog, n=2 * L, axis=0)
            x_fft = jnp.fft.fft(x.astype(jnp.complex64), n=2 * L, axis=1)
            conv = jnp.fft.ifft(filt_fft[None] * x_fft, axis=1)[:, :L]
            conv = conv + last_conv_c[None, None, :] * prog[None] * p[None, None, :]
            return conv.real.astype(x.dtype)

        def _forward(x, Win, bin, ln1_w, ln1_b, phz_re, phz_im, lc_re, lc_im, sc_lin, ln2_w, ln2_b, W1, b1, W2, b2, lnl_w, lnl_b, Wout, bout):
            h = jnp.einsum('blv,dv->bld', x, Win) + bin

            def body(h, p):
                l1w, l1b, pr, pi, lr, li, scl, l2w, l2b, w1, b1_, w2, b2_ = p
                y = jax.nn.silu(layernorm(h, l1w, l1b))
                y = sconv(y, pr + 1j * pi, lr + 1j * li)
                h = h + y * scl
                y = layernorm(h, l2w, l2b)
                y = jax.nn.silu(jnp.einsum('bld,fd->blf', y, w1) + b1_)
                y = jnp.einsum('blf,df->bld', y, w2) + b2_
                return (h + y, None)
            xs = (ln1_w, ln1_b, phz_re, phz_im, lc_re, lc_im, sc_lin, ln2_w, ln2_b, W1, b1, W2, b2)
            h, _ = jax.lax.scan(body, h, xs)
            h = layernorm(h, lnl_w, lnl_b)
            return jnp.einsum('bld,vd->blv', h, Wout) + bout
        key = jax.random.key(seed)
        ks = jax.random.split(key, 20)
        f32 = jnp.float32
        inp = {}
        inp['x'] = jax.random.normal(ks[0], (2, 512, VOCAB), dtype=f32)
        inp['Win'] = jax.random.normal(ks[1], (DIM, VOCAB), dtype=f32) * VOCAB ** (-0.5)
        inp['bin'] = jnp.zeros((DIM,), f32)
        inp['ln1_w'] = jnp.ones((DEPTH, DIM), f32)
        inp['ln1_b'] = jnp.zeros((DEPTH, DIM), f32)
        ang = 2 * np.pi * jnp.arange(DIM, dtype=f32) / DIM
        mag = jnp.abs(jax.random.normal(ks[2], (DEPTH, DIM), dtype=f32))
        inp['phz_re'] = mag * jnp.cos(ang)[None]
        inp['phz_im'] = mag * jnp.sin(ang)[None]
        inp['lc_re'] = jax.random.normal(ks[3], (DEPTH, DIM), dtype=f32)
        inp['lc_im'] = jax.random.normal(ks[4], (DEPTH, DIM), dtype=f32)
        inp['sc_lin'] = jnp.ones((DEPTH, DIM), f32)
        inp['ln2_w'] = jnp.ones((DEPTH, DIM), f32)
        inp['ln2_b'] = jnp.zeros((DEPTH, DIM), f32)
        inp['W1'] = jax.random.normal(ks[5], (DEPTH, DFF, DIM), dtype=f32) * DIM ** (-0.5)
        inp['b1'] = jnp.zeros((DEPTH, DFF), f32)
        inp['W2'] = jax.random.normal(ks[6], (DEPTH, DIM, DFF), dtype=f32) * DFF ** (-0.5)
        inp['b2'] = jnp.zeros((DEPTH, DIM), f32)
        inp['lnl_w'] = jnp.ones((DIM,), f32)
        inp['lnl_b'] = jnp.zeros((DIM,), f32)
        inp['Wout'] = jax.random.normal(ks[7], (VOCAB, DIM), dtype=f32) * DIM ** (-0.5)
        inp['bout'] = jnp.zeros((VOCAB,), f32)
        return inp
    _L1_attn_in = _L1_attn_setup()

    def _L1_ffn_setup():
        import jax, jax.numpy as jnp
        import numpy as np
        _TRIPLES = [(1, 2, 3), (1, 4, 5), (1, 7, 6), (2, 4, 6), (2, 5, 7), (3, 4, 7), (3, 6, 5)]

        def _oct_struct():
            S = np.zeros((8, 8, 8), np.float32)
            S[0, 0, 0] = 1.0
            for i in range(1, 8):
                S[0, i, i] = 1.0
                S[i, 0, i] = 1.0
                S[i, i, 0] = -1.0
            for a, b, c in _TRIPLES:
                for x, y, z in ((a, b, c), (b, c, a), (c, a, b)):
                    S[x, y, z] = 1.0
                    S[y, x, z] = -1.0
            return jnp.asarray(S)
        S_OCT = _oct_struct()
        N_EMBD = 512
        HIDDEN = 1366

        def ternary_dequant(W):
            scale = jnp.mean(jnp.abs(W))
            Wq = scale * jnp.clip(jnp.round(W / scale), -1.0, 1.0)
            return W + jax.lax.stop_gradient(Wq - W)

        def oct_ternary_linear(xp, W):
            Wq = ternary_dequant(W)
            M = jnp.einsum('jik,jod->koid', S_OCT, Wq)
            return jnp.einsum('...id,koid->...ko', xp, M)
        key = jax.random.key(seed)
        k1, k2, k3, k4 = jax.random.split(key, 4)
        B, T = (2, 256)
        d8, h8 = (N_EMBD // 8, HIDDEN // 8)
        std_in = 1.0 / np.sqrt(N_EMBD)
        std_h = 1.0 / np.sqrt(HIDDEN)
        return {'x': jax.random.normal(k1, (B, T, N_EMBD), jnp.float32), 'w_gate': jax.random.normal(k2, (8, h8, d8), jnp.float32) * std_in, 'w_up': jax.random.normal(k3, (8, h8, d8), jnp.float32) * std_in, 'w_down': jax.random.normal(k4, (8, d8, h8), jnp.float32) * std_h}
    _L1_ffn_in = _L1_ffn_setup()
    _d = {'L0_attn_hidden_states': _L0_attn_in['hidden_states'], 'L0_attn_qkv_w': _L0_attn_in['qkv_w'], 'L0_attn_qkv_b': _L0_attn_in['qkv_b'], 'L0_attn_out_w': _L0_attn_in['out_w'], 'L0_attn_out_b': _L0_attn_in['out_b'], 'L0_ffn_W_gate': _L0_ffn_in['W_gate'], 'L0_ffn_W_up': _L0_ffn_in['W_up'], 'L0_ffn_W_down': _L0_ffn_in['W_down'], 'L1_attn_Win': _L1_attn_in['Win'], 'L1_attn_bin': _L1_attn_in['bin'], 'L1_attn_ln1_w': _L1_attn_in['ln1_w'], 'L1_attn_ln1_b': _L1_attn_in['ln1_b'], 'L1_attn_phz_re': _L1_attn_in['phz_re'], 'L1_attn_phz_im': _L1_attn_in['phz_im'], 'L1_attn_lc_re': _L1_attn_in['lc_re'], 'L1_attn_lc_im': _L1_attn_in['lc_im'], 'L1_attn_sc_lin': _L1_attn_in['sc_lin'], 'L1_attn_ln2_w': _L1_attn_in['ln2_w'], 'L1_attn_ln2_b': _L1_attn_in['ln2_b'], 'L1_attn_W1': _L1_attn_in['W1'], 'L1_attn_b1': _L1_attn_in['b1'], 'L1_attn_W2': _L1_attn_in['W2'], 'L1_attn_b2': _L1_attn_in['b2'], 'L1_attn_lnl_w': _L1_attn_in['lnl_w'], 'L1_attn_lnl_b': _L1_attn_in['lnl_b'], 'L1_attn_Wout': _L1_attn_in['Wout'], 'L1_attn_bout': _L1_attn_in['bout'], 'L1_ffn_w_gate': _L1_ffn_in['w_gate'], 'L1_ffn_w_up': _L1_ffn_in['w_up'], 'L1_ffn_w_down': _L1_ffn_in['w_down']}
    _x0 = _d['L0_attn_hidden_states']
    _d['L0_attn_hidden_states'] = jax.random.normal(jax.random.fold_in(jax.random.key(seed), 1), (2, 512, 512), dtype=_x0.dtype)
    del _x0
    return _d

def reference(L0_attn_hidden_states, L0_attn_qkv_w, L0_attn_qkv_b, L0_attn_out_w, L0_attn_out_b, L0_ffn_W_gate, L0_ffn_W_up, L0_ffn_W_down, L1_attn_Win, L1_attn_bin, L1_attn_ln1_w, L1_attn_ln1_b, L1_attn_phz_re, L1_attn_phz_im, L1_attn_lc_re, L1_attn_lc_im, L1_attn_sc_lin, L1_attn_ln2_w, L1_attn_ln2_b, L1_attn_W1, L1_attn_b1, L1_attn_W2, L1_attn_b2, L1_attn_lnl_w, L1_attn_lnl_b, L1_attn_Wout, L1_attn_bout, L1_ffn_w_gate, L1_ffn_w_up, L1_ffn_w_down):

    def _L0_attn_ref(hidden_states, qkv_w, qkv_b, out_w, out_b):
        import jax, jax.numpy as jnp
        import numpy as np
        B, S, E, H = (2, 256, 512, 32)
        D = E // H
        ROPE_BASE = 10000.0
        MASK_VAL = -66504.0

        def _rope(x, cos, sin):
            x1, x2 = jnp.split(x, 2, axis=-1)
            return jnp.concatenate([x1 * cos - x2 * sin, x2 * cos + x1 * sin], axis=-1)
        b, s, e = hidden_states.shape
        qkv = hidden_states @ qkv_w + qkv_b
        q, k, v = jnp.split(qkv, 3, axis=-1)
        q = q.reshape(b, s, H, D)
        k = k.reshape(b, s, H, D)
        v = v.reshape(b, s, H, D)
        half = D // 2
        inv_freq = 1.0 / ROPE_BASE ** (jnp.arange(0, half, dtype=jnp.float32) / half)
        ang = jnp.arange(s, dtype=jnp.float32)[:, None] * inv_freq[None, :]
        cos = jnp.cos(ang)[None, :, None, :]
        sin = jnp.sin(ang)[None, :, None, :]
        q = _rope(q, cos, sin)
        k = _rope(k, cos, sin)
        scale = 1.0 / jnp.sqrt(jnp.asarray(D, dtype=hidden_states.dtype))
        scores = jnp.einsum('bqhd,bkhd->bhqk', q, k) * scale
        causal = jnp.tril(jnp.ones((s, s), dtype=scores.dtype))
        scores = scores + (1.0 - causal) * MASK_VAL
        probs = jax.nn.softmax(scores, axis=-1)
        ctx = jnp.einsum('bhqk,bkhd->bqhd', probs, v).reshape(b, s, e)
        return ctx @ out_w + out_b

    def _L0_ffn_ref(x, W_gate, W_up, W_down):
        import jax, jax.numpy as jnp
        import numpy as np
        D = 512
        F = 1376
        B, S = (4, 256)
        out_shape = x.shape[:-1] + (W_down.shape[0],)
        xt = x.reshape(-1, x.shape[-1])
        up = xt @ W_up.T
        gate = jax.nn.silu(xt @ W_gate.T)
        y = gate * up @ W_down.T
        return y.reshape(out_shape)

    def _L1_attn_ref(x, Win, bin, ln1_w, ln1_b, phz_re, phz_im, lc_re, lc_im, sc_lin, ln2_w, ln2_b, W1, b1, W2, b2, lnl_w, lnl_b, Wout, bout):
        import jax, jax.numpy as jnp
        import numpy as np
        DEPTH, DIM, DFF, VOCAB = (4, 64, 256, 512)
        EPS = 1e-05

        def layernorm(x, w, b):
            mu = jnp.mean(x, axis=-1, keepdims=True)
            var = jnp.mean((x - mu) ** 2, axis=-1, keepdims=True)
            return (x - mu) * jax.lax.rsqrt(var + EPS) * w + b

        def sconv(x, phazor_c, last_conv_c):
            B, L, D = x.shape
            r = jnp.abs(phazor_c)
            p = jnp.tanh(r) * jnp.exp(1j * jnp.angle(phazor_c))
            prog = p[None, :] ** jnp.arange(L, dtype=jnp.float32)[:, None]
            filt_fft = jnp.fft.fft(prog, n=2 * L, axis=0)
            x_fft = jnp.fft.fft(x.astype(jnp.complex64), n=2 * L, axis=1)
            conv = jnp.fft.ifft(filt_fft[None] * x_fft, axis=1)[:, :L]
            conv = conv + last_conv_c[None, None, :] * prog[None] * p[None, None, :]
            return conv.real.astype(x.dtype)

        def _forward(x, Win, bin, ln1_w, ln1_b, phz_re, phz_im, lc_re, lc_im, sc_lin, ln2_w, ln2_b, W1, b1, W2, b2, lnl_w, lnl_b, Wout, bout):
            h = jnp.einsum('blv,dv->bld', x, Win) + bin

            def body(h, p):
                l1w, l1b, pr, pi, lr, li, scl, l2w, l2b, w1, b1_, w2, b2_ = p
                y = jax.nn.silu(layernorm(h, l1w, l1b))
                y = sconv(y, pr + 1j * pi, lr + 1j * li)
                h = h + y * scl
                y = layernorm(h, l2w, l2b)
                y = jax.nn.silu(jnp.einsum('bld,fd->blf', y, w1) + b1_)
                y = jnp.einsum('blf,df->bld', y, w2) + b2_
                return (h + y, None)
            xs = (ln1_w, ln1_b, phz_re, phz_im, lc_re, lc_im, sc_lin, ln2_w, ln2_b, W1, b1, W2, b2)
            h, _ = jax.lax.scan(body, h, xs)
            h = layernorm(h, lnl_w, lnl_b)
            return jnp.einsum('bld,vd->blv', h, Wout) + bout
        return _forward(x, Win, bin, ln1_w, ln1_b, phz_re, phz_im, lc_re, lc_im, sc_lin, ln2_w, ln2_b, W1, b1, W2, b2, lnl_w, lnl_b, Wout, bout)

    def _L1_ffn_ref(x, w_gate, w_up, w_down):
        import jax, jax.numpy as jnp
        import numpy as np
        _TRIPLES = [(1, 2, 3), (1, 4, 5), (1, 7, 6), (2, 4, 6), (2, 5, 7), (3, 4, 7), (3, 6, 5)]

        def _oct_struct():
            S = np.zeros((8, 8, 8), np.float32)
            S[0, 0, 0] = 1.0
            for i in range(1, 8):
                S[0, i, i] = 1.0
                S[i, 0, i] = 1.0
                S[i, i, 0] = -1.0
            for a, b, c in _TRIPLES:
                for x, y, z in ((a, b, c), (b, c, a), (c, a, b)):
                    S[x, y, z] = 1.0
                    S[y, x, z] = -1.0
            return jnp.asarray(S)
        S_OCT = _oct_struct()
        N_EMBD = 512
        HIDDEN = 1366

        def ternary_dequant(W):
            scale = jnp.mean(jnp.abs(W))
            Wq = scale * jnp.clip(jnp.round(W / scale), -1.0, 1.0)
            return W + jax.lax.stop_gradient(Wq - W)

        def oct_ternary_linear(xp, W):
            Wq = ternary_dequant(W)
            M = jnp.einsum('jik,jod->koid', S_OCT, Wq)
            return jnp.einsum('...id,koid->...ko', xp, M)
        B, T, D = x.shape
        xp = x.reshape(B, T, 8, D // 8)
        gate = oct_ternary_linear(xp, w_gate).reshape(B, T, -1)
        up = oct_ternary_linear(xp, w_up).reshape(B, T, -1)
        h = jax.nn.silu(gate) * up
        hp = h.reshape(B, T, 8, h.shape[-1] // 8)
        out = oct_ternary_linear(hp, w_down).reshape(B, T, D)
        return out
    x = L0_attn_hidden_states
    xn = _layernorm(x, axis=-1)
    s = _L0_attn_ref(xn, L0_attn_qkv_w, L0_attn_qkv_b, L0_attn_out_w, L0_attn_out_b)
    g = _silu(_L0_ffn_ref(xn, L0_ffn_W_gate, L0_ffn_W_up, L0_ffn_W_down))
    x = x + s * g
    xn = _layernorm(x, axis=-1)
    s = _L1_attn_ref(xn, L1_attn_Win, L1_attn_bin, L1_attn_ln1_w, L1_attn_ln1_b, L1_attn_phz_re, L1_attn_phz_im, L1_attn_lc_re, L1_attn_lc_im, L1_attn_sc_lin, L1_attn_ln2_w, L1_attn_ln2_b, L1_attn_W1, L1_attn_b1, L1_attn_W2, L1_attn_b2, L1_attn_lnl_w, L1_attn_lnl_b, L1_attn_Wout, L1_attn_bout)
    g = _silu(_L1_ffn_ref(xn, L1_ffn_w_gate, L1_ffn_w_up, L1_ffn_w_down))
    x = x + s * g
    return x

_drawn_inputs = setup_inputs


def setup_inputs(seed=0):
    import zlib

    import numpy as np

    out = dict(_drawn_inputs(seed))
    spreads = {'L1_attn_bin': (0.0, 0.1),
     'L1_attn_ln1_w': (1.0, 0.2),
     'L1_attn_ln1_b': (0.0, 0.1),
     'L1_attn_sc_lin': (1.0, 0.2),
     'L1_attn_ln2_w': (1.0, 0.2),
     'L1_attn_ln2_b': (0.0, 0.1),
     'L1_attn_b1': (0.0, 0.1),
     'L1_attn_b2': (0.0, 0.1),
     'L1_attn_lnl_w': (1.0, 0.2),
     'L1_attn_lnl_b': (0.0, 0.1),
     'L1_attn_bout': (0.0, 0.1)}
    factors = {}
    for name, (base, spread) in spreads.items():
        noise = np.random.default_rng([zlib.crc32(name.encode()), seed]).standard_normal(out[name].shape)
        drawn = base * np.exp(spread * noise) if base else spread * noise
        out[name] = jnp.asarray(drawn.astype(out[name].dtype))
    for name, factor in factors.items():
        out[name] = (out[name] * factor).astype(out[name].dtype)
    return out
```

```python
import numpy as np
import concourse.bass as bass
from concourse import mybir

f32 = mybir.dt.float32
f32r = mybir.dt.float32r
bf16 = mybir.dt.bfloat16
ALU = mybir.AluOpType
ACT = mybir.ActivationFunctionType
AX = mybir.AxisListType

P = 128
B, S, E, H = 2, 512, 512, 32
D = E // H
NT = S // P
KC = E // P
FC = 11
GROUPS = 8
PAIRS = 16
EPS = 1e-5
MASK_L, MASK_R = 163.0, 408.0

DEPTH, C1, F1 = 4, 64, 256
OCT, H8 = 8, 170
HID1 = OCT * H8


def oct_signs():
    s = np.zeros((8, 8, 8), np.float32)
    s[0, 0, 0] = 1.0
    for i in range(1, 8):
        s[0, i, i] = s[i, 0, i] = 1.0
        s[i, i, 0] = -1.0
    for a, b, c in [(1, 2, 3), (1, 4, 5), (1, 7, 6), (2, 4, 6), (2, 5, 7), (3, 4, 7), (3, 6, 5)]:
        for x, y, z in ((a, b, c), (b, c, a), (c, a, b)):
            s[x, y, z], s[y, x, z] = 1.0, -1.0
    return np.array([[s[i ^ k, i, k] for k in range(8)] for i in range(8)], np.float32)


S_BANKS = [[(0, 3, 0)], [(0, 2, 0), (0, 0, 384)], [(0, 1, 0), (1, 1, 256)], [(1, 3, 0)], [(1, 2, 0), (1, 0, 384)]]
T_BANKS = [[(0, 0, 0), (0, 0, 1), (0, 0, 2), (0, 0, 3)], [(0, 1, 1), (0, 1, 2), (0, 1, 3), (0, 3, 3)],
           [(0, 2, 2), (0, 2, 3), (1, 2, 2), (1, 2, 3)],
           [(1, 0, 0), (1, 0, 1), (1, 0, 2), (1, 0, 3)], [(1, 1, 1), (1, 1, 2), (1, 1, 3), (1, 3, 3)]]
T_BY_ACT = (0, 2, 3)
SLOTS = 5 * (PAIRS + 3)
TRIPLES = 2 * FC * KC


def p_off(qt):
    return P * qt * (qt + 1) // 2


def t_col(hh, kt):
    if kt == 2:
        return 2 * 512 + 256 * hh
    return (3 * hh + (kt > 0)) * 512 + (384 if kt == 3 else 0)


def triple_slot(k):
    return k * 5 * PAIRS // TRIPLES


def triples_in(s):
    return [k for k in range(TRIPLES) if triple_slot(k) == s]


def ffn_units_after(s):
    return [k // KC for k in triples_in(s - 1) if k % KC == KC - 1]


def down_in(s):
    f = s - (5 * PAIRS + 1)
    return f if 0 <= f < FC else None


def score_in(s):
    return (s // 5, s % 5) if s < 5 * PAIRS else None


def turn_in(s):
    j = s // 5 - 1
    return (j, s % 5) if 0 <= j < PAIRS else None


def stack_in(s):
    j, i = s // 5, s % 5
    return (j // 2 + 1, i) if j % 2 == 1 and i < 4 and j // 2 + 1 < GROUPS else None


def pv_in(s):
    j, i = s // 5, s % 5
    return ((j - 3) // 2, i) if j % 2 == 1 and 3 <= j <= 2 * GROUPS + 1 else None


def ctx_in(s):
    j, i = s // 5, s % 5
    return (j - 4) // 2 if j % 2 == 0 and j >= 4 and i == 0 and (j - 4) // 2 < GROUPS else None


def turn_order():
    at = {}
    for kc in range(KC):
        at["xn", kc] = len(at)
    for i in range(4):
        at["stack", 0, i] = len(at)
    for s in range(SLOTS):
        if ctx_in(s) is not None:
            at["ctx", ctx_in(s)] = len(at)
        if stack_in(s):
            at["stack", *stack_in(s)] = len(at)
        if turn_in(s):
            at["p", *turn_in(s)] = len(at)
    for kc in range(KC):
        at["ctxf", kc] = len(at)
    return at


TURN = turn_order()
TURNS = len(TURN)
assert TURNS % 2 == 0

U_QKV, U_FFN, U_DOWN, U_OUT = 0, 12, 12 + 2 * FC, 12 + 3 * FC
UNITS = U_OUT + KC
RAW, SPLIT = 4, 5


W_GATE, W_UP, W_DOWN = range(3)
FLAT = OCT * H8 * C1 // P
HCOLS = FC * P
SIGN = oct_signs()
LAYER = [("centre", 1), ("var", 3), ("rsT", 1), ("spread", 7), ("centre", 1), ("var", 3), ("rsT", 1), ("spread", 2),
         ("mlp", 2), ("mlp", 2), ("mlpout", 1)]
FIRST_ITEMS = 6


def items1():
    out = []
    for b in range(B):
        out += [("hid", b, f, m, half) for f in range(FC) for m in range(2) for half in range(2)]
        out += [("down", b, pr, f) for pr in range(2) for f in range(FC)]
    return out


def steps1():
    items = items1()
    seq, n = [], 0

    def take(k):
        nonlocal n
        for _ in range(k):
            if n < len(items):
                seq.append(("item", n, items[n]))
                n += 1

    take(FIRST_ITEMS)
    seq.append(("proj",))
    take(1)
    for q in range(2 * DEPTH + 1):
        for name, k in (LAYER[0:4] if q % 2 == 0 else LAYER[4:]):
            if name == "mlp":
                fc = 0 if seq_count(seq, "mlp", q) == 0 else 1
                seq.append(("mlp", q, fc))
            else:
                seq.append((name, q))
            take(k)
    take(len(items))
    return seq


def seq_count(seq, name, q):
    return sum(1 for x in seq if x[0] == name and x[1] == q)


STEPS1 = steps1()
AHEAD, HS = 2, 4


def down_number(b, pr, f):
    return FC * (2 * b + pr) + f


def down_segments():
    out = []
    for i in range(OCT):
        r, end = i * H8, (i + 1) * H8
        while r < end:
            n = min(end, (r // P + 1) * P) - r
            out.append((i, r // P, r % P, r - i * H8, n))
            r += n
    return out


def program(nc, A, out, stop_after_block0=False):
    at = [0]

    def sb(name, shape, dt, offset=None):
        size = int(np.prod(shape[1:])) * (2 if dt == bf16 else 4)
        if offset is None:
            offset = at[0]
            at[0] += (size + 31) // 32 * 32
        return nc.alloc_sbuf_tensor_at(name, shape, dt, offset=BASE + offset)

    BASE = (nc.sbuf_base + 31) // 32 * 32

    ident = sb("ident", [P, P], f32)
    maskL = sb("maskL", [P, P], bf16)
    maskR = sb("maskR", [P, P], bf16)
    rope = sb("rope", [P, 4, NT, D], f32)
    centre_m = sb("centre_m", [P, P], f32)
    seq_mean = sb("seq_mean", [P, B], f32)
    o_bias = at[0]
    qkv_bias = sb("qkv_bias", [P, 3 * E], f32)
    out_bias = sb("out_bias", [P, E], f32)
    half = sb("half", [P, 8], f32)
    vec = sb("vec", [P, NVEC], f32)
    b1v = sb("b1v", [P, 2 * DEPTH], f32)
    hb1v = sb("hb1v", [P, 2 * DEPTH], f32)
    hln = sb("hln", [P, 8], f32)
    hscl = sb("hscl", [P, 4], f32)
    init = sb("init", [P, 2, 4], f32)
    ph = sb("ph", [P, 10, 4], f32)
    decay = sb("decay", [P, 4], f32)
    asum = sb("asum", [P, 3], f32)
    theta = sb("theta", [P, 2, 3], f32)
    scales = sb("scales", [P, 4], f32)
    X = sb("X", [P, NT, E], f32)
    o_xn = at[0]
    XNh = sb("XNh", [P, KC, S], f32r)
    XNl = sb("XNl", [P, KC, S], f32r)
    o_qk = at[0]
    QK = [sb(f"QK{t}", [P, GROUPS, NT, 64], f32) for t in range(2)]
    TS = [sb(f"TS{t}", [P, 16, 64], f32r) for t in range(2)]
    V = sb("V", [P, NT, H * 32], f32)
    CN = sb("CN", [P, NT, E], f32)
    o_stack = at[0]
    QS = [sb(f"QS{n}", [P, 2, S], f32r) for n in range(2)]
    KS = [sb(f"KS{n}", [P, 2, S], f32r) for n in range(2)]
    o_p = at[0]
    PR = [sb(f"PR{n}", [P, 2, 1280], f32) for n in range(2)]
    o_pt = at[0]
    PT = [sb(f"PT{n}", [P, 2560], f32) for n in range(3)]
    o_h = at[0]
    HT = sb("HT", [P, FC, S], f32)
    o_work = at[0]
    CU = sb("CU", [P, 512], f32)
    raw = [sb(f"raw{n}", [P, 512], f32) for n in range(RAW)]
    Wh = [sb(f"Wh{n}", [P, 512], f32r) for n in range(SPLIT)]
    Wl = [sb(f"Wl{n}", [P, 512], f32r) for n in range(SPLIT)]
    tb = sb("tb", [P, 512], f32)
    ab = sb("ab", [P, 512], f32)
    sS = sb("sS", [P, 512], f32)
    nm = sb("nm", [P, 2, 8], f32)
    stat = sb("stat", [P, NT, 6], f32)
    mv = sb("mv", [P, NT, 2], f32)
    vep = sb("vep", [P, NT], f32)
    rstd = sb("rstd", [P, NT], f32)
    rinv = sb("rinv", [P, 16], f32)
    assert BASE + at[0] <= nc.sbuf_usable_end, at[0]
    xn = sb("xn", [P, NT, E], f32, offset=o_h)
    rx = [sb(f"rx{n}", [P, E], f32, offset=o_h + 8192 + 2048 * n) for n in range(2)]
    r1 = [sb(f"r1{n}", [P, E], f32, offset=o_h + 12288 + 2048 * n) for n in range(2)]
    r2 = sb("r2", [P, E], f32, offset=o_h + 16384)
    hsh = [sb(f"hsh{n}", [P, S], f32r, offset=o_stack + 4096 * n) for n in range(2)]
    hsl = [sb(f"hsl{n}", [P, S], f32r, offset=o_stack + 4096 * n + 2048) for n in range(2)]
    CTh = sb("CTh", [P, KC, S], f32r, offset=o_p)
    CTl = sb("CTl", [P, KC, S], f32r, offset=o_p + 8192)

    wc = [sb(f"wc{w}", [P, FLAT], f32, offset=o_p + 2720 * w) for w in range(3)]
    wa = [sb(f"wa{w}", [P, FLAT], f32, offset=o_p + 2720 * (3 + w)) for w in range(3)]
    wn = [sb(f"wn{w}", [P, FLAT], f32, offset=o_p + 2720 * (6 + w)) for w in range(3)]
    wp = [sb(f"wp{w}", [P, FLAT], f32r, offset=o_p + 2720 * (9 + w)) for w in range(3)]
    wm = [sb(f"wm{w}", [P, FLAT], f32r, offset=o_p + 2720 * (12 + w)) for w in range(3)]
    TG = sb("TG", [P, KC, HCOLS], f32r, offset=o_qk)
    TU = sb("TU", [P, KC, HCOLS], f32r, offset=o_qk + 22528)
    TD = sb("TD", [P, FC, E], f32r, offset=o_h)
    H1 = sb("H1", [P, FC, S], f32, offset=o_pt)
    xn1 = sb("xn1", [P, NT, E], f32, offset=o_pt)
    w1T = sb("w1T", [P, DEPTH, F1], f32, offset=o_pt + 22528)
    w2T = sb("w2T", [P, DEPTH, 2, C1], f32, offset=o_pt + 22528 + 4096)
    X20 = sb("X20", [P, NT, E], f32, offset=o_stack)
    TAB = [sb(f"TAB{n}", [P, 2, S], f32, offset=o_stack + 8192 + 4096 * n) for n in range(2)]
    XMh = sb("XMh", [P, KC, S], f32r, offset=o_p)
    XMl = sb("XMl", [P, KC, S], f32r, offset=o_p + 8192)
    tabA = sb("tabA", [P, 2, 256], f32, offset=o_p + 16384)
    tabB = sb("tabB", [P, 2, 256], f32, offset=o_p + 16384 + 2048)
    woT = sb("woT", [P, E], f32, offset=o_bias)
    bout = sb("bout", [P, E], f32, offset=o_bias + 2048)
    sel = sb("sel", [8, NT, P], f32, offset=o_bias + 4096)
    Ds = [sb(f"Ds{b}", [P, NT, E], f32, offset=(o_xn, o_p)[b]) for b in range(B)]
    wk = [sb(f"wk{n}", [P, S], f32, offset=o_work + 2048 * n) for n in range(13)]
    wk12b = sb("wk12b", [P, S], f32, offset=o_bias + 6144)
    h_, hb_, sq_, dS, y_, tz, z_, y2, xc, xs, w_, v_, st_ = wk
    hsH = [sb(f"hsH{n}", [P, 2 * P], f32r, offset=o_work + 26624 + 2048 * n) for n in range(HS)]
    hsL = [sb(f"hsL{n}", [P, 2 * P], f32r, offset=o_work + 26624 + 2048 * n + 1024) for n in range(HS)]
    ve1 = sb("ve1", [P, 8], f32, offset=o_work + 34816)
    rs1 = sb("rs1", [P, 8], f32, offset=o_work + 34816 + 32)
    rT = sb("rT", [8, P], f32, offset=o_work + 34816 + 64)
    winR = sb("winR", [P, KC, 192], f32, offset=o_h + 0)
    winH = sb("winH", [P, KC, 192], f32r, offset=o_h + 3072)
    winL = sb("winL", [P, KC, 192], f32r, offset=o_h + 6144)
    XN1 = [(XNh, XNl), (XMh, XMl)]
    X2 = [X20, X]

    def bank(name):
        return nc.alloc_psum_tensor(name, [P, 512], f32)

    sc = [bank(f"sc{n}") for n in range(3)]
    tr = [bank(f"tr{n}") for n in range(2)]
    cx = bank("cx")
    fb = [bank(f"fb{n}") for n in range(2)]
    dn = [sc[0], sc[1], sc[2], fb[0]]
    ob = [fb[1], cx]
    dn1 = [sc[2], cx]
    MT, MZ = [tz, z_], [y_, dS]
    t1, ab1 = st_, wk12b
    MU = [w_, v_, xc, xs]

    def sem(name):
        return nc.alloc_semaphore(name)

    const_in = sem("const_in")
    x_in = sem("x_in")
    mask_ready = sem("mask_ready")
    x2_stored = sem("x2_stored")
    raw_in = [sem(f"raw_in{n}") for n in range(RAW)]
    hi_done = sem("hi_done")
    unit_ready = sem("unit_ready")
    down_used = sem("down_used")
    ones_set = sem("ones_set")
    stats = sem("stats")
    mv_ready = sem("mv_ready")
    eps_added = sem("eps_added")
    rstd_ready = sem("rstd_ready")
    xn_ready = sem("xn_ready")
    turned = sem("turned")
    tr_free = [sem(f"tr_free{n}") for n in range(2)]
    xh_ready = sem("xh_ready")
    f_ready = sem("f_ready")
    f_free = sem("f_free")
    r1_ready = sem("r1_ready")
    r2_ready = sem("r2_ready")
    qk_ready = sem("qk_ready")
    ts_hi = sem("ts_hi")
    ts_ready = sem("ts_ready")
    s_half = sem("s_half")
    s_ready = sem("s_ready")
    m_ready = sem("m_ready")
    s_free = sem("s_free")
    pv_done = sem("pv_done")
    cu_ready = sem("cu_ready")
    rinv_ready = sem("rinv_ready")
    tanh_ready = sem("tanh_ready")
    hs_hi = sem("hs_hi")
    hs_ready = sem("hs_ready")
    ct_hi = sem("ct_hi")
    o_ready = sem("o_ready")
    s_out = sem("s_out")
    dtanh = sem("dtanh")
    comb = sem("comb")
    out_stored = sem("out_stored")
    wc_in = sem("wc_in")
    asum_ready = sem("asum_ready")
    tot_ready = sem("tot_ready")
    theta_ready = sem("theta_ready")
    tern_a = sem("tern_a")
    tern_n = sem("tern_n")
    tern_ready = sem("tern_ready")
    tern_stored = sem("tern_stored")
    small_in = sem("small_in")
    small1_in = sem("small1_in")
    x20_in = sem("x20_in")
    wout_in = sem("wout_in")
    mv1 = sem("mv1")
    stats1 = sem("stats1")
    eps1 = sem("eps1")
    rstd1 = sem("rstd1")
    xn1_ready = sem("xn1_ready")
    xh1_ready = sem("xh1_ready")
    win_hi = sem("win_hi")
    win_ready = sem("win_ready")
    tg_in = sem("tg_in")
    tu_in = sem("tu_in")
    td_in = sem("td_in")
    pads_set = sem("pads_set")
    td_pad = sem("td_pad")
    vecs_ready = sem("vecs_ready")
    ph_step = sem("ph_step")
    polar_ready = sem("polar_ready")
    decay_ready = sem("decay_ready")
    tab_step = sem("tab_step")
    proj_ready = sem("proj_ready")
    h_ready1 = sem("h_ready1")
    ctr_ready = sem("ctr_ready")
    sq_ready = sem("sq_ready")
    ds_ready = sem("ds_ready")
    var_ready = sem("var_ready")
    ve_ready = sem("ve_ready")
    rs_ready = sem("rs_ready")
    rst_ready = sem("rst_ready")
    rt_ready = sem("rt_ready")
    rb_ready = sem("rb_ready")
    y_ready = sem("y_ready")
    tz_ready = sem("tz_ready")
    z_ready = sem("z_ready")
    y2_ready = sem("y2_ready")
    conv_step = sem("conv_step")
    yn_ready = sem("yn_ready")
    m_ready1 = sem("m_ready1")
    mt_ready = sem("mt_ready")
    mz_ready = sem("mz_ready")
    mu_ready = sem("mu_ready")
    o1_ready = sem("o1_ready")
    hb_ready = sem("hb_ready")
    g1_ready = sem("g1_ready")
    g1_free = sem("g1_free")
    t1_ready = sem("t1_ready")
    hs1_hi = sem("hs1_hi")
    hs1_ready = sem("hs1_ready")
    d1_used = sem("d1_used")
    d1_tanh = sem("d1_tanh")
    ds1_ready = sem("ds1_ready")
    s1_ready = sem("s1_ready")
    s1_free = sem("s1_free")
    fin = sem("fin")
    scale_ready = sem("scale_ready")

    x_d, w_d, qkvb_d, outb_d = A["x"], A["w0"], A["qkv_b"], A["out_b"]
    x2_d = out if stop_after_block0 else nc.dram_tensor("x2_scratch", (B, NT, P, E), f32, kind="Internal").ap()

    tern_d = [nc.dram_tensor(f"tern{w}", (2, P * FLAT), f32, kind="Internal").ap() for w in range(3)]

    def block_of(w, i, k, rows, width, first=0):
        return (0 if SIGN[i, k] > 0 else P * FLAT) + (i ^ k) * rows * width + first * width

    def signed_loads(w):
        pairs = [[block_of(w, 2 * kc + x, k, C1, H8) for x in range(2)] for kc in range(KC) for k in range(OCT)]
        return sum(1 if o1 > o0 else 2 for o0, o1 in pairs)

    def wide(ap, n):
        return ap.unsqueeze(1).broadcast_to([P, n, ap.shape[-1]])

    def F32(t):
        return t.bitcast(f32)

    FU = 12 + 2 * FC

    def unit_free(n):
        b, u = divmod(n, UNITS)
        if u < U_FFN:
            return f_ready, FU * b + 4 * (u // KC) + 4
        if u < U_DOWN:
            return f_ready, FU * b + 12 + u - U_FFN + 1
        if u < U_OUT:
            return down_used, FC * b + u - U_DOWN + 1
        return o_ready, NT * (b + 1)

    def copied(b, key):
        n = TURNS * b + TURN[key]
        return tr_free[n % 2], n // 2 + 1

    def hidden(b, w):
        return f_free, FU * b + 12 + w + 1

    with nc.Block() as block:

        @block.sync
        def _(sp):
            for dst, src in ((ident[:, :], A["ident"]), (rope[:, :, :, :], A["rope"]),
                             (tb[:, 0:2 * P], A["mask"])):
                sp.dma_start(dst, src).then_inc(const_in, 16)
            sp.dma_start(qkv_bias[:, :], qkvb_d.partition_broadcast(P)).then_inc(const_in, 16)
            sp.dma_start(out_bias[:, :], outb_d.partition_broadcast(P)).then_inc(const_in, 16)

            def signed_blocks(w, T, done):
                for kc in range(KC):
                    for k in range(OCT):
                        o0, o1 = (block_of(w, 2 * kc + x, k, C1, H8) for x in range(2))
                        for first, n, step in ((0, 2, o1 - o0),) if o1 > o0 else ((0, 1, 1), (1, 1, 1)):
                            src = bass.AP(tensor=tern_d[w].tensor, offset=(o0, o1)[first], ap=[[step, n], [H8, C1], [1, H8]])
                            rows = slice(64 * first, 64 * (first + n))
                            sp.dma_start(F32(T[rows, kc, k * H8:(k + 1) * H8]), src).then_inc(done, 16)

            for b in range(B):
                if b:
                    sp.wait_ge(x2_stored, 16 * b)
                sp.dma_start(X[:, :, :], x_d[b].rearrange("t p e -> p t e")).then_inc(x_in, 16)
                for u in range(UNITS):
                    n = b * UNITS + u
                    if n >= RAW:
                        sp.wait_ge(unit_ready, n - RAW + 1)
                    sp.dma_start(raw[n % RAW][:, :], w_d[u]).then_inc(raw_in[n % RAW], 16)
                    if b == 0 and u == 4:
                        for w in range(3):
                            sp.dma_start(wc[w][:, :], A["tern_w"][w]).then_inc(wc_in, 16)
                        for dst, src in ((centre_m[:, :], A["centre"]), (seq_mean[:, :], A["seq_mean"]), (vec[:, :], A["vec"]),
                                         (b1v[:, :], A["b1v"])):
                            sp.dma_start(dst, src).then_inc(small_in, 16)
                    if b == B - 1 and u == U_DOWN + 2 and not stop_after_block0:
                        sp.wait_ge(*copied(b, ("stack", GROUPS - 1, 3)))
                        sp.wait_ge(*copied(b, ("stack", GROUPS - 1, 2)))
                        sp.wait_ge(tern_stored, 96)
                        signed_blocks(W_GATE, TG, tg_in)
                if b == B - 1 and not stop_after_block0:
                    sp.wait_ge(pv_done, GROUPS * B)
                    for dst, src in ((w1T[:, :, :], A["w1T"]), (w2T[:, :, :, :], A["w2T"]), (woT[:, :], A["woT"]),
                                     (sel[:, :, :], A["sel"]), (bout[:, :], A["bout"].partition_broadcast(P))):
                        sp.dma_start(dst, src).then_inc(small1_in, 16)
                    sp.wait_ge(*copied(b, ("ctxf", KC - 2)))
                    sp.wait_ge(*copied(b, ("ctxf", KC - 1)))
                    signed_blocks(W_UP, TU, tu_in)
                    sp.wait_ge(down_used, FC * B)
                    sp.dma_start(X20[:, :, :], x2_d[0].rearrange("t p e -> p t e")).then_inc(x20_in, 16)
                    sp.dma_start(winR[:, :, :], A["win"]).then_inc(wout_in, 16)
                    break
                sp.wait_ge(comb, 3 * NT * (b + 1))
                sp.dma_start(x2_d[b].rearrange("t p e -> p t e"), X[:, :, :]).then_inc(x2_stored, 16)
            if stop_after_block0:
                sp.wait_ge(x2_stored, 16 * B)
                return
            sp.wait_ge(proj_ready, 1)
            sp.wait_ge(td_pad, 1)
            for i, c, p0, d0, rows in down_segments():
                for k in range(0, OCT, 2):
                    o0, o1 = (block_of(W_DOWN, i, k + x, H8, C1, d0) for x in range(2))
                    src = bass.AP(tensor=tern_d[W_DOWN].tensor, offset=o0, ap=[[C1, rows], [o1 - o0, 2], [1, C1]])
                    sp.dma_start(F32(TD[p0:p0 + rows, c, k * C1:(k + 2) * C1]).rearrange("p (a o) -> p a o", a=2), src).then_inc(td_in, 16)
            for t in range(B * NT):
                b, i = divmod(t, NT)
                sp.wait_ge(fin, 3 * (t + 1))
                sp.dma_start(out[b, i], X2[b][:, i, :]).then_inc(out_stored, 16)
            sp.wait_ge(out_stored, 16 * B * NT)

        @block.gpsimd
        def _(pool):
            nc.gpsimd.memset(half[:, :], -0.5).then_inc(ones_set, 1)
            nc.gpsimd.memset(V[:, :, :], 1.0).then_inc(ones_set, 1)

            def split(n):
                pool.wait_ge(raw_in[n % RAW], 16 * (n // RAW + 1))
                if n >= SPLIT:
                    pool.wait_ge(*unit_free(n - SPLIT))
                nc.gpsimd.tensor_scalar(Wh[n % SPLIT][:, :], raw[n % RAW][:, :], 1.0, 0.0, ALU.mult, ALU.add).then_inc(hi_done, 1)
                pool.wait_ge(hi_done, n + 1)
                nc.gpsimd.tensor_tensor(Wl[n % SPLIT][:, :], raw[n % RAW][:, :], F32(Wh[n % SPLIT][:, :]),
                                        ALU.subtract).then_inc(unit_ready, 1)

            def rope_cos(b, t, i):
                r = 8 * b + 4 * t + i
                pool.wait_ge(f_free, FU * b + 4 * t + i + 1)
                if r >= 2:
                    pool.wait_ge(qk_ready, r - 1)
                if r == 0:
                    pool.wait_ge(const_in, 80)
                nc.gpsimd.tensor_tensor(r1[r % 2][:, :].rearrange("p (h d) -> p h d", d=D),
                                        rx[r % 2][:, :].rearrange("p (h d) -> p h d", d=D),
                                        wide(rope[:, 2 * t, i, :], H), ALU.mult).then_inc(r1_ready, 1)

            def stack(b, g):
                for t in range(2):
                    n = 2 * (GROUPS * b + g) + t
                    if n >= 2:
                        b0, g0 = divmod(GROUPS * b + g - 1, GROUPS)
                        pool.wait_ge(turned, TURNS * b0 + TURN["stack", g0, 2 * t + 1] + 1)
                    src = QK[t][:, g, :, :].rearrange("p t (h d) -> p (t h) d", d=D).unsqueeze(2).broadcast_to([P, 16, 2, D])
                    dst = TS[t][:, :, :].rearrange("p n (a c d) -> p n a c d", a=2, c=2)
                    hi, lo = (dst[:, :, :, 0, :], dst[:, :, :, 1, :]) if t == 0 else (dst[:, :, 0, :, :], dst[:, :, 1, :, :])
                    nc.gpsimd.tensor_scalar(hi, src, 1.0, 0.0, ALU.mult, ALU.add).then_inc(ts_hi, 1)
                    pool.wait_ge(ts_hi, n + 1)
                    nc.gpsimd.tensor_tensor(lo, src, F32(hi), ALU.subtract).then_inc(ts_ready, 1)

            def polar():
                mult, add, sub = ALU.mult, ALU.add, ALU.subtract
                pool.wait_ge(small_in, 64)
                re, im = vec[:, V_RE:V_RE + 4], vec[:, V_IM:V_IM + 4]
                steps = [0]

                def step(ins):
                    steps[0] += 1
                    ins.then_inc(ph_step, 1)
                    pool.wait_ge(ph_step, steps[0])

                t = [ph[:, n, :] for n in range(10)]
                step(nc.gpsimd.tensor_tensor(t[0], re, re, mult))
                step(nc.gpsimd.tensor_tensor(t[1], im, im, mult))
                step(nc.gpsimd.tensor_tensor(t[0], t[0], t[1], add))
                step(nc.gpsimd.tensor_scalar(t[1], t[0], 1e-37, 1e38, ALU.max, ALU.min))
                step(nc.gpsimd.tensor_tensor(t[2], t[1], half[:, 0:4], ALU.pow))
                step(nc.gpsimd.tensor_tensor(t[3], t[1], t[2], mult))
                step(nc.gpsimd.tensor_tensor(t[3], t[3], t[2], mult))
                step(nc.gpsimd.tensor_scalar(t[3], t[3], -0.5, 1.5, mult, add))
                step(nc.gpsimd.tensor_tensor(t[2], t[2], t[3], mult))
                step(nc.gpsimd.tensor_tensor(t[7], t[0], t[2], mult))
                step(nc.gpsimd.tensor_scalar(t[8], t[0], 1e-37, 1.0, ALU.is_lt, mult))
                step(nc.gpsimd.tensor_scalar(t[9], t[8], -1.0, 1.0, mult, add))
                step(nc.gpsimd.tensor_tensor(t[2], t[2], t[9], mult))
                step(nc.gpsimd.tensor_tensor(t[4], re, t[2], mult))
                step(nc.gpsimd.tensor_tensor(t[4], t[4], t[8], add))
                nc.gpsimd.tensor_tensor(t[5], im, t[2], mult).then_inc(polar_ready, 1)
                pool.wait_ge(polar_ready, 1)

            for b in range(B):
                u0 = UNITS * b
                pool.wait_ge(mv_ready, NT * (b + 1))
                nc.gpsimd.tensor_scalar(vep[:, :], mv[:, :, 1], EPS, 1.0, ALU.add, ALU.mult).then_inc(eps_added, 1)
                pool.wait_ge(eps_added, b + 1)
                if b == 0:
                    pool.wait_ge(ones_set, 2)
                nc.gpsimd.tensor_tensor(rstd[:, :], vep[:, :], half[:, 0:NT], ALU.pow).then_inc(rstd_ready, 1)
                for n in range(0, 5):
                    split(u0 + n)
                for t in range(2):
                    for i in range(NT):
                        rope_cos(b, t, i)
                    for n in range(5 + 4 * t, 9 + 4 * t):
                        split(u0 + n)
                pool.wait_ge(qk_ready, 8 * (b + 1))
                stack(b, 0)
                done = 13
                for j in range(PAIRS):
                    if j % 2 == 0 and j // 2 + 1 < GROUPS:
                        stack(b, j // 2 + 1)
                    upto = min(U_DOWN, U_FFN + (2 * FC * (j + 2) + PAIRS - 1) // PAIRS)
                    for n in range(done, upto):
                        split(u0 + n)
                    done = max(done, upto)
                for n in range(done, UNITS):
                    split(u0 + n)
                if b == 0:
                    polar()
            if stop_after_block0:
                return

            mult, add, sub = ALU.mult, ALU.add, ALU.subtract
            pool.wait_ge(*copied(B - 1, ("ctxf", KC - 2)))
            pool.wait_ge(*copied(B - 1, ("ctxf", KC - 1)))
            nc.gpsimd.memset(F32(TG[:, :, HID1:]).bitcast(mybir.dt.uint32), 0).then_inc(pads_set, 1)
            nc.gpsimd.memset(F32(TU[:, :, HID1:]).bitcast(mybir.dt.uint32), 0).then_inc(pads_set, 1)
            pool.wait_ge(wout_in, 16)
            nc.gpsimd.tensor_scalar(winH[:, :, :], winR[:, :, :], 1.0, 0.0, mult, add).then_inc(win_hi, 1)
            pool.wait_ge(win_hi, 1)
            nc.gpsimd.tensor_tensor(winL[:, :, :], winR[:, :, :], F32(winH[:, :, :]), sub).then_inc(win_ready, 1)
            for b in range(B):
                pool.wait_ge(mv1, NT * (b + 1))
                nc.gpsimd.tensor_scalar(vep[:, :], mv[:, :, 1], EPS, 1.0, add, mult).then_inc(eps1, 1)
                pool.wait_ge(eps1, b + 1)
                nc.gpsimd.tensor_tensor(rstd[:, :], vep[:, :], half[:, 0:NT], ALU.pow).then_inc(rstd1, 1)

            def table_start(l):
                if l >= 2:
                    pool.wait_ge(h_ready1, 1 + 2 * (l - 2) + 1)
                nc.gpsimd.tensor_scalar(TAB[l % 2][:, :, 0], ph[:, 4:6, l], 1.0, 0.0, mult, add).then_inc(tab_step, 1)

            def table_double(l, e):
                m, T = 1 << e, TAB[l % 2]
                base = l * (1 + 4 * 9) + 1 + 4 * e
                pool.wait_ge(tab_step, base)
                nc.gpsimd.tensor_scalar(tabA[:, :, 0:m], T[:, :, 0:m], T[:, 0, m - 1:m], 1.0, mult, mult).then_inc(tab_step, 1)
                nc.gpsimd.tensor_scalar(tabB[:, :, 0:m], T[:, :, 0:m], T[:, 1, m - 1:m], 1.0, mult, mult).then_inc(tab_step, 1)
                pool.wait_ge(tab_step, base + 2)
                nc.gpsimd.tensor_tensor(T[:, 0, m:2 * m], tabA[:, 0, 0:m], tabB[:, 1, 0:m], sub).then_inc(tab_step, 1)
                nc.gpsimd.tensor_tensor(T[:, 1, m:2 * m], tabB[:, 0, 0:m], tabA[:, 1, 0:m], add).then_inc(tab_step, 1)

            table_start(0)
            for e in range(9):
                table_double(0, e)
            pool.wait_ge(proj_ready, 1)
            nc.gpsimd.memset(F32(TD[:, FC - 1, :]).bitcast(mybir.dt.uint32), 0).then_inc(td_pad, 1)
            todo = []
            for x in range(1, 2):
                todo += [(x, -1)] + [(x, e) for e in range(9)]
            for n_step, step in enumerate(STEPS1):
                if step[0] == "item":
                    _, n, it = step
                    nxt = items1()[n + AHEAD] if n + AHEAD < len(items1()) else None
                    if nxt and nxt[0] == "down":
                        _, b, pr, f = nxt
                        d = down_number(b, pr, f)
                        pool.wait_ge(hs1_hi, d + 1)
                        nc.gpsimd.tensor_tensor(hsL[d % HS][:, :], H1[:, f, 256 * pr:256 * pr + 256], F32(hsH[d % HS][:, :]),
                                                sub).then_inc(hs1_ready, 1)
                    if todo:
                        l, e = todo.pop(0)
                        table_start(l) if e < 0 else table_double(l, e)
                elif step[0] == "var":
                    q = step[1]
                    pool.wait_ge(ve_ready, q + 1)
                    nc.gpsimd.tensor_tensor(rs1[:, :], ve1[:, :], half[:, :], ALU.pow).then_inc(rs_ready, 1)
                elif step[0] == "centre" and step[1] % 2 == 1 and step[1] // 2 + 2 < DEPTH:
                    l = step[1] // 2 + 2
                    todo += [(l, -1)] + [(l, e) for e in range(9)]

        @block.tensor
        def _(pe):
            def turn(b, key, blocks):
                n = TURNS * b + TURN[key]
                if n >= 2:
                    pe.wait_ge(tr_free[n % 2], n // 2)
                for c, src in enumerate(blocks):
                    m = nc.tensor.transpose(tr[n % 2][:, c * P:(c + 1) * P], src, ident[:, :])
                m.then_inc(turned, 1)

            def passes(acc, lh, ll, rh, rl, first, last):
                nc.tensor.matmul(acc, lh, rh, start=first, stop=False)
                nc.tensor.matmul(acc, ll, rh, start=False, stop=False)
                return nc.tensor.matmul(acc, lh, rl, start=False, stop=last)

            def unit(b, u):
                n = UNITS * b + u
                return Wh[n % SPLIT], Wl[n % SPLIT]

            def stack_turn(b, g, i):
                t, p = divmod(i, 2)
                pe.wait_ge(ts_ready, 2 * (GROUPS * b + g) + t + 1)
                turn(b, ("stack", g, i), [F32(TS[t][:, 4 * c + 2 * p:4 * c + 2 * p + 2, :].rearrange("p n c -> p (n c)"))
                                          for c in range(NT)])

            def score(acc, q, k, j, hh, qt, c):
                rows, w = slice(64 * hh, 64 * hh + 64), P * (qt + 1)
                nc.tensor.matmul(acc[:, c:c + w], q[rows, j % 2, qt * P:(qt + 1) * P], k[rows, j % 2, 0:w], start=True, stop=False)
                return nc.tensor.matmul(acc[:, c + w - P:c + w], maskL[:, :], maskR[:, :], start=False, stop=True)

            pe.wait_ge(const_in, 80)
            pe.wait_ge(ones_set, 2)
            pe.wait_ge(asum_ready, 3)
            nc.tensor.matmul(cx[:, 0:3], V[:, 0, 0:P], asum[:, :], start=True, stop=True).then_inc(tot_ready, 1)
            for b in range(B):
                f0 = FU * b
                for kc in range(KC):
                    pe.wait_ge(xn_ready, NT * (b + 1))
                    turn(b, ("xn", kc), [xn[:, t, kc * P:(kc + 1) * P] for t in range(NT)])
                if b:
                    pe.wait_ge(comb, 3 * NT * b)
                for t in range(3):
                    for i in range(NT):
                        n = 4 * t + i
                        if n >= 2:
                            pe.wait_ge(f_free, f0 + n - 1)
                        for kc in range(KC):
                            if i == 0:
                                pe.wait_ge(unit_ready, UNITS * b + U_QKV + 4 * t + kc + 1)
                            if n == 0:
                                pe.wait_ge(*copied(b, ("xn", kc)))
                            wh, wl = unit(b, U_QKV + 4 * t + kc)
                            c = slice(i * P, (i + 1) * P)
                            m = passes(fb[n % 2][:, :], XNh[:, kc, c], XNl[:, kc, c], wh[:, :], wl[:, :], kc == 0, kc == KC - 1)
                            if kc == KC - 1:
                                m.then_inc(f_ready, 1)
                for i in range(4):
                    stack_turn(b, 0, i)
                for s in range(SLOTS):
                    if score_in(s):
                        j, i = score_in(s)
                        g, n = j // 2, 5 * PAIRS * b + s
                        if n == 0:
                            pe.wait_ge(mask_ready, 2)
                        if i == 0:
                            for x in range(4):
                                pe.wait_ge(*copied(b, ("stack", g, x)))
                        if n >= 3:
                            pe.wait_ge(s_free, n - 2)
                        q, k = QS[g % 2], KS[g % 2]
                        for hh, qt, c in S_BANKS[i][:1 if i == 2 else 2]:
                            m = score(sc[n % 3], q, k, j, hh, qt, c)
                        m.then_inc(s_half if i == 2 else s_ready, 1)
                    if ctx_in(s) is not None:
                        g = ctx_in(s)
                        pe.wait_ge(cu_ready, GROUPS * b + g + 1)
                        turn(b, ("ctx", g), [CU[:, t * P:(t + 1) * P] for t in range(NT)])
                    for triple in triples_in(s):
                        w, kc = divmod(triple, KC)
                        if kc == 0:
                            pe.wait_ge(unit_ready, UNITS * b + U_FFN + w + 1)
                            pe.wait_ge(f_free, f0 + 12 + w - 1)
                        wh, wl = unit(b, U_FFN + w)
                        c = slice(kc * P, (kc + 1) * P)
                        m = passes(fb[w % 2][:, :], wh[:, c], wl[:, c], XNh[:, kc, :], XNl[:, kc, :], kc == 0, kc == KC - 1)
                        if kc == KC - 1:
                            m.then_inc(f_ready, 1)
                    if score_in(s) and s % 5 == 2:
                        pe.wait_ge(s_half, PAIRS * b + j + 1)
                        score(sc[n % 3], q, k, j, *S_BANKS[2][1]).then_inc(s_ready, 1)
                    if stack_in(s):
                        stack_turn(b, *stack_in(s))
                    if down_in(s) is not None:
                        f = down_in(s)
                        pe.wait_ge(hs_ready, FC * b + f + 1)
                        pe.wait_ge(unit_ready, UNITS * b + U_DOWN + f + 1)
                        if f == 0:
                            pe.wait_ge(s_free, 5 * PAIRS * (b + 1))
                            pe.wait_ge(f_free, f0 + FU)
                        wh, wl = unit(b, U_DOWN + f)
                        for t in range(NT):
                            c = slice(t * P, (t + 1) * P)
                            m = passes(dn[t][:, :], hsh[f % 2][:, c], hsl[f % 2][:, c], wh[:, :], wl[:, :], f == 0, f == FC - 1)
                        m.then_inc(down_used, 1)
                    if turn_in(s):
                        j, i = turn_in(s)
                        pe.wait_ge(s_free, 5 * PAIRS * b + 5 * j + (3 if i < 2 else 5))
                        turn(b, ("p", j, i), [PR[j % 2][:, hh, p_off(qt) + kt * P:p_off(qt) + kt * P + P] for hh, kt, qt in T_BANKS[i]])
                    if pv_in(s) and pv_in(s)[1] < NT:
                        g, kt = pv_in(s)
                        gp = PAIRS * b + 2 * g
                        if kt == 0:
                            for x in range(5):
                                pe.wait_ge(*copied(b, ("p", 2 * g + 1, x)))
                            pe.wait_ge(f_free, f0 + 12)
                            if GROUPS * b + g:
                                pe.wait_ge(cu_ready, GROUPS * b + g)
                        for h in range(4):
                            c = t_col(h % 2, kt)
                            m = nc.tensor.matmul(cx[32 * h:32 * h + 32, kt * P:S], V[:, kt, (4 * g + h) * 32:(4 * g + h + 1) * 32],
                                                 PT[(gp + h // 2) % 3][:, c:c + S - kt * P], start=kt == 0, stop=kt == NT - 1,
                                                 skip_group_check=True)
                        if kt == NT - 1:
                            m.then_inc(pv_done, 1)
                for kc in range(KC):
                    pe.wait_ge(*copied(b, ("ctx", GROUPS - 1)))
                    turn(b, ("ctxf", kc), [CN[:, t, kc * P:(kc + 1) * P] for t in range(NT)])
                for i in range(NT):
                    if i >= 2:
                        pe.wait_ge(s_out, NT * b + i - 1)
                    for kc in range(KC):
                        if i == 0:
                            pe.wait_ge(*copied(b, ("ctxf", kc)))
                            pe.wait_ge(unit_ready, UNITS * b + U_OUT + kc + 1)
                        wh, wl = unit(b, U_OUT + kc)
                        c = slice(i * P, (i + 1) * P)
                        m = passes(ob[i % 2][:, :], CTh[:, kc, c], CTl[:, kc, c], wh[:, :], wl[:, :], kc == 0, kc == KC - 1)
                        if kc == KC - 1:
                            m.then_inc(o_ready, 1)
            if stop_after_block0:
                return

            for b in range(B):
                for kc in range(KC):
                    n = TURNS * B + KC * b + kc
                    pe.wait_ge(xn1_ready, NT * (b + 1))
                    pe.wait_ge(tr_free[n % 2], n // 2)
                    for t in range(NT):
                        m = nc.tensor.transpose(tr[n % 2][:, t * P:(t + 1) * P], xn1[:, t, kc * P:(kc + 1) * P], ident[:, :])
                    m.then_inc(turned, 1)

            def hidden_item(n, b, f, mm, halfway):
                u = 2 * (FC * b + f) + mm
                if halfway == 0:
                    if u >= 2:
                        pe.wait_ge(g1_free, u - 1)
                    if b == 0 and f == 0:
                        pe.wait_ge((tg_in, tu_in)[mm], 16 * signed_loads((W_GATE, W_UP)[mm]))
                        pe.wait_ge(pads_set, 2)
                        pe.wait_ge(comb, 3 * NT * B)
                    if f == 0 and mm == 0:
                        for x in range(2):
                            last = TURNS * B + KC * b + 2 + x
                            pe.wait_ge(tr_free[last % 2], last // 2 + 1)
                T, (xh, xl) = (TG, TU)[mm], XN1[b]
                for kc in range(2 * halfway, 2 * halfway + 2):
                    lhs = T[:, kc, f * P:(f + 1) * P]
                    nc.tensor.matmul(fb[mm][:, :], lhs, xh[:, kc, :], start=kc == 0, stop=False)
                    m = nc.tensor.matmul(fb[mm][:, :], lhs, xl[:, kc, :], start=False, stop=kc == KC - 1)
                if halfway:
                    m.then_inc(g1_ready, 1)

            def down_item(b, pr, f):
                d = down_number(b, pr, f)
                if d == 0:
                    pe.wait_ge(td_in, 16 * 4 * len(down_segments()))
                if f == 0 and d:
                    pe.wait_ge(ds1_ready, 2 * (2 * b + pr))
                pe.wait_ge(hs1_ready, d + 1)
                for t in range(2):
                    c = slice(t * P, (t + 1) * P)
                    nc.tensor.matmul(dn1[t][:, :], hsH[d % HS][:, c], TD[:, f, :], start=f == 0, stop=False)
                    m = nc.tensor.matmul(dn1[t][:, :], hsL[d % HS][:, c], TD[:, f, :], start=False, stop=f == FC - 1)
                m.then_inc(d1_used, 1)

            for step in STEPS1:
                kind = step[0]
                if kind == "item":
                    it = step[2]
                    if it[0] == "hid":
                        hidden_item(step[1], *it[1:])
                    else:
                        down_item(*it[1:])
                elif kind == "proj":
                    pe.wait_ge(win_ready, 1)
                    pe.wait_ge(comb, 3 * NT * B)
                    for x in range(2):
                        last = TURNS * B + KC + 2 + x
                        pe.wait_ge(tr_free[last % 2], last // 2 + 1)
                    for b in range(B):
                        cols = slice(64 * (1 - b), 64 * (1 - b) + P)
                        for kc in range(KC):
                            xh, xl = XN1[b]
                            m = passes(sc[0][:, :], winH[:, kc, cols], winL[:, kc, cols], xh[:, kc, :], xl[:, kc, :],
                                       b == 0 and kc == 0, b == 1 and kc == KC - 1)
                    m.then_inc(proj_ready, 1)
                elif kind == "centre":
                    q = step[1]
                    pe.wait_ge(h_ready1, q + 1)
                    nc.tensor.matmul(sc[0][:, :], centre_m[:, :], h_[:, :], start=True, stop=True).then_inc(ctr_ready, 1)
                elif kind == "var":
                    q = step[1]
                    pe.wait_ge(sq_ready, q + 1)
                    for t in range(NT):
                        m = nc.tensor.matmul(tr[1][:, 2 * t:2 * t + 2], sq_[:, t * P:(t + 1) * P], seq_mean[:, :], start=True, stop=True)
                    m.then_inc(var_ready, 1)
                elif kind == "rsT":
                    q = step[1]
                    pe.wait_ge(rs_ready, q + 1)
                    nc.tensor.transpose(tr[1][0:8, P:2 * P], rs1[:, :], ident[:, :]).then_inc(rst_ready, 1)
                elif kind == "spread":
                    q = step[1]
                    pe.wait_ge(rt_ready, q + 1)
                    if q == 0:
                        pe.wait_ge(small1_in, 80)
                    for t in range(NT):
                        m = nc.tensor.matmul(tr[0][:, t * P:(t + 1) * P], sel[:, t, :], rT[:, :], start=True, stop=True)
                    m.then_inc(rb_ready, 1)
                elif kind == "mlp":
                    q, fc = step[1:]
                    l = q // 2
                    pe.wait_ge(yn_ready, l + 1)
                    for b in range(B):
                        n = 4 * l + 2 * fc + b
                        if b == 0:
                            pe.wait_ge(ds_ready, q + 1)
                        if fc:
                            pe.wait_ge(mz_ready, n - 1)
                        rows = slice(64 * b, 64 * b + 64)
                        nc.tensor.matmul(sc[b][:, :], w1T[rows, l, fc * P:(fc + 1) * P], y2[rows, :], start=True, stop=True)\
                            .then_inc(m_ready1, 1)
                elif kind == "mlpout":
                    l = step[1] // 2
                    pe.wait_ge(mu_ready, 4 * (l + 1))
                    for fc in range(2):
                        for b in range(B):
                            m = nc.tensor.matmul(tr[1][64 * b:64 * b + 64, :], w2T[:, l, fc, :], MU[2 * fc + b][:, :],
                                                 start=fc == 0, stop=fc == 1, skip_group_check=True)
                    m.then_inc(o1_ready, 1)
            pe.wait_ge(yn_ready, DEPTH + 1)
            pe.wait_ge(mz_ready, 4 * DEPTH)
            for t in range(B * NT):
                b, i = divmod(t, NT)
                if t >= 2:
                    pe.wait_ge(s1_ready, t - 1)
                rows = slice(64 * b, 64 * b + 64)
                nc.tensor.matmul(sc[t % 2][:, :], y2[rows, i * P:(i + 1) * P], woT[rows, :], start=True, stop=True).then_inc(s1_free, 1)

        @block.scalar
        def _(act):
            def copy_out(n, dst):
                act.wait_ge(turned, n + 1)
                return nc.scalar.activation(dst, tr[n % 2][:, :], ACT.Copy)

            def stack_out(b, g, i):
                t, p = divmod(i, 2)
                n = TURNS * b + TURN["stack", g, i]
                copy_out(n, (QS, KS)[t][g % 2][:, p, :]).then_inc(tr_free[n % 2], 1)

            act.wait_ge(wc_in, 48)
            for w in range(3):
                nc.scalar.activation(wa[w][:, :], wc[w][:, :], ACT.Abs, accum_out=asum[:, w:w + 1]).then_inc(asum_ready, 1)
            for b in range(B):
                for kc in range(KC):
                    n = TURNS * b + TURN["xn", kc]
                    copy_out(n, XNh[:, kc, :]).then_inc(xh_ready, 1)
                for i in (0, 2):
                    stack_out(b, 0, i)
                if b == 0:
                    act.wait_ge(tern_ready, 6)
                    for w in range(3):
                        for x, src in enumerate((wp[w], wm[w])):
                            act.dma_start(tern_d[w][x].rearrange("(p n) -> p n", p=P), F32(src[:, :])).then_inc(tern_stored, 16)
                    act.wait_ge(tern_stored, 96)
                for s in range(SLOTS):
                    if score_in(s):
                        j, i = score_in(s)
                        n = 5 * PAIRS * b + s
                        if i == 0 and j >= 2:
                            act.wait_ge(turned, TURNS * b + TURN["p", j - 2, 4] + 1)
                        act.wait_ge(m_ready, n + 1)
                        for x, (hh, qt, c) in enumerate(S_BANKS[i]):
                            w = P * (qt + 1)
                            e = nc.scalar.activation(PR[j % 2][:, hh, p_off(qt):p_off(qt) + w], sc[n % 3][:, c:c + w], ACT.Exp,
                                                     bias=nm[:, j % 2, S_COL[i] + x:S_COL[i] + x + 1], scale=-1.0)
                        e.then_inc(s_free, 1)
                    for w in ffn_units_after(s):
                        if w % 2 == 0:
                            n = FC * b + w // 2
                            act.wait_ge(f_ready, FU * b + 12 + w + 1)
                            if n:
                                act.wait_ge(*(hidden(b, w - 2) if w else hidden(b - 1, 2 * FC - 2)))
                            else:
                                act.wait_ge(mask_ready, 2)
                            nc.scalar.activation(tb[:, :], fb[0][:, :], ACT.Tanh, scale=0.5).then_inc(tanh_ready, 1)
                    if stack_in(s) and stack_in(s)[1] % 2 == 0:
                        stack_out(b, *stack_in(s))
                    if down_in(s) is not None:
                        f = down_in(s)
                        act.wait_ge(*hidden(b, 2 * f + 1))
                        if f >= 2:
                            act.wait_ge(down_used, FC * b + f - 1)
                        nc.scalar.activation(hsh[f % 2][:, :], HT[:, f, :], ACT.Copy).then_inc(hs_hi, 1)
                    if turn_in(s) and turn_in(s)[1] in T_BY_ACT:
                        j, i = turn_in(s)
                        gp = PAIRS * b + j
                        if i == 0 and gp >= 3:
                            act.wait_ge(pv_done, (gp - 3) // 2 + 1)
                        n = TURNS * b + TURN["p", j, i]
                        copy_out(n, PT[gp % 3][:, 512 * i:512 * i + 512]).then_inc(tr_free[n % 2], 1)
                    if pv_in(s) and pv_in(s)[1] == NT:
                        g = pv_in(s)[0]
                        act.wait_ge(pv_done, GROUPS * b + g + 1)
                        if g:
                            act.wait_ge(turned, TURNS * b + TURN["ctx", g - 1] + 1)
                        nc.scalar.activation(CU[:, :], cx[:, :], ACT.Copy).then_inc(cu_ready, 1)
                for kc in range(KC):
                    copy_out(TURNS * b + TURN["ctxf", kc], CTh[:, kc, :]).then_inc(ct_hi, 1)
                act.wait_ge(down_used, FC * (b + 1))
                for i in range(NT):
                    if i == 0:
                        act.wait_ge(*hidden(b, 2 * FC - 2))
                    else:
                        act.wait_ge(comb, 3 * (NT * b + i - 1) + 1)
                    nc.scalar.activation(tb[:, :], dn[i][:, :], ACT.Tanh, scale=0.25).then_inc(dtanh, 1)
                if b == 0:
                    act.wait_ge(polar_ready, 1)
                    nc.scalar.activation(decay[:, :], ph[:, 7, :], ACT.Tanh).then_inc(decay_ready, 1)
            if stop_after_block0:
                return

            for b in range(B):
                for kc in range(KC):
                    n = TURNS * B + KC * b + kc
                    if n == TURNS * B + KC:
                        act.wait_ge(o_ready, NT * B)
                    copy_out(n, XN1[b][0][:, kc, :]).then_inc(xh1_ready, 1)
            for step in STEPS1:
                kind = step[0]
                if kind == "item":
                    _, n, it = step
                    if it[0] == "hid" and it[3] == 0 and it[4] == 1:
                        _, b, f, _, _ = it
                        act.wait_ge(g1_ready, 2 * (FC * b + f) + 1)
                        if FC * b + f:
                            act.wait_ge(g1_free, 2 * (FC * b + f) - 1)
                        if b and f == 0:
                            act.wait_ge(ds1_ready, NT * b)
                        nc.scalar.activation(t1[:, :], fb[0][:, :], ACT.Tanh, scale=scales[:, 0:1]).then_inc(t1_ready, 1)
                    nxt = items1()[n + AHEAD] if n + AHEAD < len(items1()) else None
                    if nxt and nxt[0] == "down":
                        _, b, pr, f = nxt
                        d = down_number(b, pr, f)
                        act.wait_ge(g1_free, 2 * (FC * b + f) + 2)
                        if d >= HS:
                            act.wait_ge(d1_used, d - HS + 1)
                        nc.scalar.activation(hsH[d % HS][:, :], H1[:, f, 256 * pr:256 * pr + 256], ACT.Copy).then_inc(hs1_hi, 1)
                    if it[0] == "down" and it[3] == FC - 1:
                        _, b, pr, f = it
                        act.wait_ge(d1_used, down_number(b, pr, f) + 1)
                        for t in range(2):
                            n = 2 * (2 * b + pr) + t
                            act.wait_ge(g1_free, 2 * FC * (b + 1))
                            if n:
                                act.wait_ge(ds1_ready, n)
                            nc.scalar.activation(t1[:, :], dn1[t][:, :], ACT.Tanh, scale=scales[:, 1:2]).then_inc(d1_tanh, 1)
                elif kind == "centre":
                    q = step[1]
                    act.wait_ge(ctr_ready, q + 1)
                    nc.scalar.activation(sq_[:, :], sc[0][:, :], ACT.Square).then_inc(sq_ready, 1)
                    nc.scalar.activation(dS[:, :], sc[0][:, :], ACT.Copy).then_inc(ds_ready, 1)
                elif kind == "rsT":
                    q = step[1]
                    act.wait_ge(rst_ready, q + 1)
                    nc.scalar.activation(rT[:, :], tr[1][0:8, P:2 * P], ACT.Copy).then_inc(rt_ready, 1)
                elif kind == "spread" and step[1] % 2 == 0 and step[1] < 2 * DEPTH:
                    q = step[1]
                    l = q // 2
                    act.wait_ge(y_ready, q + 1)
                    if q == 0:
                        act.wait_ge(vecs_ready, 4)
                    nc.scalar.activation(tz[:, :], y_[:, :], ACT.Tanh, bias=hln[:, 4 + l:5 + l], scale=hln[:, l:l + 1]).then_inc(tz_ready, 1)
                elif kind == "mlp":
                    q, fc = step[1:]
                    l = q // 2
                    for b in range(B):
                        n = 4 * l + 2 * fc + b
                        act.wait_ge(m_ready1, n + 1)
                        if n >= 2:
                            act.wait_ge(mu_ready, n - 1)
                        c = 2 * l + fc
                        nc.scalar.activation(MT[b][:, :], sc[b][:, :], ACT.Tanh, bias=hb1v[:, c:c + 1], scale=0.5).then_inc(mt_ready, 1)
                        nc.scalar.activation(MZ[b][:, :], sc[b][:, :], ACT.Identity, bias=b1v[:, c:c + 1]).then_inc(mz_ready, 1)

        @block.vector
        def _(dve):
            def minus_hi(n, dst, hi):
                nc.vector.tensor_tensor(dst, tr[n % 2][:, :], F32(hi), ALU.subtract).then_inc(tr_free[n % 2], 1)

            def stack_out(b, g, i):
                t, p = divmod(i, 2)
                n = TURNS * b + TURN["stack", g, i]
                dve.wait_ge(turned, n + 1)
                nc.vector.tensor_copy((QS, KS)[t][g % 2][:, p, :], tr[n % 2][:, :]).then_inc(tr_free[n % 2], 1)

            dve.wait_ge(const_in, 80)
            nc.vector.tensor_copy(maskL[:, :], tb[:, 0:P]).then_inc(mask_ready, 1)
            nc.vector.tensor_copy(maskR[:, :], tb[:, P:2 * P]).then_inc(mask_ready, 1)
            for b in range(B):
                dve.wait_ge(x_in, 16 * (b + 1))
                for t in range(NT):
                    nc.vector.bn_stats(stat[:, t, :], X[:, t, :]).then_inc(stats, 1)
                for t in range(NT):
                    dve.wait_ge(stats, NT * b + t + 1)
                    nc.vector.bn_aggr(mv[:, t, :], stat[:, t, :]).then_inc(mv_ready, 1)
                dve.wait_ge(mv_ready, NT * (b + 1))
                dve.wait_ge(rstd_ready, b + 1)
                for t in range(NT):
                    nc.vector.tensor_scalar(xn[:, t, :], X[:, t, :], mv[:, t, 0:1], rstd[:, t:t + 1],
                                            ALU.subtract, ALU.mult).then_inc(xn_ready, 1)
                for kc in range(KC):
                    n = TURNS * b + TURN["xn", kc]
                    dve.wait_ge(xh_ready, KC * b + kc + 1)
                    minus_hi(n, XNl[:, kc, :], XNh[:, kc, :])
                if b == 0:
                    dve.wait_ge(tot_ready, 1)
                    mean = 1.0 / (OCT * H8 * C1)
                    nc.vector.tensor_scalar(theta[:, 0, :], cx[:, 0:3], mean, 0.5, ALU.mult, ALU.mult).then_inc(theta_ready, 1)
                    nc.vector.tensor_scalar(theta[:, 1, :], cx[:, 0:3], mean, -0.5, ALU.mult, ALU.mult).then_inc(theta_ready, 1)
                    dve.wait_ge(theta_ready, 2)
                    nc.vector.tensor_copy(scales[:, 0:1], theta[:, 0, 0:1]).then_inc(scale_ready, 1)
                    nc.vector.tensor_tensor(scales[:, 2:3], theta[:, 0, 0:1], theta[:, 0, 1:2], ALU.mult).then_inc(scale_ready, 1)
                    dve.wait_ge(scale_ready, 2)
                    nc.vector.tensor_scalar(scales[:, 1:2], scales[:, 2:3], theta[:, 0, 2:3], 2.0, ALU.mult, ALU.mult).then_inc(scale_ready, 1)
                for t in range(3):
                    for i in range(NT):
                        n, r = 4 * t + i, 8 * b + 4 * t + i
                        if b == 0 and n in (3, 6, 9):
                            w = n // 3 - 1
                            nc.vector.tensor_scalar(wa[w][:, :], wc[w][:, :], theta[:, 0, w:w + 1], None, ALU.is_gt).then_inc(tern_a, 1)
                            nc.vector.tensor_scalar(wn[w][:, :], wc[w][:, :], theta[:, 1, w:w + 1], None, ALU.is_lt).then_inc(tern_a, 1)
                            dve.wait_ge(tern_a, 2 * (w + 1))
                            nc.vector.tensor_tensor(wp[w][:, :], wa[w][:, :], wn[w][:, :], ALU.subtract).then_inc(tern_ready, 1)
                            nc.vector.tensor_tensor(wm[w][:, :], wn[w][:, :], wa[w][:, :], ALU.subtract).then_inc(tern_ready, 1)
                        dve.wait_ge(f_ready, FU * b + n + 1)
                        acc, bias = fb[n % 2][:, :], qkv_bias[:, t * E:(t + 1) * E]
                        if t == 2:
                            if b == 0 and i == 0:
                                dve.wait_ge(ones_set, 2)
                            nc.vector.tensor_tensor(V[:, i, :].rearrange("p (h c) -> p h c", c=32)[:, :, 0:D],
                                                    acc.rearrange("p (h d) -> p h d", d=D), bias.rearrange("p (h d) -> p h d", d=D),
                                                    ALU.add).then_inc(f_free, 1)
                            continue
                        if r >= 2:
                            dve.wait_ge(r1_ready, r - 1)
                        nc.vector.tensor_tensor(rx[r % 2][:, :], acc, bias, ALU.add).then_inc(f_free, 1)
                        dve.wait_ge(f_free, FU * b + n + 1)
                        if r:
                            dve.wait_ge(qk_ready, r)
                        x4 = rx[r % 2][:, :].rearrange("p (h c d) -> p h c d", c=2, d=D // 2)
                        y4 = r2[:, :].rearrange("p (h c d) -> p h c d", c=2, d=D // 2)
                        for c in range(2):
                            nc.vector.tensor_tensor(y4[:, :, c, :], x4[:, :, 1 - c, :],
                                                    wide(rope[:, 2 * t + 1, i, c * 8:c * 8 + 8], H), ALU.mult).then_inc(r2_ready, 1)
                        dve.wait_ge(r2_ready, 2 * (r + 1))
                        dve.wait_ge(r1_ready, r + 1)
                        nc.vector.tensor_tensor(QK[t][:, :, i, :], r1[r % 2][:, :].rearrange("p (g c) -> p g c", c=64),
                                                r2[:, :].rearrange("p (g c) -> p g c", c=64), ALU.add).then_inc(qk_ready, 1)
                for i in (1, 3):
                    stack_out(b, 0, i)
                for s in range(SLOTS):
                    if score_in(s):
                        j, i = score_in(s)
                        n = 5 * PAIRS * b + s
                        dve.wait_ge(s_ready, n + 1)
                        col = S_COL[i]
                        if i == 2:
                            m = nc.vector.tensor_reduce(nm[:, j % 2, col:col + 2], sc[n % 3][:, :].rearrange("p (a c) -> p a c", a=2),
                                                        AX.X, ALU.min)
                        else:
                            for x, (hh, qt, c) in enumerate(S_BANKS[i]):
                                m = nc.vector.tensor_reduce(nm[:, j % 2, col + x:col + x + 1], sc[n % 3][:, c:c + P * (qt + 1)],
                                                            AX.X, ALU.min)
                        m.then_inc(m_ready, 1)
                    if ctx_in(s) is not None:
                        g = ctx_in(s)
                        n = TURNS * b + TURN["ctx", g]
                        dve.wait_ge(turned, n + 1)
                        c3 = tr[n % 2][:, :].rearrange("p (n c) -> p n c", c=32)
                        if g:
                            dve.wait_ge(*copied(b, ("ctx", g - 1)))
                        nc.vector.reciprocal(rinv[:, :], c3[:, :, D]).then_inc(rinv_ready, 1)
                        dve.wait_ge(rinv_ready, GROUPS * b + g + 1)
                        nc.vector.tensor_tensor(CN[:, :, g * 64:(g + 1) * 64].rearrange("p t (h d) -> p t h d", d=D),
                                                c3[:, :, 0:D].rearrange("p (t h) d -> p t h d", t=NT),
                                                rinv[:, :].rearrange("p (t h) -> p t h", t=NT).unsqueeze(3).broadcast_to([P, NT, 4, D]),
                                                ALU.mult).then_inc(tr_free[n % 2], 1)
                    for w in ffn_units_after(s):
                        n = FC * b + w // 2
                        dve.wait_ge(f_ready, FU * b + 12 + w + 1)
                        if w % 2 == 0:
                            dve.wait_ge(tanh_ready, n + 1)
                            if n:
                                dve.wait_ge(*(hidden(b, w - 1) if w else hidden(b - 1, 2 * FC - 1)))
                            nc.vector.scalar_tensor_tensor(out=ab[:, :], in0=tb[:, :], scalar=1.0, in1=fb[0][:, :],
                                                           op0=ALU.add, op1=ALU.mult).then_inc(f_free, 1)
                        else:
                            dve.wait_ge(*hidden(b, w - 1))
                            nc.vector.tensor_tensor(HT[:, w // 2, :], ab[:, :], fb[1][:, :], ALU.mult)\
                                .then_inc(f_free, 1)
                    if stack_in(s) and stack_in(s)[1] % 2 == 1:
                        stack_out(b, *stack_in(s))
                    if down_in(s) is not None:
                        f = down_in(s)
                        dve.wait_ge(hs_hi, FC * b + f + 1)
                        nc.vector.tensor_tensor(hsl[f % 2][:, :], HT[:, f, :], F32(hsh[f % 2][:, :]), ALU.subtract).then_inc(hs_ready, 1)
                    if turn_in(s) and turn_in(s)[1] not in T_BY_ACT:
                        j, i = turn_in(s)
                        gp = PAIRS * b + j
                        if i == 1 and gp == 0:
                            dve.wait_ge(tern_stored, 96)
                        if i == 1 and gp >= 3:
                            dve.wait_ge(pv_done, (gp - 3) // 2 + 1)
                        n = TURNS * b + TURN["p", j, i]
                        dve.wait_ge(turned, n + 1)
                        nc.vector.tensor_copy(PT[gp % 3][:, 512 * i:512 * i + 512], tr[n % 2][:, :])\
                            .then_inc(tr_free[n % 2], 1)
                for kc in range(KC):
                    dve.wait_ge(ct_hi, KC * b + kc + 1)
                    minus_hi(TURNS * b + TURN["ctxf", kc], CTl[:, kc, :], CTh[:, kc, :])
                for i in range(NT):
                    n = NT * b + i
                    dve.wait_ge(o_ready, n + 1)
                    if n:
                        dve.wait_ge(comb, 3 * n)
                    nc.vector.tensor_tensor(sS[:, :], ob[i % 2][:, :], out_bias[:, :], ALU.add).then_inc(s_out, 1)
                    dve.wait_ge(dtanh, n + 1)
                    nc.vector.scalar_tensor_tensor(out=ab[:, :], in0=tb[:, :], scalar=1.0, in1=dn[i][:, :],
                                                   op0=ALU.add, op1=ALU.mult).then_inc(comb, 1)
                    dve.wait_ge(comb, 3 * n + 1)
                    dve.wait_ge(s_out, n + 1)
                    nc.vector.tensor_tensor(ab[:, :], ab[:, :], sS[:, :], ALU.mult).then_inc(comb, 1)
                    dve.wait_ge(comb, 3 * n + 2)
                    nc.vector.scalar_tensor_tensor(out=X[:, i, :], in0=ab[:, :], scalar=0.25, in1=X[:, i, :],
                                                   op0=ALU.mult, op1=ALU.add).then_inc(comb, 1)
            if stop_after_block0:
                return

            steps = [0]

            def step_done(ins):
                steps[0] += 1
                ins.then_inc(conv_step, 1)
                dve.wait_ge(conv_step, steps[0])

            dve.wait_ge(x20_in, 16)
            dve.wait_ge(comb, 3 * NT * B)
            for b in range(B):
                if b:
                    dve.wait_ge(rstd1, b)
                for t in range(NT):
                    nc.vector.bn_stats(stat[:, t, :], X2[b][:, t, :]).then_inc(stats1, 1)
                for t in range(NT):
                    dve.wait_ge(stats1, NT * b + t + 1)
                    nc.vector.bn_aggr(mv[:, t, :], stat[:, t, :]).then_inc(mv1, 1)
                dve.wait_ge(mv1, NT * (b + 1))
                dve.wait_ge(rstd1, b + 1)
                if b:
                    dve.wait_ge(xh1_ready, KC)
                for t in range(NT):
                    nc.vector.tensor_scalar(xn1[:, t, :], X2[b][:, t, :], mv[:, t, 0:1], rstd[:, t:t + 1],
                                            ALU.subtract, ALU.mult).then_inc(xn1_ready, 1)
                for kc in range(KC):
                    dve.wait_ge(xh1_ready, KC * b + kc + 1)
                    minus_hi(TURNS * B + KC * b + kc, XN1[b][1][:, kc, :], XN1[b][0][:, kc, :])
            nc.vector.tensor_scalar(hln[:, :], vec[:, V_LN1:V_LN1 + 8], 0.5, None, ALU.mult).then_inc(vecs_ready, 1)
            nc.vector.tensor_scalar(hscl[:, :], vec[:, V_SCL:V_SCL + 4], 0.5, None, ALU.mult).then_inc(vecs_ready, 1)
            nc.vector.tensor_scalar(init[:, 0, :], vec[:, V_LRE:V_LRE + 4], 2.0, None, ALU.mult).then_inc(vecs_ready, 1)
            nc.vector.tensor_scalar(hb1v[:, :], b1v[:, :], 0.5, None, ALU.mult).then_inc(vecs_ready, 1)
            step_done(nc.vector.tensor_scalar(init[:, 1, :], vec[:, V_LIM:V_LIM + 4], -2.0, None, ALU.mult))
            dve.wait_ge(vecs_ready, 4)

            def normed(q):
                dve.wait_ge(rb_ready, q + 1)
                dve.wait_ge(ds_ready, q + 1)
                nc.vector.tensor_tensor(y_[:, :], dS[:, :], tr[0][:, :], ALU.mult).then_inc(y_ready, 1)
                dve.wait_ge(y_ready, q + 1)

            for step in STEPS1:
                kind = step[0]
                if kind == "item":
                    _, n, it = step
                    if it[0] == "hid" and it[4] == 1:
                        _, b, f, mm, _ = it
                        u = 2 * (FC * b + f) + mm
                        dve.wait_ge(g1_ready, u + 1)
                        if mm == 0:
                            dve.wait_ge(t1_ready, FC * b + f + 1)
                            if u:
                                dve.wait_ge(g1_free, u)
                            nc.vector.scalar_tensor_tensor(out=ab1[:, :], in0=t1[:, :], scalar=1.0, in1=fb[0][:, :],
                                                           op0=ALU.add, op1=ALU.mult).then_inc(g1_free, 1)
                        else:
                            dve.wait_ge(g1_free, u)
                            if b == 1:
                                dve.wait_ge(hs1_ready, FC + f + 1)
                            nc.vector.tensor_tensor(H1[:, f, :], ab1[:, :], fb[1][:, :], ALU.mult).then_inc(g1_free, 1)
                    if it[0] == "down" and it[3] == FC - 1:
                        _, b, pr, f = it
                        for t in range(2):
                            n = 2 * (2 * b + pr) + t
                            dve.wait_ge(d1_tanh, n + 1)
                            if b == 1:
                                dve.wait_ge(proj_ready, 1)
                            nc.vector.scalar_tensor_tensor(out=Ds[b][:, 2 * pr + t, :], in0=t1[:, :], scalar=1.0, in1=dn1[t][:, :],
                                                           op0=ALU.add, op1=ALU.mult).then_inc(ds1_ready, 1)
                elif kind == "proj":
                    dve.wait_ge(proj_ready, 1)
                    nc.vector.tensor_scalar(h_[:, :], sc[0][:, :], vec[:, V_BIN:V_BIN + 1], None, ALU.add).then_inc(h_ready1, 1)
                elif kind == "var":
                    q = step[1]
                    dve.wait_ge(var_ready, q + 1)
                    nc.vector.tensor_scalar(ve1[:, :], tr[1][:, 0:8], EPS, None, ALU.add).then_inc(ve_ready, 1)
                elif kind == "spread":
                    q = step[1]
                    l = q // 2
                    normed(q)
                    if q == 2 * DEPTH:
                        nc.vector.tensor_scalar(y2[:, :], y_[:, :], vec[:, V_LNL:V_LNL + 1], vec[:, V_LNL + 1:V_LNL + 2],
                                                ALU.mult, ALU.add).then_inc(yn_ready, 1)
                    elif q % 2 == 0:
                        C, Sn = TAB[l % 2][:, 0, :], TAB[l % 2][:, 1, :]
                        step_done(nc.vector.tensor_scalar(z_[:, :], y_[:, :], vec[:, V_LN1 + l:V_LN1 + l + 1],
                                                          vec[:, V_LN1 + 4 + l:V_LN1 + 5 + l], ALU.mult, ALU.add))
                        dve.wait_ge(tz_ready, l + 1)
                        step_done(nc.vector.scalar_tensor_tensor(out=y2[:, :], in0=tz[:, :], scalar=1.0, in1=z_[:, :],
                                                                 op0=ALU.add, op1=ALU.mult))
                        dve.wait_ge(tab_step, 37 * (l + 1))
                        nc.vector.tensor_tensor(xc[:, :], y2[:, :], C, ALU.mult).then_inc(conv_step, 1)
                        nc.vector.tensor_tensor(xs[:, :], y2[:, :], Sn, ALU.mult).then_inc(conv_step, 1)
                        steps[0] += 2
                        if l == 0:
                            dve.wait_ge(decay_ready, 1)
                        r = decay[:, l:l + 1].broadcast_to([P, S])
                        dve.wait_ge(conv_step, steps[0] - 1)
                        nc.vector.tensor_tensor_scan(w_[:, :], r, xc[:, :], init[:, 0, l:l + 1], ALU.mult, ALU.add).then_inc(conv_step, 1)
                        dve.wait_ge(conv_step, steps[0])
                        nc.vector.tensor_tensor_scan(v_[:, :], r, xs[:, :], init[:, 1, l:l + 1], ALU.mult, ALU.add).then_inc(conv_step, 1)
                        steps[0] += 2
                        dve.wait_ge(conv_step, steps[0] - 1)
                        nc.vector.tensor_tensor(xc[:, :], w_[:, :], C, ALU.mult).then_inc(conv_step, 1)
                        dve.wait_ge(conv_step, steps[0])
                        nc.vector.tensor_tensor(xs[:, :], v_[:, :], Sn, ALU.mult).then_inc(conv_step, 1)
                        steps[0] += 2
                        dve.wait_ge(conv_step, steps[0])
                        step_done(nc.vector.tensor_tensor(w_[:, :], xc[:, :], xs[:, :], ALU.add))
                        nc.vector.scalar_tensor_tensor(out=h_[:, :], in0=w_[:, :], scalar=hscl[:, l:l + 1], in1=h_[:, :],
                                                       op0=ALU.mult, op1=ALU.add).then_inc(h_ready1, 1)
                    else:
                        nc.vector.tensor_scalar(y2[:, :], y_[:, :], vec[:, V_LN2 + l:V_LN2 + l + 1],
                                                vec[:, V_LN2 + 4 + l:V_LN2 + 5 + l], ALU.mult, ALU.add).then_inc(yn_ready, 1)
                        dve.wait_ge(h_ready1, q + 1)
                        nc.vector.tensor_scalar(hb_[:, :], h_[:, :], vec[:, V_B2 + l:V_B2 + l + 1], None, ALU.add).then_inc(hb_ready, 1)
                elif kind == "mlp":
                    q, fc = step[1:]
                    l = q // 2
                    for b in range(B):
                        n = 4 * l + 2 * fc + b
                        dve.wait_ge(mt_ready, n + 1)
                        dve.wait_ge(mz_ready, n + 1)
                        nc.vector.scalar_tensor_tensor(out=MU[2 * fc + b][:, :], in0=MT[b][:, :], scalar=1.0, in1=MZ[b][:, :],
                                                       op0=ALU.add, op1=ALU.mult).then_inc(mu_ready, 1)
                elif kind == "mlpout":
                    l = step[1] // 2
                    dve.wait_ge(o1_ready, l + 1)
                    dve.wait_ge(hb_ready, l + 1)
                    nc.vector.scalar_tensor_tensor(out=h_[:, :], in0=tr[1][:, :], scalar=0.5, in1=hb_[:, :],
                                                   op0=ALU.mult, op1=ALU.add).then_inc(h_ready1, 1)
            s1 = [z_, tz]
            dve.wait_ge(ds1_ready, 2 * NT)
            for t in range(B * NT):
                b, i = divmod(t, NT)
                dve.wait_ge(s1_free, t + 1)
                if t >= 2:
                    dve.wait_ge(fin, 3 * (t - 1))
                nc.vector.tensor_tensor(s1[t % 2][:, :], sc[t % 2][:, :], bout[:, :], ALU.add).then_inc(s1_ready, 1)
                dve.wait_ge(s1_ready, t + 1)
                nc.vector.tensor_tensor(s1[t % 2][:, :], s1[t % 2][:, :], Ds[b][:, i, :], ALU.mult).then_inc(fin, 1)
                dve.wait_ge(fin, 3 * t + 1)
                nc.vector.scalar_tensor_tensor(out=X2[b][:, i, :], in0=s1[t % 2][:, :], scalar=scales[:, 1:2], in1=X2[b][:, i, :],
                                               op0=ALU.mult, op1=ALU.add).then_inc(fin, 2)


S_COL = [0, 1, 3, 5, 6]


V_BIN, V_LN1, V_RE, V_IM, V_LRE, V_LIM, V_SCL, V_LN2, V_B2, V_LNL, NVEC = 0, 1, 9, 13, 17, 21, 25, 29, 37, 41, 43


def constants():
    half = D // 2
    inv_freq = (1.0 / np.float32(10000.0) ** (np.arange(half, dtype=np.float32) / np.float32(half))).astype(np.float32)
    ang = (np.arange(S, dtype=np.float32)[:, None] * inv_freq[None, :]).astype(np.float32)
    cos, sin = np.cos(ang).astype(np.float32), np.sin(ang).astype(np.float32)
    c2, s2 = np.concatenate([cos, cos], 1), np.concatenate([-sin, sin], 1)
    scale = np.float32(-0.25)
    rope = np.stack([c2 * scale, s2 * scale, c2, s2])
    rope = np.ascontiguousarray(rope.reshape(4, NT, P, D).transpose(2, 0, 1, 3))
    return {
        "ident": np.eye(P, dtype=np.float32),
        "rope": rope.astype(np.float32),
        "centre": np.kron(np.eye(B), np.eye(C1) - 1.0 / C1).astype(np.float32),
        "seq_mean": (np.kron(np.eye(B), np.ones((C1, 1))) / C1).astype(np.float32),
        "sel": np.stack([[np.repeat(np.arange(B) + 2 * t == r, C1) for t in range(NT)] for r in range(8)]).astype(np.float32),
        "mask": np.concatenate([np.eye(P) * MASK_L, np.triu(np.ones((P, P)), 1) * MASK_R], 1).astype(np.float32),
    }


def layout(inputs):
    x = np.asarray(inputs["L0_attn_hidden_states"]).reshape(B, NT, P, E)
    w_qkv = np.asarray(inputs["L0_attn_qkv_w"])
    units = np.zeros((UNITS, P, 512), np.float32)
    for t in range(3):
        for kc in range(KC):
            units[U_QKV + 4 * t + kc] = w_qkv[kc * P:(kc + 1) * P, t * E:(t + 1) * E]
    for m, name in enumerate(("L0_ffn_W_gate", "L0_ffn_W_up")):
        w = np.asarray(inputs[name])
        pad = np.zeros((FC * P, E), np.float32)
        pad[:w.shape[0]] = w
        u = pad.reshape(FC, P, KC, P).transpose(0, 3, 2, 1)
        units[U_FFN + m:U_DOWN:2] = u.reshape(FC, P, 512)
    w = np.asarray(inputs["L0_ffn_W_down"])
    pad = np.zeros((FC * P, E), np.float32)
    pad[:w.shape[1]] = w.T
    units[U_DOWN:U_OUT] = pad.reshape(FC, P, E)
    units[U_OUT:] = np.asarray(inputs["L0_attn_out_w"]).reshape(KC, P, E)
    g = {k[8:]: np.asarray(v) for k, v in inputs.items() if k.startswith("L1_attn_")}
    v4 = [g[k].T for k in ("ln1_w", "ln1_b", "phz_re", "phz_im", "lc_re", "lc_im", "sc_lin", "ln2_w", "ln2_b", "b2")]
    vec = np.concatenate([g["bin"][:, None], *v4, g["lnl_w"][:, None], g["lnl_b"][:, None]], 1)
    win = np.zeros((P, KC, 192), np.float32)
    win[:, :, 64:128] = g["Win"].T.reshape(KC, P, C1).transpose(1, 0, 2)
    block1 = {
        "vec": np.concatenate([vec, vec], 0),
        "b1v": np.ascontiguousarray(g["b1"].reshape(DEPTH, 2, P).transpose(2, 0, 1).reshape(P, 2 * DEPTH)),
        "win": win,
        "w1T": np.concatenate([g["W1"].transpose(2, 0, 1)] * 2, 0),
        "w2T": np.ascontiguousarray(g["W2"].transpose(2, 0, 1).reshape(2, P, DEPTH, C1).transpose(1, 2, 0, 3)),
        "woT": np.concatenate([g["Wout"].T] * 2, 0),
        "bout": g["bout"],
        "tern_w": np.stack([np.asarray(inputs["L1_ffn_" + k]).transpose(0, 2, 1).reshape(P, FLAT) for k in ("w_gate", "w_up", "w_down")]),
    }
    return {
        **block1,
        "x": np.ascontiguousarray(x), "w0": units,
        "qkv_b": np.asarray(inputs["L0_attn_qkv_b"]), "out_b": np.asarray(inputs["L0_attn_out_b"]),
    }


def kernel(**inputs):
    import concourse.bacc as bacc
    from concourse.bass_utils import run_bass_kernel_spmd

    nc = bacc.Bacc("TRN2", target_bir_lowering=False, num_devices=1)
    arrays = {name: np.ascontiguousarray(a) for name, a in {**layout(inputs), **constants()}.items()}
    A = {name: nc.dram_tensor(name, a.shape, mybir.dt.from_np(a.dtype), kind="ExternalInput").ap() for name, a in arrays.items()}
    out = nc.dram_tensor("out", (B, NT, P, E), f32, kind="ExternalOutput").ap()
    program(nc, A, out)
    r = run_bass_kernel_spmd(nc, [arrays], core_ids=[0])
    return r.results[0]["out"].reshape(B, S, E)
```

```python
import numpy as np
import concourse.bass as bass
from concourse import mybir

f32 = mybir.dt.float32
f32r = mybir.dt.float32r
bf16 = mybir.dt.bfloat16
ALU = mybir.AluOpType
ACT = mybir.ActivationFunctionType
AX = mybir.AxisListType

P = 128
B, S, E, H = 2, 512, 512, 32
D = E // H
NT = S // P
KC = E // P
FC = 11
GROUPS = 8
PAIRS = 16
EPS = 1e-5
MASK_L, MASK_R = 163.0, 408.0

DEPTH, C1, F1 = 4, 64, 256
OCT, H8 = 8, 170
HID1 = OCT * H8


def oct_signs():
    s = np.zeros((8, 8, 8), np.float32)
    s[0, 0, 0] = 1.0
    for i in range(1, 8):
        s[0, i, i] = s[i, 0, i] = 1.0
        s[i, i, 0] = -1.0
    for a, b, c in [(1, 2, 3), (1, 4, 5), (1, 7, 6), (2, 4, 6), (2, 5, 7), (3, 4, 7), (3, 6, 5)]:
        for x, y, z in ((a, b, c), (b, c, a), (c, a, b)):
            s[x, y, z], s[y, x, z] = 1.0, -1.0
    return np.array([[s[i ^ k, i, k] for k in range(8)] for i in range(8)], np.float32)


S_BANKS = [[(0, 3, 0)], [(0, 2, 0), (0, 0, 384)], [(0, 1, 0), (1, 1, 256)], [(1, 3, 0)], [(1, 2, 0), (1, 0, 384)]]
T_BANKS = [[(0, 0, 0), (0, 0, 1), (0, 0, 2), (0, 0, 3)], [(0, 1, 1), (0, 1, 2), (0, 1, 3), (0, 3, 3)],
           [(0, 2, 2), (0, 2, 3), (1, 2, 2), (1, 2, 3)],
           [(1, 0, 0), (1, 0, 1), (1, 0, 2), (1, 0, 3)], [(1, 1, 1), (1, 1, 2), (1, 1, 3), (1, 3, 3)]]
T_BY_ACT = (0, 2, 3)
SLOTS = 5 * PAIRS + FC + 1
HEAD_UNITS = 2
TRIPLES = 2 * FC * KC


LAST_DOWN = 5 * PAIRS + FC
NORM_STATS, NORM_ROWS, NORM_TURN = 5 * PAIRS + 4, 5 * PAIRS + 6, 5 * PAIRS + 8


def p_off(qt):
    return P * qt * (qt + 1) // 2


def t_col(hh, kt):
    if kt == 2:
        return 2 * 512 + 256 * hh
    return (3 * hh + (kt > 0)) * 512 + (384 if kt == 3 else 0)


def triple_slot(k):
    return max(-1, (k - HEAD_UNITS * KC) * 5 * PAIRS // (TRIPLES - HEAD_UNITS * KC))


def triples_in(s):
    return [k for k in range(TRIPLES) if triple_slot(k) == s]


def ffn_units_after(s):
    return [k // KC for k in triples_in(s - 1) if k % KC == KC - 1 and k >= HEAD_UNITS * KC]


def down_in(s):
    f = s - (5 * PAIRS + 1)
    return f if 0 <= f < FC else None


def score_in(s):
    return (s // 5, s % 5) if s < 5 * PAIRS else None


def turn_in(s):
    j = s // 5 - 1
    return (j, s % 5) if 0 <= j < PAIRS else None


def stack_in(s):
    j, i = s // 5, s % 5
    return (j // 2 + 1, i) if j % 2 == 1 and i < 4 and j // 2 + 1 < GROUPS else None


def pv_in(s):
    j, i = s // 5, s % 5
    return ((j - 3) // 2, i) if j % 2 == 1 and 3 <= j <= 2 * GROUPS + 1 else None


def ctx_in(s):
    j, i = s // 5, s % 5
    g = (j - 4) // 2
    return g if j % 2 == 0 and j >= 4 and i == (1 if g < GROUPS - 1 else 0) and g < GROUPS else None


def turn_order():
    at = {}
    for i in range(4):
        at["stack", 0, i] = len(at)
    for s in range(SLOTS):
        if ctx_in(s) is not None:
            at["ctx", ctx_in(s)] = len(at)
        if stack_in(s):
            at["stack", *stack_in(s)] = len(at)
        if turn_in(s):
            at["p", *turn_in(s)] = len(at)
        if s == NORM_TURN:
            for kc in range(KC):
                at["xn", kc] = len(at)
        if s == LAST_DOWN:
            for kc in range(KC):
                at["ctxf", kc] = len(at)
    return at


TURN = turn_order()
TURNS = len(TURN)
assert TURNS % 2 == 0

U_QKV, U_FFN, U_DOWN, U_OUT = 0, 12, 12 + 2 * FC, 12 + 3 * FC
UNITS = U_OUT + KC
HI_BY_ACT = U_FFN + 4
ROPE_SPLITS = [[], [9], [10], [11], [12], [13], [14], []]
RAW, SPLIT = 4, 5


W_GATE, W_UP, W_DOWN = range(3)
FLAT = OCT * H8 * C1 // P
HCOLS = FC * P
SIGN = oct_signs()
LAYER = [("centre", 1), ("var", 3), ("rsT", 1), ("spread", 8), ("centre", 1), ("var", 3), ("rsT", 1), ("spread", 2),
         ("mlp", 1), ("mlp", 3), ("mlpout", 1)]
PRE, FIRST = 2, [("norm", 4), ("rows", 8), ("turn", 4)]


def items1():
    out = []
    for b in range(B):
        out += [("hid", b, f, m, half) for f in range(FC) for m in range(2) for half in range(2)]
        out += [("down", b, pr, f) for pr in range(2) for f in range(FC)]
    return out


def steps1():
    items = items1()
    seq, n = [], 0

    def take(k):
        nonlocal n
        for _ in range(k):
            if n < len(items):
                seq.append(("item", n, items[n]))
                n += 1

    take(PRE)
    for name, k in FIRST:
        seq.append((name,))
        take(k)
    seq.append(("proj",))
    take(1)
    for q in range(2 * DEPTH + 1):
        for name, k in (LAYER[0:4] if q % 2 == 0 else LAYER[4:]):
            if name == "mlp":
                fc = 0 if seq_count(seq, "mlp", q) == 0 else 1
                seq.append(("mlp", q, fc))
            else:
                seq.append((name, q))
            take(k)
    take(len(items))
    return seq


def seq_count(seq, name, q):
    return sum(1 for x in seq if x[0] == name and x[1] == q)


STEPS1 = steps1()
LAST_BY_POOL = (1, 3, 6)
ADD_BIAS = {("hid", 1, 2 * i + 2, 1, 1): i for i in range(NT)}
DOWN_HI = [min(5 * PAIRS - 3 + n, LAST_DOWN) for n in range(FC + KC)]
CONV_FIRST = 1
AHEAD, HS = 4, 4
TD_PART = 6


def down_number(b, pr, f):
    return FC * (2 * b + pr) + f


def program(nc, A, out):
    at = [0]

    def sb(name, shape, dt, offset=None):
        size = int(np.prod(shape[1:])) * (2 if dt == bf16 else 4)
        if offset is None:
            offset = at[0]
            at[0] += (size + 31) // 32 * 32
        return nc.alloc_sbuf_tensor_at(name, shape, dt, offset=BASE + offset)

    BASE = (nc.sbuf_base + 31) // 32 * 32

    ident = sb("ident", [P, P], f32)
    maskL = sb("maskL", [P, P], bf16)
    maskR = sb("maskR", [P, P], bf16)
    rope = sb("rope", [P, 4, NT, D], f32)
    centre_m = sb("centre_m", [P, P], f32)
    seq_mean = sb("seq_mean", [P, B], f32)
    o_bias = at[0]
    qkv_bias = sb("qkv_bias", [P, 2 * E], f32)
    at[0] += E * 4
    out_bias = sb("out_bias", [P, E], f32)
    v_bias = sb("v_bias", [P, KC], f32)
    half = sb("half", [P, 8], f32)
    vec = sb("vec", [P, NVEC], f32)
    b1v = sb("b1v", [P, 2 * DEPTH], f32)
    hb1v = sb("hb1v", [P, 2 * DEPTH], f32)
    hln = sb("hln", [P, 8], f32)
    hscl = sb("hscl", [P, 4], f32)
    init = sb("init", [P, 2, 4], f32)
    ph = sb("ph", [P, 10, 4], f32)
    decay = sb("decay", [P, 4], f32)
    asum = sb("asum", [P, 3], f32)
    theta = sb("theta", [P, 2, 3], f32)
    scales = sb("scales", [P, 4], f32)
    X = sb("X", [P, NT, E], f32)
    o_xn = at[0]
    XNh = sb("XNh", [P, KC, S], f32r)
    XNl = sb("XNl", [P, KC, S], f32r)
    o_qk = at[0]
    QK = [sb(f"QK{t}", [P, GROUPS, NT, 64], f32) for t in range(2)]
    TS = [sb(f"TS{t}", [P, 16, 64], f32r) for t in range(2)]
    V = sb("V", [P, NT, H * 32], f32)
    CN = sb("CN", [P, NT, E], f32)
    o_stack = at[0]
    QS = [sb(f"QS{n}", [P, 2, S], f32r) for n in range(2)]
    KS = [sb(f"KS{n}", [P, 2, S], f32r) for n in range(2)]
    o_p = at[0]
    PR = [sb(f"PR{n}", [P, 2, 1280], f32) for n in range(2)]
    o_pt = at[0]
    PT = [sb(f"PT{n}", [P, 2560], f32) for n in range(3)]
    o_h = at[0]
    HT = sb("HT", [P, FC, S], f32)
    o_work = at[0]
    CU = sb("CU", [P, 512], f32)
    raw = [sb(f"raw{n}", [P, 512], f32) for n in range(RAW)]
    Wh = [sb(f"Wh{n}", [P, 512], f32r) for n in range(SPLIT)]
    Wl = [sb(f"Wl{n}", [P, 512], f32r) for n in range(SPLIT)]
    tb = sb("tb", [P, 512], f32)
    ab = sb("ab", [P, 512], f32)
    sS = sb("sS", [P, 512], f32)
    nm = sb("nm", [P, 2, 8], f32)
    stat = sb("stat", [P, NT, 6], f32)
    mv = sb("mv", [P, NT, 2], f32)
    vep = sb("vep", [P, NT], f32)
    rstd = sb("rstd", [P, NT], f32)
    rinv = sb("rinv", [P, 16], f32)
    assert BASE + at[0] <= nc.sbuf_usable_end, at[0]
    xn_first = sb("xn_first", [P, NT, E], f32, offset=o_h)
    xn_later = [sb(f"xn_later{b}", [P, NT, E], f32, offset=o_pt + 10240 * ((PAIRS * (b + 1) - 3) % 3)) for b in range(B)]
    XB = sb("XB", [P, NT, E], f32, offset=o_stack + 8192)
    rx = [sb(f"rx{n}", [P, E], f32, offset=o_h + 8192 + 2048 * n) for n in range(2)]
    r1 = [sb(f"r1{n}", [P, E], f32, offset=o_h + 12288 + 2048 * n) for n in range(2)]
    gt = [sb(f"gt{n}", [P, E], f32, offset=o_h + 2048 * n) for n in range(NT)]
    ga = [sb(f"ga{n}", [P, E], f32, offset=o_stack + 2048 * n) for n in range(NT)]
    r2 = sb("r2", [P, E], f32, offset=o_h + 16384)
    hsh = [sb(f"hsh{n}", [P, S], f32r, offset=o_stack + 4096 * n) for n in range(2)]
    hsl = [sb(f"hsl{n}", [P, S], f32r, offset=o_stack + 4096 * n + 2048) for n in range(2)]
    CTh = sb("CTh", [P, KC, S], f32r, offset=o_p)
    CTl = sb("CTl", [P, KC, S], f32r, offset=o_p + 8192)

    wc = [sb(f"wc{w}", [P, FLAT], f32, offset=o_p + 2720 * w) for w in range(3)]
    wa = [sb(f"wa{w}", [P, FLAT], f32, offset=o_p + 2720 * (3 + w)) for w in range(3)]
    wp = [sb(f"wp{w}", [P, FLAT], f32r, offset=o_p + 2720 * (9 + w)) for w in range(3)]
    wm = [sb(f"wm{w}", [P, FLAT], f32r, offset=o_p + 2720 * (12 + w)) for w in range(3)]
    TG = sb("TG", [P, KC, HCOLS], f32r, offset=o_qk)
    TU = sb("TU", [P, KC, HCOLS], f32r, offset=o_qk + 22528)
    TD = sb("TD", [P, FC, E], f32r, offset=o_h)
    H1 = sb("H1", [P, FC, S], f32, offset=o_pt)
    w1T = sb("w1T", [P, DEPTH, F1], f32, offset=o_pt + 22528)
    biased = sb("biased", [P, E], f32, offset=o_pt + 28672)
    w2T = sb("w2T", [P, DEPTH, 2, C1], f32, offset=o_pt + 22528 + 4096)
    X20 = sb("X20", [P, NT, E], f32, offset=o_stack)
    TAB = [sb(f"TAB{n}", [P, 2, S], f32, offset=o_stack + 8192 + 4096 * n) for n in range(2)]
    XMh = sb("XMh", [P, KC, S], f32r, offset=o_p)
    XMl = sb("XMl", [P, KC, S], f32r, offset=o_p + 8192)
    tabA = sb("tabA", [P, 2, 256], f32, offset=o_p + 16384)
    tabB = sb("tabB", [P, 2, 256], f32, offset=o_p + 16384 + 2048)
    woT = sb("woT", [P, E], f32, offset=o_bias)
    bout = sb("bout", [P, E], f32, offset=o_bias + 2048)
    sel = sb("sel", [8, NT, P], f32, offset=o_bias + 4096)
    Ds = [sb(f"Ds{b}", [P, NT, E], f32, offset=(o_xn, o_p)[b]) for b in range(B)]
    wk = [sb(f"wk{n}", [P, S], f32, offset=o_work + 2048 * n) for n in range(12)]
    t1 = [sb(f"t1_{n}", [P, S], f32, offset=(o_work + 24576, o_qk + 45056)[n]) for n in range(2)]
    ab1 = [sb(f"ab1_{n}", [P, S], f32, offset=(o_bias + 6144, o_qk + 47104)[n]) for n in range(2)]
    xn_last = sb("xn_last", [P, NT, E], f32, offset=o_work)
    h_, hb_, sq_, dS, y_, tz, z_, y2, xc, xs, w_, v_ = wk
    hsH = [sb(f"hsH{n}", [P, 2 * P], f32r, offset=o_work + 26624 + 2048 * n) for n in range(HS)]
    hsL = [sb(f"hsL{n}", [P, 2 * P], f32r, offset=o_work + 26624 + 2048 * n + 1024) for n in range(HS)]
    ve1 = sb("ve1", [P, 8], f32, offset=o_work + 34816)
    rs1 = sb("rs1", [P, 8], f32, offset=o_work + 34816 + 32)
    rT = sb("rT", [8, P], f32, offset=o_work + 34816 + 64)
    winR = sb("winR", [P, KC, 192], f32, offset=o_work + 12288)
    winH = sb("winH", [P, KC, 192], f32r, offset=o_work + 12288 + 3072)
    winL = sb("winL", [P, KC, 192], f32r, offset=o_work + 12288 + 6144)
    XN1 = [(XNh, XNl), (XMh, XMl)]
    X2 = [X20, X]
    NORM = [(X, xn_first, XN1[0]), (XB, xn_later[0], XN1[0]), (XB, xn_later[1], XN1[0]), (X, xn_last, XN1[1])]

    def bank(name):
        return nc.alloc_psum_tensor(name, [P, 512], f32)

    sc = [bank(f"sc{n}") for n in range(3)]
    tr = [bank(f"tr{n}") for n in range(2)]
    cx = bank("cx")
    fb = [bank(f"fb{n}") for n in range(2)]
    dn = [sc[0], sc[1], sc[2], fb[0]]
    QKV_BANKS = [[fb[0], sc[0], sc[1], sc[2]], [fb[1], cx, tr[0], tr[1]]]
    ob = [fb[1], cx, tr[0], tr[1]]
    OUT_TILES = (3, 0, 1, 2)
    HB = [fb[0], fb[1], sc[2], cx]
    dn1 = [[sc[2], cx], [fb[0], fb[1]]]
    last_s = [t1[0], t1[1], biased]
    LAST_BANKS = [sc[0], sc[1], tr[0], tr[1], sc[2], cx, fb[0], fb[1]]
    MT, MZ = [tz, z_], [y_, dS]
    MU = [w_, v_, xc, xs]

    def sem(name):
        return nc.alloc_semaphore(name)

    const_in = sem("const_in")
    x_in = [sem(f"x_in{t}") for t in range(NT)]
    ident_in = sem("ident_in")
    qkv_used = sem("qkv_used")
    ab_ready = sem("ab_ready")
    bias_step = sem("bias_step")
    mask_ready = sem("mask_ready")
    x2_stored = sem("x2_stored")
    raw_in = [sem(f"raw_in{n}") for n in range(RAW)]
    hi_done = sem("hi_done")
    unit_ready = sem("unit_ready")
    down_used = sem("down_used")
    ones_set = sem("ones_set")
    stats = sem("stats")
    mv_ready = sem("mv_ready")
    eps_added = sem("eps_added")
    rstd_ready = sem("rstd_ready")
    xn_ready = sem("xn_ready")
    turned = sem("turned")
    tr_free = [sem(f"tr_free{n}") for n in range(2)]
    xh_ready = sem("xh_ready")
    f_ready = sem("f_ready")
    f_free = sem("f_free")
    r1_ready = sem("r1_ready")
    r2_ready = sem("r2_ready")
    qk_ready = sem("qk_ready")
    ts_hi = sem("ts_hi")
    ts_ready = sem("ts_ready")
    s_half = sem("s_half")
    s_ready = sem("s_ready")
    m_ready = sem("m_ready")
    s_free = sem("s_free")
    pv_done = sem("pv_done")
    cu_ready = sem("cu_ready")
    rinv_ready = sem("rinv_ready")
    tanh_ready = sem("tanh_ready")
    hs_hi = sem("hs_hi")
    hs_ready = sem("hs_ready")
    ct_hi = sem("ct_hi")
    o_ready = sem("o_ready")
    s_out = sem("s_out")
    dtanh = sem("dtanh")
    comb = sem("comb")
    out_stored = sem("out_stored")
    wc_in = sem("wc_in")
    asum_ready = sem("asum_ready")
    tot_ready = sem("tot_ready")
    theta_ready = sem("theta_ready")
    tern_a = sem("tern_a")
    wp_ready = sem("wp_ready")
    tern_ready = sem("tern_ready")
    tern_stored = sem("tern_stored")
    small_in = sem("small_in")
    small1_in = sem("small1_in")
    x20_in = sem("x20_in")
    xb_in = sem("xb_in")
    arranged = sem("arranged")
    out_used = sem("out_used")
    wout_in = sem("wout_in")
    win_hi = sem("win_hi")
    win_ready = sem("win_ready")
    tg_in = sem("tg_in")
    tu_in = sem("tu_in")
    td_in = [sem(f"td_in{n}") for n in range(2)]
    vecs_ready = sem("vecs_ready")
    ph_step = sem("ph_step")
    polar_ready = sem("polar_ready")
    decay_ready = sem("decay_ready")
    tab_step = sem("tab_step")
    proj_ready = sem("proj_ready")
    h_ready1 = sem("h_ready1")
    ctr_ready = sem("ctr_ready")
    sq_ready = sem("sq_ready")
    ds_ready = sem("ds_ready")
    var_ready = sem("var_ready")
    ve_ready = sem("ve_ready")
    rs_ready = sem("rs_ready")
    rst_ready = sem("rst_ready")
    rt_ready = sem("rt_ready")
    rb_ready = sem("rb_ready")
    y_ready = sem("y_ready")
    tz_ready = sem("tz_ready")
    z_ready = sem("z_ready")
    y2_ready = sem("y2_ready")
    conv_step = sem("conv_step")
    im_ready = sem("im_ready")
    v_ready = sem("v_ready")
    v_written = sem("v_written")
    yn_ready = sem("yn_ready")
    m_ready1 = sem("m_ready1")
    mt_ready = sem("mt_ready")
    mz_ready = sem("mz_ready")
    mu_ready = sem("mu_ready")
    o1_ready = sem("o1_ready")
    hb_ready = sem("hb_ready")
    g1_ready = sem("g1_ready")
    g1_free = sem("g1_free")
    t1_ready = sem("t1_ready")
    hs1_hi = sem("hs1_hi")
    hs1_ready = sem("hs1_ready")
    d1_used = sem("d1_used")
    d1_tanh = sem("d1_tanh")
    ds1_ready = sem("ds1_ready")
    s1_ready = sem("s1_ready")
    s1_free = sem("s1_free")
    fin = sem("fin")
    fin_pool = sem("fin_pool")
    s1_scaled = sem("s1_scaled")
    pool_gated = sem("pool_gated")
    pre_ready = sem("pre_ready")
    bias1 = sem("bias1")
    scale_ready = sem("scale_ready")

    x_d, w_d, outb_d = A["x"], A["w0"], A["out_b"]
    x2_d = nc.dram_tensor("x2_scratch", (B, NT, P, E), f32, kind="Internal").ap()

    tern_d = [nc.dram_tensor(f"tern{w}", (2, P * FLAT), f32, kind="Internal").ap() for w in range(3)]

    arr_d = [nc.dram_tensor(f"arranged{w}", shape, f32, kind="Internal").ap() for w, shape in
             enumerate(((E, HCOLS), (E, HCOLS), (HCOLS, E)))]

    def block_of(w, i, k, rows, width):
        return (0 if SIGN[i, k] > 0 else P * FLAT) + (i ^ k) * rows * width

    def arrangement():
        out = []
        for w in (W_GATE, W_UP, W_DOWN):
            rows, width = (C1, H8) if w != W_DOWN else (H8, C1)
            pitch = OCT * width if w == W_DOWN else HCOLS
            for i in range(OCT):
                for k in range(0, OCT, 2):
                    o0, o1 = (block_of(w, i, k + x, rows, width) for x in range(2))
                    src = bass.AP(tensor=tern_d[w].tensor, offset=o0, ap=[[width, rows], [o1 - o0, 2], [1, width]])
                    dst = bass.AP(tensor=arr_d[w].tensor, offset=i * rows * pitch + k * width,
                                  ap=[[pitch, rows], [width, 2], [1, width]])
                    out.append((dst, src))
            if w == W_DOWN:
                out.append((arr_d[w][HID1:, :], A["zeros"].rearrange("(p n) -> p n", n=E)))
            else:
                out.append((arr_d[w][:, HID1:], A["zeros"].rearrange("(p n) -> p n", p=E)))
        return out

    ARRANGE = arrangement()

    def wide(ap, n):
        return ap.unsqueeze(1).broadcast_to([P, n, ap.shape[-1]])

    def F32(t):
        return t.bitcast(f32)

    FU, FV = 12 + 2 * FC, 8 + 2 * FC

    def unit_free(n):
        b, u = divmod(n, UNITS)
        if u < U_FFN:
            return (qkv_used, 3 * (3 * b + u // KC) + u % KC + 1) if u % KC < KC - 1 else (f_ready, FU * b + u + 1)
        if u < U_DOWN:
            return f_ready, FU * b + 12 + u - U_FFN + 1
        if u < U_OUT:
            return down_used, FC * b + u - U_DOWN + 1
        return out_used, KC * b + u - U_OUT + 1

    def hi_by_act(n):
        u = n % UNITS
        return u < HI_BY_ACT or u >= U_DOWN

    def copied(b, key):
        n = use(b, key)
        return tr_free[n % 2], n // 2 + 1

    def stacked(t, g):
        src = QK[t][:, g, :, :].rearrange("p t (h d) -> p (t h) d", d=D).unsqueeze(2).broadcast_to([P, 16, 2, D])
        dst = TS[t][:, :, :].rearrange("p n (a c d) -> p n a c d", a=2, c=2)
        return (src, dst[:, :, :, 0, :], dst[:, :, :, 1, :]) if t == 0 else (src, dst[:, :, 0, :, :], dst[:, :, 1, :, :])

    def norm_use(k, kc):
        return kc if k == 0 else use(k - 1, ("xn", kc)) if k <= B else KC + TURNS * B + kc

    def use(b, key):
        return KC + TURNS * b + TURN[key]

    def hidden(b, w):
        return f_free, FV * b + 8 + w + 1

    with nc.Block() as block:

        @block.sync
        def _(sp):
            for t in range(NT):
                sp.dma_start(X[:, t, :], x_d[0, t]).then_inc(x_in[t], 16)
                if t == 0:
                    sp.dma_start(ident[:, :], A["ident"]).then_inc(ident_in, 16)
            copies = list(ARRANGE)
            for b in range(B):
                for u in range(UNITS):
                    n = b * UNITS + u
                    if n >= RAW:
                        sp.wait_ge(unit_ready, n - RAW + 1)
                    sp.dma_start(raw[n % RAW][:, :], w_d[u]).then_inc(raw_in[n % RAW], 16)
                    if b == 0 and u == RAW - 1:
                        sp.dma_start(qkv_bias[:, :], A["qk_bias"].partition_broadcast(P)).then_inc(const_in, 16)
                        for dst, src in ((rope[:, :, :, :], A["rope"]), (tb[:, 0:2 * P], A["mask"]), (v_bias[:, :], A["v_bias"]),
                                         (out_bias[:, :], outb_d.partition_broadcast(P))):
                            sp.dma_start(dst, src).then_inc(const_in, 16)
                        for w in range(3):
                            sp.dma_start(wc[w][:, :], A["tern_w"][w]).then_inc(wc_in, 16)
                        for dst, src in ((centre_m[:, :], A["centre"]), (seq_mean[:, :], A["seq_mean"]), (vec[:, :], A["vec"]),
                                         (b1v[:, :], A["b1v"])):
                            sp.dma_start(dst, src).then_inc(small_in, 16)
                    if b == 0 and U_FFN + 5 <= u < U_DOWN:
                        if u == U_FFN + 5:
                            sp.wait_ge(tern_stored, 96)
                        for _ in range(6):
                            if copies:
                                sp.dma_start(*copies.pop(0)).then_inc(arranged, 16)
                    if b == 1 and u == 8:
                        sp.wait_ge(comb, 2 * NT)
                        sp.dma_start(x2_d[0].rearrange("t p e -> p t e"), X[:, :, :]).then_inc(x2_stored, 16)
                    if b == 1 and u == U_FFN:
                        sp.wait_ge(x2_stored, 16)
                        for t in range(NT):
                            sp.dma_start(X[:, t, :], x_d[1, t]).then_inc(x_in[t], 16)
            assert not copies
            sp.wait_ge(arranged, 16 * len(ARRANGE))
            sp.wait_ge(out_used, KC * B)
            sp.dma_start(winR[:, :, :], A["win"]).then_inc(wout_in, 16)
            sp.wait_ge(comb, 2 * NT * B)
            sp.dma_start(X20[:, :, :], x2_d[0].rearrange("t p e -> p t e")).then_inc(x20_in, 16)
            down_rows = arr_d[W_DOWN].rearrange("(c p) e -> p c e", p=P)
            sp.dma_start(F32(TD[:, :TD_PART, :]), down_rows[:, :TD_PART, :]).then_inc(td_in[0], 16)
            sp.dma_start(F32(TD[:, TD_PART:, :]), down_rows[:, TD_PART:, :]).then_inc(td_in[1], 16)
            for t in range(B * NT):
                b, i = divmod(t, NT)
                sp.wait_ge(*((fin_pool, LAST_BY_POOL.index(t) + 1) if t in LAST_BY_POOL else
                             (fin, t + 1 - sum(1 for x in LAST_BY_POOL if x < t))))
                sp.dma_start(out[b, i], X2[b][:, i, :]).then_inc(out_stored, 16)
            sp.wait_ge(out_stored, 16 * B * NT)

        @block.gpsimd
        def _(pool):
            nc.gpsimd.memset(half[:, :], -0.5).then_inc(ones_set, 1)
            nc.gpsimd.memset(V[:, :, :], 1.0).then_inc(ones_set, 1)

            def split(n):
                if not hi_by_act(n):
                    pool.wait_ge(raw_in[n % RAW], 16 * (n // RAW + 1))
                    if n >= SPLIT:
                        pool.wait_ge(*unit_free(n - SPLIT))
                    nc.gpsimd.tensor_scalar(Wh[n % SPLIT][:, :], raw[n % RAW][:, :], 1.0, 0.0, ALU.mult, ALU.add).then_inc(hi_done, 1)
                pool.wait_ge(hi_done, n + 1)
                nc.gpsimd.tensor_tensor(Wl[n % SPLIT][:, :], raw[n % RAW][:, :], F32(Wh[n % SPLIT][:, :]),
                                        ALU.subtract).then_inc(unit_ready, 1)

            def rope_cos(b, t, i):
                r = 8 * b + 4 * t + i
                pool.wait_ge(f_free, FV * b + 4 * t + i + 1)
                if r >= 2:
                    pool.wait_ge(qk_ready, r - 1)
                if r == 0:
                    pool.wait_ge(const_in, 80)
                nc.gpsimd.tensor_tensor(r1[r % 2][:, :].rearrange("p (h d) -> p h d", d=D),
                                        rx[r % 2][:, :].rearrange("p (h d) -> p h d", d=D),
                                        wide(rope[:, 2 * t, i, :], H), ALU.mult).then_inc(r1_ready, 1)

            def stack(b, g):
                for t in range(2):
                    n = 2 * (GROUPS * b + g) + t
                    if n >= 2:
                        b0, g0 = divmod(GROUPS * b + g - 1, GROUPS)
                        pool.wait_ge(turned, use(b0, ("stack", g0, 2 * t + 1)) + 1)
                    src, hi, lo = stacked(t, g)
                    if g:
                        nc.gpsimd.tensor_scalar(hi, src, 1.0, 0.0, ALU.mult, ALU.add).then_inc(ts_hi, 1)
                    pool.wait_ge(ts_hi, n + 1)
                    nc.gpsimd.tensor_tensor(lo, src, F32(hi), ALU.subtract).then_inc(ts_ready, 1)

            def polar():
                mult, add, sub = ALU.mult, ALU.add, ALU.subtract
                pool.wait_ge(small_in, 64)
                re, im = vec[:, V_RE:V_RE + 4], vec[:, V_IM:V_IM + 4]
                steps = [0]

                def step(ins):
                    steps[0] += 1
                    ins.then_inc(ph_step, 1)
                    pool.wait_ge(ph_step, steps[0])

                t = [ph[:, n, :] for n in range(10)]
                step(nc.gpsimd.tensor_tensor(t[0], re, re, mult))
                step(nc.gpsimd.tensor_tensor(t[1], im, im, mult))
                step(nc.gpsimd.tensor_tensor(t[0], t[0], t[1], add))
                step(nc.gpsimd.tensor_scalar(t[1], t[0], 1e-37, 1e38, ALU.max, ALU.min))
                step(nc.gpsimd.tensor_tensor(t[2], t[1], half[:, 0:4], ALU.pow))
                step(nc.gpsimd.tensor_tensor(t[3], t[1], t[2], mult))
                step(nc.gpsimd.tensor_tensor(t[3], t[3], t[2], mult))
                step(nc.gpsimd.tensor_scalar(t[3], t[3], -0.5, 1.5, mult, add))
                step(nc.gpsimd.tensor_tensor(t[2], t[2], t[3], mult))
                step(nc.gpsimd.tensor_tensor(t[7], t[0], t[2], mult))
                step(nc.gpsimd.tensor_scalar(t[8], t[0], 1e-37, 1.0, ALU.is_lt, mult))
                step(nc.gpsimd.tensor_scalar(t[9], t[8], -1.0, 1.0, mult, add))
                step(nc.gpsimd.tensor_tensor(t[2], t[2], t[9], mult))
                step(nc.gpsimd.tensor_tensor(t[4], re, t[2], mult))
                step(nc.gpsimd.tensor_tensor(t[4], t[4], t[8], add))
                nc.gpsimd.tensor_tensor(t[5], im, t[2], mult).then_inc(polar_ready, 1)
                pool.wait_ge(polar_ready, 1)

            def norm_rstd(k):
                pool.wait_ge(mv_ready, NT * (k + 1))
                nc.gpsimd.tensor_scalar(vep[:, :], mv[:, :, 1], EPS, 1.0, ALU.add, ALU.mult).then_inc(eps_added, 1)
                pool.wait_ge(eps_added, k + 1)
                nc.gpsimd.tensor_tensor(rstd[:, :], vep[:, :], half[:, 0:NT], ALU.pow).then_inc(rstd_ready, 1)

            pool.wait_ge(ones_set, 2)
            norm_rstd(0)
            for b in range(B):
                u0 = UNITS * b
                for n in range(0, 9):
                    split(u0 + n)
                for t in range(2):
                    for i in range(NT):
                        rope_cos(b, t, i)
                        for n in ROPE_SPLITS[4 * t + i]:
                            split(u0 + n)
                pool.wait_ge(qk_ready, 8 * (b + 1))
                stack(b, 0)
                done = U_FFN + HEAD_UNITS + 1
                for j in range(PAIRS):
                    upto = min(U_DOWN, U_FFN + HEAD_UNITS + (5 * (j + 1) + KC - 1) // KC + 1)
                    for n in range(done, upto):
                        split(u0 + n)
                    done = max(done, upto)
                    if j % 2 == 0 and j // 2 + 1 < GROUPS:
                        stack(b, j // 2 + 1)
                for n in range(done, UNITS):
                    if n == U_DOWN + 8:
                        norm_rstd(b + 1)
                    split(u0 + n)
                if b == 0:
                    polar()
            mult, add, sub = ALU.mult, ALU.add, ALU.subtract
            def table_start(l):
                if l >= 2:
                    pool.wait_ge(h_ready1, 1 + 2 * (l - 2) + 1)
                nc.gpsimd.tensor_scalar(TAB[l % 2][:, :, 0], ph[:, 4:6, l], 1.0, 0.0, mult, add).then_inc(tab_step, 1)

            def table_double(l, e):
                m, T = 1 << e, TAB[l % 2]
                base = l * (1 + 4 * 9) + 1 + 4 * e
                pool.wait_ge(tab_step, base)
                nc.gpsimd.tensor_scalar(tabA[:, :, 0:m], T[:, :, 0:m], T[:, 0, m - 1:m], 1.0, mult, mult).then_inc(tab_step, 1)
                nc.gpsimd.tensor_scalar(tabB[:, :, 0:m], T[:, :, 0:m], T[:, 1, m - 1:m], 1.0, mult, mult).then_inc(tab_step, 1)
                pool.wait_ge(tab_step, base + 2)
                nc.gpsimd.tensor_tensor(T[:, 0, m:2 * m], tabA[:, 0, 0:m], tabB[:, 1, 0:m], sub).then_inc(tab_step, 1)
                nc.gpsimd.tensor_tensor(T[:, 1, m:2 * m], tabB[:, 0, 0:m], tabA[:, 1, 0:m], add).then_inc(tab_step, 1)

            pool.wait_ge(turned, use(B - 1, ("p", PAIRS - 1, 4)) + 1)
            table_start(0)
            for e in range(9):
                table_double(0, e)
            pool.wait_ge(wout_in, 16)
            nc.gpsimd.tensor_scalar(winH[:, :, :], winR[:, :, :], 1.0, 0.0, mult, add).then_inc(win_hi, 1)
            pool.wait_ge(win_hi, 1)
            nc.gpsimd.tensor_tensor(winL[:, :, :], winR[:, :, :], F32(winH[:, :, :]), sub).then_inc(win_ready, 1)
            def add_bias(t):
                b, i = divmod(t, NT)
                pool.wait_ge(ds1_ready, t + 1)
                if t == 0:
                    pool.wait_ge(x20_in, 16)
                if t:
                    pool.wait_ge(pre_ready, 3 * t)
                nc.gpsimd.tensor_scalar(biased[:, :], Ds[b][:, i, :], scales[:, 1:2], 1.0, mult, mult).then_inc(pre_ready, 1)
                pool.wait_ge(pre_ready, 3 * t + 1)
                nc.gpsimd.tensor_tensor(biased[:, :], biased[:, :], bout[:, :], mult).then_inc(pre_ready, 1)
                pool.wait_ge(pre_ready, 3 * t + 2)
                nc.gpsimd.tensor_tensor(X2[b][:, i, :], X2[b][:, i, :], biased[:, :], add).then_inc(pre_ready, 1)

            todo = []
            for x in range(1, 2):
                todo += [(x, -1)] + [(x, e) for e in range(9)]
            for n_step, step in enumerate(STEPS1):
                if step[0] == "item":
                    _, n, it = step
                    nxt = items1()[n + AHEAD] if n + AHEAD < len(items1()) else None
                    if nxt and nxt[0] == "down":
                        _, b, pr, f = nxt
                        d = down_number(b, pr, f)
                        pool.wait_ge(hs1_hi, d + 1)
                        nc.gpsimd.tensor_tensor(hsL[d % HS][:, :], H1[:, f, 256 * pr:256 * pr + 256], F32(hsH[d % HS][:, :]),
                                                sub).then_inc(hs1_ready, 1)
                    if it in ADD_BIAS:
                        add_bias(ADD_BIAS[it])
                    if todo:
                        l, e = todo.pop(0)
                        table_start(l) if e < 0 else table_double(l, e)
                elif step[0] == "norm":
                    norm_rstd(3)
                elif step[0] == "var":
                    q = step[1]
                    pool.wait_ge(ve_ready, q + 1)
                    nc.gpsimd.tensor_tensor(rs1[:, :], ve1[:, :], half[:, :], ALU.pow).then_inc(rs_ready, 1)
                elif step[0] == "spread" and step[1] % 2 == 0 and step[1] < 2 * DEPTH:
                    l = step[1] // 2
                    pool.wait_ge(tab_step, 37 * (l + 1))
                    pool.wait_ge(conv_step, CONV_FIRST + 6 * l + 2)
                    nc.gpsimd.tensor_tensor(xs[:, :], y2[:, :], TAB[l % 2][:, 1, :], mult).then_inc(im_ready, 1)
                    pool.wait_ge(v_ready, l + 1)
                    nc.gpsimd.tensor_tensor(xs[:, :], v_[:, :], TAB[l % 2][:, 1, :], mult).then_inc(im_ready, 1)
                elif step[0] == "centre" and step[1] % 2 == 1 and step[1] // 2 + 2 < DEPTH:
                    l = step[1] // 2 + 2
                    todo += [(l, -1)] + [(l, e) for e in range(9)]

            for n, t in enumerate(LAST_BY_POOL):
                b, i = divmod(t, NT)
                pool.wait_ge(s1_scaled, n + 1)
                nc.gpsimd.tensor_tensor(last_s[n][:, :], last_s[n][:, :], Ds[b][:, i, :], mult).then_inc(pool_gated, 1)
                pool.wait_ge(pool_gated, n + 1)
                pool.wait_ge(*((bias1, 2 * NT) if b else (pre_ready, 3 * NT)))
                nc.gpsimd.tensor_tensor(X2[b][:, i, :], X2[b][:, i, :], last_s[n][:, :], add).then_inc(fin_pool, 1)

        @block.tensor
        def _(pe):
            def turn(b, key, blocks):
                n = use(b, key)
                if n >= 2:
                    pe.wait_ge(tr_free[n % 2], n // 2)
                for c, src in enumerate(blocks):
                    m = nc.tensor.transpose(tr[n % 2][:, c * P:(c + 1) * P], src, ident[:, :])
                m.then_inc(turned, 1)

            def passes(acc, lh, ll, rh, rl, first, last):
                nc.tensor.matmul(acc, lh, rh, start=first, stop=False)
                nc.tensor.matmul(acc, ll, rh, start=False, stop=False)
                return nc.tensor.matmul(acc, lh, rl, start=False, stop=last)

            def unit(b, u):
                n = UNITS * b + u
                return Wh[n % SPLIT], Wl[n % SPLIT]

            def stack_turn(b, g, i):
                t, p = divmod(i, 2)
                pe.wait_ge(ts_ready, 2 * (GROUPS * b + g) + t + 1)
                turn(b, ("stack", g, i), [F32(TS[t][:, 4 * c + 2 * p:4 * c + 2 * p + 2, :].rearrange("p n c -> p (n c)"))
                                          for c in range(NT)])

            def score(acc, q, k, j, hh, qt, c):
                rows, w = slice(64 * hh, 64 * hh + 64), P * (qt + 1)
                nc.tensor.matmul(acc[:, c:c + w], q[rows, j % 2, qt * P:(qt + 1) * P], k[rows, j % 2, 0:w], start=True, stop=False)
                return nc.tensor.matmul(acc[:, c + w - P:c + w], maskL[:, :], maskR[:, :], start=False, stop=True)

            pe.wait_ge(ident_in, 16)

            def norm_turn(k):
                pe.wait_ge(xn_ready, NT * (k + 1))
                for kc in range(KC):
                    n = norm_use(k, kc)
                    if n >= 2:
                        pe.wait_ge(tr_free[n % 2], n // 2)
                    for t in range(NT):
                        m = nc.tensor.transpose(tr[n % 2][:, t * P:(t + 1) * P], NORM[k][1][:, t, kc * P:(kc + 1) * P], ident[:, :])
                    m.then_inc(turned, 1)

            def ffn_triple(b, triple):
                w, kc = divmod(triple, KC)
                if kc == 0:
                    pe.wait_ge(unit_ready, UNITS * b + U_FFN + w + 1)
                    pe.wait_ge(*((v_written, NT * b + 1) if w == 0 else (f_free, FV * b + (5 if w == 1 else 8 + w - 1))))
                wh, wl = unit(b, U_FFN + w)
                c = slice(kc * P, (kc + 1) * P)
                m = passes(fb[w % 2][:, :], wh[:, c], wl[:, c], XNh[:, kc, :], XNl[:, kc, :], kc == 0, kc == KC - 1)
                if kc == KC - 1:
                    m.then_inc(f_ready, 1)

            norm_turn(0)
            for b in range(B):
                f0 = FV * b
                for t in range(3):
                    for kc in range(KC):
                        pe.wait_ge(unit_ready, UNITS * b + U_QKV + 4 * t + kc + 1)
                        if t == 0:
                            n0 = norm_use(b, kc)
                            pe.wait_ge(tr_free[n0 % 2], n0 // 2 + 1)
                        wh, wl = unit(b, U_QKV + 4 * t + kc)
                        if b == 0 and t == 0 and kc == KC - 2:
                            pe.wait_ge(ones_set, 2)
                            pe.wait_ge(asum_ready, 3)
                            nc.tensor.matmul(cx[:, 0:3], V[:, 0, 0:P], asum[:, :], start=True, stop=True).then_inc(tot_ready, 1)
                        for i in range(NT):
                            if kc == 0 and t == 0 and b:
                                pe.wait_ge(ab_ready, NT * b)
                            elif kc == 0 and t == 1:
                                if b:
                                    pe.wait_ge(comb, 2 * NT * (b - 1) + NT)
                                elif i == 1:
                                    pe.wait_ge(theta_ready, 2)
                            elif kc == 0 and t == 2:
                                pe.wait_ge(f_free, f0 + i + 1)
                            c = slice(i * P, (i + 1) * P)
                            m = passes(QKV_BANKS[t % 2][i][:, :], XNh[:, kc, c], XNl[:, kc, c], wh[:, :], wl[:, :], kc == 0, kc == KC - 1)
                            if kc == KC - 1:
                                m.then_inc(f_ready, 1)
                        if kc < KC - 1:
                            m.then_inc(qkv_used, 1)
                for triple in triples_in(-1):
                    ffn_triple(b, triple)
                pe.wait_ge(f_free, f0 + 8)
                for i in range(4):
                    stack_turn(b, 0, i)
                for s in range(SLOTS):
                    if score_in(s):
                        j, i = score_in(s)
                        g, n = j // 2, 5 * PAIRS * b + s
                        if n == 0:
                            pe.wait_ge(mask_ready, 2)
                        if s == 0:
                            pe.wait_ge(v_written, NT * (b + 1))
                        if i == 0:
                            for x in range(4):
                                pe.wait_ge(*copied(b, ("stack", g, x)))
                        if n >= 3:
                            pe.wait_ge(s_free, n - 2)
                        q, k = QS[g % 2], KS[g % 2]
                        for hh, qt, c in S_BANKS[i][:1 if i == 2 else 2]:
                            m = score(sc[n % 3], q, k, j, hh, qt, c)
                        m.then_inc(s_half if i == 2 else s_ready, 1)
                    if ctx_in(s) is not None:
                        g = ctx_in(s)
                        pe.wait_ge(cu_ready, GROUPS * b + g + 1)
                        turn(b, ("ctx", g), [CU[:, t * P:(t + 1) * P] for t in range(NT)])
                    for triple in triples_in(s):
                        ffn_triple(b, triple)
                    if score_in(s) and s % 5 == 2:
                        pe.wait_ge(s_half, PAIRS * b + j + 1)
                        score(sc[n % 3], q, k, j, *S_BANKS[2][1]).then_inc(s_ready, 1)
                    if stack_in(s):
                        stack_turn(b, *stack_in(s))
                    if s == LAST_DOWN:
                        for kc in range(2):
                            turn(b, ("ctxf", kc), [CN[:, t, kc * P:(kc + 1) * P] for t in range(NT)])
                    if down_in(s) is not None:
                        f = down_in(s)
                        pe.wait_ge(hs_ready, FC * b + f + 1)
                        pe.wait_ge(unit_ready, UNITS * b + U_DOWN + f + 1)
                        if f == 0:
                            pe.wait_ge(s_free, 5 * PAIRS * (b + 1))
                            pe.wait_ge(f_free, f0 + FV)
                        wh, wl = unit(b, U_DOWN + f)
                        for t in range(NT):
                            c = slice(t * P, (t + 1) * P)
                            m = passes(dn[t][:, :], hsh[f % 2][:, c], hsl[f % 2][:, c], wh[:, :], wl[:, :], f == 0, f == FC - 1)
                        m.then_inc(down_used, 1)
                    if s == LAST_DOWN:
                        for kc in range(2, KC):
                            turn(b, ("ctxf", kc), [CN[:, t, kc * P:(kc + 1) * P] for t in range(NT)])
                    if turn_in(s):
                        j, i = turn_in(s)
                        pe.wait_ge(s_free, 5 * PAIRS * b + 5 * j + (3 if i < 2 else 5))
                        turn(b, ("p", j, i), [PR[j % 2][:, hh, p_off(qt) + kt * P:p_off(qt) + kt * P + P] for hh, kt, qt in T_BANKS[i]])
                    if pv_in(s) and pv_in(s)[1] < NT:
                        g, kt = pv_in(s)
                        gp = PAIRS * b + 2 * g
                        if kt == 0:
                            for x in range(5):
                                pe.wait_ge(*copied(b, ("p", 2 * g + 1, x)))
                            pe.wait_ge(v_written, NT * (b + 1))
                            if GROUPS * b + g:
                                pe.wait_ge(cu_ready, GROUPS * b + g)
                        for h in range(4):
                            c = t_col(h % 2, kt)
                            m = nc.tensor.matmul(cx[32 * h:32 * h + 32, kt * P:S], V[:, kt, (4 * g + h) * 32:(4 * g + h + 1) * 32],
                                                 PT[(gp + h // 2) % 3][:, c:c + S - kt * P], start=kt == 0, stop=kt == NT - 1,
                                                 skip_group_check=True)
                        if kt == NT - 1:
                            m.then_inc(pv_done, 1)
                    if s == NORM_TURN:
                        norm_turn(b + 1)
                for kc in range(KC):
                    pe.wait_ge(*copied(b, ("ctxf", kc)))
                    pe.wait_ge(unit_ready, UNITS * b + U_OUT + kc + 1)
                    wh, wl = unit(b, U_OUT + kc)
                    for x, i in enumerate(OUT_TILES):
                        if kc == 0 and x == 2:
                            pe.wait_ge(*copied(b, ("ctxf", KC - 2)))
                            pe.wait_ge(*copied(b, ("ctxf", KC - 1)))
                        c = slice(i * P, (i + 1) * P)
                        m = passes(ob[x][:, :], CTh[:, kc, c], CTl[:, kc, c], wh[:, :], wl[:, :], kc == 0, kc == KC - 1)
                        if x == NT - 1:
                            m.then_inc(out_used, 1)
                        elif kc == KC - 1:
                            m.then_inc(o_ready, 1)

            def hidden_item(n, b, f, mm, halfway):
                u = 2 * (FC * b + f) + mm
                if halfway == 0:
                    if b and f < 2:
                        pe.wait_ge(ds1_ready, NT * (b - 1) + 2 * f + mm + 1)
                    elif u >= 4:
                        pe.wait_ge(g1_free, u - 3)
                    elif u >= 2:
                        pe.wait_ge(comb, 2 * NT * (B - 1) + NT)
                    elif mm == 0:
                        pe.wait_ge(ab_ready, NT * B)
                    else:
                        pe.wait_ge(comb, 2 * NT * (B - 1) + NT)
                    if b == 0 and f == 0:
                        pe.wait_ge((tg_in, tu_in)[mm], 16 * KC)
                    if f == 0 and mm == 0:
                        for x in range(2):
                            last = norm_use(B + b, 2 + x)
                            pe.wait_ge(tr_free[last % 2], last // 2 + 1)
                T, (xh, xl) = (TG, TU)[mm], XN1[b]
                for kc in range(2 * halfway, 2 * halfway + 2):
                    lhs = T[:, kc, f * P:(f + 1) * P]
                    nc.tensor.matmul(HB[u % 4][:, :], lhs, xh[:, kc, :], start=kc == 0, stop=False)
                    m = nc.tensor.matmul(HB[u % 4][:, :], lhs, xl[:, kc, :], start=False, stop=kc == KC - 1)
                if halfway:
                    m.then_inc(g1_ready, 1)

            def down_item(b, pr, f):
                d = down_number(b, pr, f)
                if d in (0, TD_PART):
                    pe.wait_ge(td_in[d > 0], 16)
                if f == 0:
                    pe.wait_ge(g1_free, 2 * FC * (b + 1))
                pe.wait_ge(hs1_ready, d + 1)
                for t in range(2):
                    c = slice(t * P, (t + 1) * P)
                    nc.tensor.matmul(dn1[pr][t][:, :], hsH[d % HS][:, c], TD[:, f, :], start=f == 0, stop=False)
                    m = nc.tensor.matmul(dn1[pr][t][:, :], hsL[d % HS][:, c], TD[:, f, :], start=False, stop=f == FC - 1)
                m.then_inc(d1_used, 1)

            for step in STEPS1:
                kind = step[0]
                if kind == "item":
                    it = step[2]
                    if it[0] == "hid":
                        hidden_item(step[1], *it[1:])
                    else:
                        down_item(*it[1:])
                elif kind == "turn":
                    pe.wait_ge(comb, 2 * NT * (B - 1) + NT)
                    norm_turn(3)
                elif kind == "proj":
                    pe.wait_ge(win_ready, 1)
                    pe.wait_ge(comb, 2 * NT * B)
                    for x in range(2):
                        last = norm_use(3, 2 + x)
                        pe.wait_ge(tr_free[last % 2], last // 2 + 1)
                    for b in range(B):
                        cols = slice(64 * (1 - b), 64 * (1 - b) + P)
                        for kc in range(KC):
                            xh, xl = XN1[b]
                            m = passes(sc[0][:, :], winH[:, kc, cols], winL[:, kc, cols], xh[:, kc, :], xl[:, kc, :],
                                       b == 0 and kc == 0, b == 1 and kc == KC - 1)
                    m.then_inc(proj_ready, 1)
                elif kind == "centre":
                    q = step[1]
                    pe.wait_ge(h_ready1, q + 1)
                    nc.tensor.matmul(sc[0][:, :], centre_m[:, :], h_[:, :], start=True, stop=True).then_inc(ctr_ready, 1)
                elif kind == "var":
                    q = step[1]
                    pe.wait_ge(sq_ready, q + 1)
                    for t in range(NT):
                        m = nc.tensor.matmul(tr[1][:, 2 * t:2 * t + 2], sq_[:, t * P:(t + 1) * P], seq_mean[:, :], start=True, stop=True)
                    m.then_inc(var_ready, 1)
                elif kind == "rsT":
                    q = step[1]
                    pe.wait_ge(rs_ready, q + 1)
                    nc.tensor.transpose(tr[1][0:8, P:2 * P], rs1[:, :], ident[:, :]).then_inc(rst_ready, 1)
                elif kind == "spread":
                    q = step[1]
                    pe.wait_ge(rt_ready, q + 1)
                    if q == 0:
                        pe.wait_ge(small1_in, 80)
                    for t in range(NT):
                        m = nc.tensor.matmul(tr[0][:, t * P:(t + 1) * P], sel[:, t, :], rT[:, :], start=True, stop=True)
                    m.then_inc(rb_ready, 1)
                elif kind == "mlp":
                    q, fc = step[1:]
                    l = q // 2
                    pe.wait_ge(yn_ready, l + 1)
                    for b in range(B):
                        n = 4 * l + 2 * fc + b
                        if b == 0:
                            pe.wait_ge(ds_ready, q + 1)
                        if fc:
                            pe.wait_ge(mz_ready, n - 1)
                        rows = slice(64 * b, 64 * b + 64)
                        nc.tensor.matmul(sc[b][:, :], w1T[rows, l, fc * P:(fc + 1) * P], y2[rows, :], start=True, stop=True)\
                            .then_inc(m_ready1, 1)
                elif kind == "mlpout":
                    l = step[1] // 2
                    pe.wait_ge(mu_ready, 4 * (l + 1))
                    for fc in range(2):
                        for b in range(B):
                            m = nc.tensor.matmul(tr[1][64 * b:64 * b + 64, :], w2T[:, l, fc, :], MU[2 * fc + b][:, :],
                                                 start=fc == 0, stop=fc == 1, skip_group_check=True)
                    m.then_inc(o1_ready, 1)
            pe.wait_ge(yn_ready, DEPTH + 1)
            pe.wait_ge(mz_ready, 4 * DEPTH)
            for t in range(B * NT):
                b, i = divmod(t, NT)
                if t >= NT:
                    pe.wait_ge(ds1_ready, 2 * NT)
                rows = slice(64 * b, 64 * b + 64)
                nc.tensor.matmul(LAST_BANKS[t][:, :], y2[rows, i * P:(i + 1) * P], woT[rows, :], start=True, stop=True).then_inc(s1_free, 1)

        @block.scalar
        def _(act):
            def copy_out(n, dst):
                act.wait_ge(turned, n + 1)
                return nc.scalar.activation(dst, tr[n % 2][:, :], ACT.Copy)

            def stack_out(b, g, i):
                t, p = divmod(i, 2)
                n = use(b, ("stack", g, i))
                copy_out(n, (QS, KS)[t][g % 2][:, p, :]).then_inc(tr_free[n % 2], 1)

            def load_rows(w, T, done, chunks):
                for kc in chunks:
                    act.dma_start(F32(T[:, kc, :]), arr_d[w][kc * P:(kc + 1) * P, :]).then_inc(done, 16)

            def magnitudes():
                act.wait_ge(wc_in, 48)
                for w in range(3):
                    nc.scalar.activation(wa[w][:, :], wc[w][:, :], ACT.Abs, accum_out=asum[:, w:w + 1]).then_inc(asum_ready, 1)
            def norm_hi(k):
                for kc in range(KC):
                    copy_out(norm_use(k, kc), NORM[k][2][0][:, kc, :]).then_inc(xh_ready, 1)

            def split_hi(n):
                act.wait_ge(raw_in[n % RAW], 16 * (n // RAW + 1))
                if n >= SPLIT:
                    act.wait_ge(*unit_free(n - SPLIT))
                act.wait_ge(hi_done, n)
                nc.scalar.activation(Wh[n % SPLIT][:, :], raw[n % RAW][:, :], ACT.Copy).then_inc(hi_done, 1)

            def ffn_tanh(b, w):
                if w % 2 == 0:
                    n = FC * b + w // 2
                    act.wait_ge(f_ready, FU * b + 12 + w + 1)
                    if n:
                        act.wait_ge(*(hidden(b, w - 2) if w else hidden(b - 1, 2 * FC - 2)))
                    else:
                        act.wait_ge(mask_ready, 2)
                    nc.scalar.activation(tb[:, :], fb[0][:, :], ACT.Tanh, scale=0.5).then_inc(tanh_ready, 1)

            def stack_hi(b, t):
                act.wait_ge(qk_ready, 8 * (b + 1))
                n = 2 * GROUPS * b + t
                if b:
                    act.wait_ge(turned, use(b - 1, ("stack", GROUPS - 1, 2 * t + 1)) + 1)
                act.wait_ge(ts_hi, n)
                src, hi, _ = stacked(t, 0)
                nc.scalar.activation(hi, src, ACT.Copy).then_inc(ts_hi, 1)

            for u in range(2):
                split_hi(u)
            norm_hi(0)
            for u in range(2, RAW):
                split_hi(u)
            magnitudes()
            for b in range(B):
                for u in range(5 if b else RAW, HI_BY_ACT):
                    split_hi(UNITS * b + u)
                    if b == 0 and u == 10:
                        for w in range(3):
                            act.wait_ge(tern_ready, w + 1)
                            nc.scalar.activation(wp[w][:, :], F32(wm[w][:, :]), ACT.Copy, scale=-1.0).then_inc(wp_ready, 1)
                            act.wait_ge(wp_ready, w + 1)
                            for x, src in enumerate((wp[w], wm[w])):
                                act.dma_start(tern_d[w][x].rearrange("(p n) -> p n", p=P), F32(src[:, :])).then_inc(tern_stored, 16)
                for i in range(NT):
                    act.wait_ge(f_ready, FU * b + 9 + i)
                    if b == 0 and i == 0:
                        act.wait_ge(ones_set, 2)
                    nc.scalar.activation(V[:, i, :].rearrange("p (h c) -> p h c", c=32)[:, :, 0:D],
                                         QKV_BANKS[0][i][:, :].rearrange("p (h d) -> p h d", d=D), ACT.Copy).then_inc(v_written, 1)
                for t in range(2):
                    stack_hi(b, t)
                ffn_tanh(b, 0)
                for i in (0, 2):
                    stack_out(b, 0, i)
                if b == 0:
                    act.wait_ge(tern_stored, 96)
                for s in range(SLOTS):
                    if score_in(s):
                        j, i = score_in(s)
                        n = 5 * PAIRS * b + s
                        if i == 0 and j >= 2:
                            act.wait_ge(turned, use(b, ("p", j - 2, 4)) + 1)
                        act.wait_ge(m_ready, n + 1)
                        for x, (hh, qt, c) in enumerate(S_BANKS[i]):
                            w = P * (qt + 1)
                            e = nc.scalar.activation(PR[j % 2][:, hh, p_off(qt):p_off(qt) + w], sc[n % 3][:, c:c + w], ACT.Exp,
                                                     bias=nm[:, j % 2, S_COL[i] + x:S_COL[i] + x + 1], scale=-1.0)
                        e.then_inc(s_free, 1)
                    for w in ffn_units_after(s):
                        ffn_tanh(b, w)
                    if stack_in(s) and stack_in(s)[1] % 2 == 0:
                        stack_out(b, *stack_in(s))
                    if down_in(s + 1) is not None:
                        f = down_in(s + 1)
                        act.wait_ge(*hidden(b, 2 * f + 1))
                        if f >= 2:
                            act.wait_ge(down_used, FC * b + f - 1)
                        nc.scalar.activation(hsh[f % 2][:, :], HT[:, f, :], ACT.Copy).then_inc(hs_hi, 1)
                    for u in range(U_DOWN, UNITS):
                        if s == DOWN_HI[u - U_DOWN]:
                            split_hi(UNITS * b + u)
                    if turn_in(s) and turn_in(s)[1] in T_BY_ACT:
                        j, i = turn_in(s)
                        gp = PAIRS * b + j
                        if i == 0 and gp >= 3:
                            act.wait_ge(pv_done, (gp - 3) // 2 + 1)
                        n = use(b, ("p", j, i))
                        copy_out(n, PT[gp % 3][:, 512 * i:512 * i + 512]).then_inc(tr_free[n % 2], 1)
                    if pv_in(s) and pv_in(s)[1] == NT:
                        g = pv_in(s)[0]
                        act.wait_ge(pv_done, GROUPS * b + g + 1)
                        if g:
                            act.wait_ge(turned, use(b, ("ctx", g - 1)) + 1)
                        nc.scalar.activation(CU[:, :], cx[:, :], ACT.Copy).then_inc(cu_ready, 1)
                    if s == 5 * PAIRS:
                        if b:
                            act.wait_ge(x2_stored, 16)
                        act.dma_start(XB[:, :, :], (x2_d[0] if b else x_d[1]).rearrange("t p e -> p t e")).then_inc(xb_in, 16)
                    if s == NORM_TURN:
                        norm_hi(b + 1)
                    if b == B - 1 and s == LAST_DOWN - 1:
                        load_rows(W_UP, TU, tu_in, range(KC - 1))
                        for dst, src in ((w1T[:, :, :], A["w1T"]), (w2T[:, :, :, :], A["w2T"]), (woT[:, :], A["woT"]),
                                         (sel[:, :, :], A["sel"]), (bout[:, :], A["bout"].partition_broadcast(P))):
                            act.dma_start(dst, src).then_inc(small1_in, 16)
                    if s == LAST_DOWN:
                        for kc in range(KC):
                            n = use(b, ("ctxf", kc))
                            act.wait_ge(turned, n + 1)
                            nc.scalar.activation(CTh[:, kc, :], tr[n % 2][:, :], ACT.Identity, bias=v_bias[:, kc:kc + 1]).then_inc(ct_hi, 1)
                    if b == B - 1 and s == 5 * PAIRS:
                        act.wait_ge(*copied(b, ("stack", GROUPS - 1, 3)))
                        act.wait_ge(arranged, 16 * len(ARRANGE))
                        load_rows(W_GATE, TG, tg_in, range(KC))
                if b == B - 1:
                    act.wait_ge(turned, use(b, ("ctxf", KC - 1)) + 1)
                    load_rows(W_UP, TU, tu_in, [KC - 1])
                if b < B - 1:
                    split_hi(UNITS * (b + 1))
                act.wait_ge(down_used, FC * (b + 1))
                for i in OUT_TILES:
                    nc.scalar.activation(gt[i][:, :], dn[i][:, :], ACT.Tanh, scale=0.25).then_inc(dtanh, 1)
                if b < B - 1:
                    for u in range(1, 5):
                        split_hi(UNITS * (b + 1) + u)
                if b == 0:
                    act.wait_ge(polar_ready, 1)
                    nc.scalar.activation(decay[:, :], ph[:, 7, :], ACT.Tanh).then_inc(decay_ready, 1)

            for step in STEPS1:
                kind = step[0]
                if kind == "item":
                    _, n, it = step
                    if it[0] == "hid" and it[3] == 0 and it[4] == 1:
                        _, b, f, _, _ = it
                        act.wait_ge(g1_ready, 2 * (FC * b + f) + 1)
                        n1 = FC * b + f
                        if n1 >= 2:
                            act.wait_ge(g1_free, 2 * n1 - 3)
                        if b and f < 2:
                            act.wait_ge(ds1_ready, NT * b - 1 + f)
                        nc.scalar.activation(t1[f % 2][:, :], HB[2 * n1 % 4][:, :], ACT.Tanh, scale=scales[:, 0:1]).then_inc(t1_ready, 1)
                    nxt = items1()[n + AHEAD] if n + AHEAD < len(items1()) else None
                    if nxt and nxt[0] == "down":
                        _, b, pr, f = nxt
                        d = down_number(b, pr, f)
                        act.wait_ge(g1_free, 2 * (FC * b + f) + 2)
                        if d >= HS:
                            act.wait_ge(d1_used, d - HS + 1)
                        nc.scalar.activation(hsH[d % HS][:, :], H1[:, f, 256 * pr:256 * pr + 256], ACT.Copy).then_inc(hs1_hi, 1)
                    if it[0] == "down" and it[3] == FC - 1:
                        _, b, pr, f = it
                        act.wait_ge(d1_used, down_number(b, pr, f) + 1)
                        for t in range(2):
                            n = 2 * (2 * b + pr) + t
                            act.wait_ge(g1_free, 2 * FC * (b + 1))
                            if n >= 2:
                                act.wait_ge(ds1_ready, n - 1)
                            nc.scalar.activation(t1[t][:, :], dn1[pr][t][:, :], ACT.Tanh, scale=scales[:, 1:2]).then_inc(d1_tanh, 1)
                elif kind == "turn":
                    act.wait_ge(out_used, KC * B)
                    norm_hi(3)
                elif kind == "centre":
                    q = step[1]
                    act.wait_ge(ctr_ready, q + 1)
                    nc.scalar.activation(sq_[:, :], sc[0][:, :], ACT.Square).then_inc(sq_ready, 1)
                    nc.scalar.activation(dS[:, :], sc[0][:, :], ACT.Copy).then_inc(ds_ready, 1)
                elif kind == "rsT":
                    q = step[1]
                    act.wait_ge(rst_ready, q + 1)
                    nc.scalar.activation(rT[:, :], tr[1][0:8, P:2 * P], ACT.Copy).then_inc(rt_ready, 1)
                elif kind == "spread" and step[1] % 2 == 0 and step[1] < 2 * DEPTH:
                    q = step[1]
                    l = q // 2
                    act.wait_ge(y_ready, q + 1)
                    if q == 0:
                        act.wait_ge(vecs_ready, 4)
                    nc.scalar.activation(tz[:, :], y_[:, :], ACT.Tanh, bias=hln[:, 4 + l:5 + l], scale=hln[:, l:l + 1]).then_inc(tz_ready, 1)
                elif kind == "mlp":
                    q, fc = step[1:]
                    l = q // 2
                    for b in range(B):
                        n = 4 * l + 2 * fc + b
                        act.wait_ge(m_ready1, n + 1)
                        if n >= 2:
                            act.wait_ge(mu_ready, n - 1)
                        c = 2 * l + fc
                        nc.scalar.activation(MT[b][:, :], sc[b][:, :], ACT.Tanh, bias=hb1v[:, c:c + 1], scale=0.5).then_inc(mt_ready, 1)
                        nc.scalar.activation(MZ[b][:, :], sc[b][:, :], ACT.Identity, bias=b1v[:, c:c + 1]).then_inc(mz_ready, 1)

            for n, t in enumerate(LAST_BY_POOL):
                act.wait_ge(s1_free, t + 1)
                act.wait_ge(ds1_ready, 2 * NT)
                if n == 0:
                    act.wait_ge(pre_ready, 3 * NT)
                nc.scalar.activation(last_s[n][:, :], LAST_BANKS[t][:, :], ACT.Copy, scale=scales[:, 1:2]).then_inc(s1_scaled, 1)

        @block.vector
        def _(dve):
            def minus_hi(n, dst, hi):
                nc.vector.tensor_tensor(dst, tr[n % 2][:, :], F32(hi), ALU.subtract).then_inc(tr_free[n % 2], 1)

            def stack_out(b, g, i):
                t, p = divmod(i, 2)
                n = use(b, ("stack", g, i))
                dve.wait_ge(turned, n + 1)
                nc.vector.tensor_copy((QS, KS)[t][g % 2][:, p, :], tr[n % 2][:, :]).then_inc(tr_free[n % 2], 1)

            def norm_stats(k):
                if k in (1, 2):
                    dve.wait_ge(xb_in, 16 * k)
                if k:
                    dve.wait_ge(xn_ready, NT * k)
                for t in range(NT):
                    if k == 0:
                        dve.wait_ge(x_in[t], 16)
                    nc.vector.bn_stats(stat[:, t, :], NORM[k][0][:, t, :]).then_inc(stats, 1)
                for t in range(NT):
                    dve.wait_ge(stats, NT * k + t + 1)
                    nc.vector.bn_aggr(mv[:, t, :], stat[:, t, :]).then_inc(mv_ready, 1)

            def norm_rows(k):
                dve.wait_ge(mv_ready, NT * (k + 1))
                dve.wait_ge(rstd_ready, k + 1)
                for t in range(NT):
                    nc.vector.tensor_scalar(NORM[k][1][:, t, :], NORM[k][0][:, t, :], mv[:, t, 0:1], rstd[:, t:t + 1],
                                            ALU.subtract, ALU.mult).then_inc(xn_ready, 1)

            def norm_lo(k):
                for kc in range(KC):
                    dve.wait_ge(xh_ready, KC * k + kc + 1)
                    minus_hi(norm_use(k, kc), NORM[k][2][1][:, kc, :], NORM[k][2][0][:, kc, :])

            def ffn_out(b, w):
                n = FC * b + w // 2
                dve.wait_ge(f_ready, FU * b + 12 + w + 1)
                if w % 2 == 0:
                    dve.wait_ge(tanh_ready, n + 1)
                    if n:
                        dve.wait_ge(*(hidden(b, w - 1) if w else hidden(b - 1, 2 * FC - 1)))
                    nc.vector.scalar_tensor_tensor(out=ab[:, :], in0=tb[:, :], scalar=1.0, in1=fb[0][:, :],
                                                   op0=ALU.add, op1=ALU.mult).then_inc(f_free, 1)
                else:
                    dve.wait_ge(*hidden(b, w - 1))
                    nc.vector.tensor_tensor(HT[:, w // 2, :], ab[:, :], fb[1][:, :], ALU.mult)\
                        .then_inc(f_free, 1)

            def qk_bias(b, t, i):
                n, r = 4 * t + i, 8 * b + 4 * t + i
                dve.wait_ge(f_ready, FU * b + n + 1)
                if r >= 2:
                    dve.wait_ge(r1_ready, r - 1)
                    dve.wait_ge(r2_ready, 2 * (r - 1))
                nc.vector.tensor_tensor(rx[r % 2][:, :], QKV_BANKS[t][i][:, :], qkv_bias[:, t * E:(t + 1) * E], ALU.add)\
                    .then_inc(f_free, 1)

            def qk_turned_part(b, t, i):
                r = 8 * b + 4 * t + i
                dve.wait_ge(f_free, FV * b + 4 * t + i + 1)
                if r:
                    dve.wait_ge(qk_ready, r)
                x4 = rx[r % 2][:, :].rearrange("p (h c d) -> p h c d", c=2, d=D // 2)
                y4 = r2[:, :].rearrange("p (h c d) -> p h c d", c=2, d=D // 2)
                for c in range(2):
                    nc.vector.tensor_tensor(y4[:, :, c, :], x4[:, :, 1 - c, :],
                                            wide(rope[:, 2 * t + 1, i, c * 8:c * 8 + 8], H), ALU.mult).then_inc(r2_ready, 1)

            def qk_add(b, t, i):
                r = 8 * b + 4 * t + i
                dve.wait_ge(r2_ready, 2 * (r + 1))
                dve.wait_ge(r1_ready, r + 1)
                nc.vector.tensor_tensor(QK[t][:, :, i, :], r1[r % 2][:, :].rearrange("p (g c) -> p g c", c=64),
                                        r2[:, :].rearrange("p (g c) -> p g c", c=64), ALU.add).then_inc(qk_ready, 1)

            norm_stats(0)
            norm_rows(0)
            norm_lo(0)
            dve.wait_ge(const_in, 80)
            nc.vector.tensor_copy(maskL[:, :], tb[:, 0:P]).then_inc(mask_ready, 1)
            nc.vector.tensor_copy(maskR[:, :], tb[:, P:2 * P]).then_inc(mask_ready, 1)
            for b in range(B):
                if b == 0:
                    dve.wait_ge(tot_ready, 1)
                    mean = 1.0 / (OCT * H8 * C1)
                    nc.vector.tensor_scalar(theta[:, 0, :], cx[:, 0:3], mean, 0.5, ALU.mult, ALU.mult).then_inc(theta_ready, 1)
                    nc.vector.tensor_scalar(theta[:, 1, :], cx[:, 0:3], mean, -0.5, ALU.mult, ALU.mult).then_inc(theta_ready, 1)
                    dve.wait_ge(theta_ready, 2)
                    nc.vector.tensor_copy(scales[:, 0:1], theta[:, 0, 0:1]).then_inc(scale_ready, 1)
                    nc.vector.tensor_tensor(scales[:, 2:3], theta[:, 0, 0:1], theta[:, 0, 1:2], ALU.mult).then_inc(scale_ready, 1)
                    dve.wait_ge(scale_ready, 2)
                    nc.vector.tensor_scalar(scales[:, 1:2], scales[:, 2:3], theta[:, 0, 2:3], 2.0, ALU.mult, ALU.mult).then_inc(scale_ready, 1)
                    for w in range(3):
                        nc.vector.tensor_scalar(wa[w][:, :], wc[w][:, :], theta[:, 0, w:w + 1], None, ALU.is_gt).then_inc(tern_a, 1)
                        dve.wait_ge(tern_a, w + 1)
                        nc.vector.scalar_tensor_tensor(out=wm[w][:, :], in0=wc[w][:, :], scalar=theta[:, 1, w:w + 1], in1=wa[w][:, :],
                                                       op0=ALU.is_lt, op1=ALU.subtract).then_inc(tern_ready, 1)
                for t in range(2):
                    qk_bias(b, t, 0)
                    for i in range(NT):
                        qk_turned_part(b, t, i)
                        if i + 1 < NT:
                            qk_bias(b, t, i + 1)
                        qk_add(b, t, i)
                ffn_out(b, 0)
                ffn_out(b, 1)
                for i in (1, 3):
                    stack_out(b, 0, i)
                for s in range(SLOTS):
                    if score_in(s):
                        j, i = score_in(s)
                        n = 5 * PAIRS * b + s
                        dve.wait_ge(s_ready, n + 1)
                        col = S_COL[i]
                        if i == 2:
                            m = nc.vector.tensor_reduce(nm[:, j % 2, col:col + 2], sc[n % 3][:, :].rearrange("p (a c) -> p a c", a=2),
                                                        AX.X, ALU.min)
                        else:
                            for x, (hh, qt, c) in enumerate(S_BANKS[i]):
                                m = nc.vector.tensor_reduce(nm[:, j % 2, col + x:col + x + 1], sc[n % 3][:, c:c + P * (qt + 1)],
                                                            AX.X, ALU.min)
                        m.then_inc(m_ready, 1)
                    if ctx_in(s) is not None:
                        g = ctx_in(s)
                        n = use(b, ("ctx", g))
                        dve.wait_ge(turned, n + 1)
                        c3 = tr[n % 2][:, :].rearrange("p (n c) -> p n c", c=32)
                        if g:
                            dve.wait_ge(*copied(b, ("ctx", g - 1)))
                        nc.vector.reciprocal(rinv[:, :], c3[:, :, D]).then_inc(rinv_ready, 1)
                        dve.wait_ge(rinv_ready, GROUPS * b + g + 1)
                        nc.vector.tensor_tensor(CN[:, :, g * 64:(g + 1) * 64].rearrange("p t (h d) -> p t h d", d=D),
                                                c3[:, :, 0:D].rearrange("p (t h) d -> p t h d", t=NT),
                                                rinv[:, :].rearrange("p (t h) -> p t h", t=NT).unsqueeze(3).broadcast_to([P, NT, 4, D]),
                                                ALU.mult).then_inc(tr_free[n % 2], 1)
                    for w in ffn_units_after(s):
                        ffn_out(b, w)
                    if stack_in(s) and stack_in(s)[1] % 2 == 1:
                        stack_out(b, *stack_in(s))
                    if down_in(s + 1) is not None:
                        f = down_in(s + 1)
                        dve.wait_ge(hs_hi, FC * b + f + 1)
                        nc.vector.tensor_tensor(hsl[f % 2][:, :], HT[:, f, :], F32(hsh[f % 2][:, :]), ALU.subtract).then_inc(hs_ready, 1)
                    if turn_in(s) and turn_in(s)[1] not in T_BY_ACT:
                        j, i = turn_in(s)
                        gp = PAIRS * b + j
                        if i == 1 and gp == 0:
                            dve.wait_ge(tern_stored, 96)
                        if i == 1 and gp >= 3:
                            dve.wait_ge(pv_done, (gp - 3) // 2 + 1)
                        n = use(b, ("p", j, i))
                        dve.wait_ge(turned, n + 1)
                        nc.vector.tensor_copy(PT[gp % 3][:, 512 * i:512 * i + 512], tr[n % 2][:, :])\
                            .then_inc(tr_free[n % 2], 1)
                    if s == NORM_STATS:
                        norm_stats(b + 1)
                    if s == NORM_ROWS:
                        norm_rows(b + 1)
                    if s == NORM_TURN:
                        norm_lo(b + 1)
                    if s == LAST_DOWN:
                        for kc in range(KC):
                            dve.wait_ge(ct_hi, KC * b + kc + 1)
                            n = use(b, ("ctxf", kc))
                            nc.vector.scalar_tensor_tensor(out=CTl[:, kc, :], in0=tr[n % 2][:, :], scalar=v_bias[:, kc:kc + 1],
                                                           in1=F32(CTh[:, kc, :]), op0=ALU.add, op1=ALU.subtract).then_inc(tr_free[n % 2], 1)
                for t in range(NT):
                    dve.wait_ge(x_in[t], 16 * (b + 1))
                for x, i in enumerate(OUT_TILES):
                    n = NT * b + x
                    dve.wait_ge(dtanh, n + 1)
                    nc.vector.scalar_tensor_tensor(out=ga[i][:, :], in0=gt[i][:, :], scalar=1.0, in1=dn[i][:, :],
                                                   op0=ALU.add, op1=ALU.mult).then_inc(ab_ready, 1)
                for x, i in enumerate(OUT_TILES):
                    n = NT * b + x
                    dve.wait_ge(ab_ready, n + 1)
                    nc.vector.tensor_tensor(gt[i][:, :], ga[i][:, :], out_bias[:, :], ALU.mult).then_inc(bias_step, 1)
                for x, i in enumerate(OUT_TILES):
                    n = NT * b + x
                    dve.wait_ge(bias_step, 2 * NT * b + x + 1)
                    nc.vector.scalar_tensor_tensor(out=X[:, i, :], in0=gt[i][:, :], scalar=0.25, in1=X[:, i, :],
                                                   op0=ALU.mult, op1=ALU.add).then_inc(bias_step, 1)
                for x, i in enumerate(OUT_TILES):
                    dve.wait_ge(*((o_ready, (NT - 1) * b + x + 1) if x < NT - 1 else (out_used, KC * (b + 1))))
                    nc.vector.tensor_tensor(ga[i][:, :], ga[i][:, :], ob[x][:, :], ALU.mult).then_inc(comb, 1)
                for x, i in enumerate(OUT_TILES):
                    dve.wait_ge(comb, 2 * NT * b + x + 1)
                    dve.wait_ge(bias_step, 2 * NT * b + NT + x + 1)
                    nc.vector.scalar_tensor_tensor(out=X[:, i, :], in0=ga[i][:, :], scalar=0.25, in1=X[:, i, :],
                                                   op0=ALU.mult, op1=ALU.add).then_inc(comb, 1)

            steps = [0]

            def step_done(ins):
                steps[0] += 1
                ins.then_inc(conv_step, 1)
                dve.wait_ge(conv_step, steps[0])

            dve.wait_ge(comb, 2 * NT * B)
            nc.vector.tensor_scalar(hln[:, :], vec[:, V_LN1:V_LN1 + 8], 0.5, None, ALU.mult).then_inc(vecs_ready, 1)
            nc.vector.tensor_scalar(hscl[:, :], vec[:, V_SCL:V_SCL + 4], 0.5, None, ALU.mult).then_inc(vecs_ready, 1)
            nc.vector.tensor_scalar(init[:, 0, :], vec[:, V_LRE:V_LRE + 4], 2.0, None, ALU.mult).then_inc(vecs_ready, 1)
            nc.vector.tensor_scalar(hb1v[:, :], b1v[:, :], 0.5, None, ALU.mult).then_inc(vecs_ready, 1)
            step_done(nc.vector.tensor_scalar(init[:, 1, :], vec[:, V_LIM:V_LIM + 4], -2.0, None, ALU.mult))
            dve.wait_ge(vecs_ready, 4)

            def normed(q):
                dve.wait_ge(rb_ready, q + 1)
                dve.wait_ge(ds_ready, q + 1)
                nc.vector.tensor_tensor(y_[:, :], dS[:, :], tr[0][:, :], ALU.mult).then_inc(y_ready, 1)
                dve.wait_ge(y_ready, q + 1)

            for step in STEPS1:
                kind = step[0]
                if kind == "item":
                    _, n, it = step
                    if it[0] == "hid" and it[4] == 1:
                        _, b, f, mm, _ = it
                        u = 2 * (FC * b + f) + mm
                        dve.wait_ge(g1_ready, u + 1)
                        if mm == 0:
                            dve.wait_ge(t1_ready, FC * b + f + 1)
                            if u:
                                dve.wait_ge(g1_free, u)
                            nc.vector.scalar_tensor_tensor(out=ab1[f % 2][:, :], in0=t1[f % 2][:, :], scalar=1.0, in1=HB[u % 4][:, :],
                                                           op0=ALU.add, op1=ALU.mult).then_inc(g1_free, 1)
                        else:
                            dve.wait_ge(g1_free, u)
                            if b == 1:
                                dve.wait_ge(hs1_ready, FC + f + 1)
                            nc.vector.tensor_tensor(H1[:, f, :], ab1[f % 2][:, :], HB[u % 4][:, :], ALU.mult).then_inc(g1_free, 1)
                    if it[0] == "down" and it[3] == FC - 1:
                        _, b, pr, f = it
                        for t in range(2):
                            n = 2 * (2 * b + pr) + t
                            dve.wait_ge(d1_tanh, n + 1)
                            if b == 1:
                                dve.wait_ge(proj_ready, 1)
                            nc.vector.scalar_tensor_tensor(out=Ds[b][:, 2 * pr + t, :], in0=t1[t][:, :], scalar=1.0, in1=dn1[pr][t][:, :],
                                                           op0=ALU.add, op1=ALU.mult).then_inc(ds1_ready, 1)
                        for t in range(2 * b):
                            n = 2 * (2 * b + pr) + t
                            dve.wait_ge(ds1_ready, n + 1)
                            nc.vector.scalar_tensor_tensor(out=ab1[t][:, :], in0=Ds[b][:, 2 * pr + t, :], scalar=scales[:, 1:2],
                                                           in1=bout[:, :], op0=ALU.mult, op1=ALU.mult).then_inc(bias1, 1)
                        for t in range(2 * b):
                            dve.wait_ge(bias1, 4 * pr + t + 1)
                            nc.vector.tensor_tensor(X2[b][:, 2 * pr + t, :], X2[b][:, 2 * pr + t, :], ab1[t][:, :], ALU.add).then_inc(bias1, 1)
                elif kind == "norm":
                    norm_stats(3)
                elif kind == "rows":
                    norm_rows(3)
                elif kind == "turn":
                    norm_lo(3)
                elif kind == "proj":
                    dve.wait_ge(proj_ready, 1)
                    nc.vector.tensor_scalar(h_[:, :], sc[0][:, :], vec[:, V_BIN:V_BIN + 1], None, ALU.add).then_inc(h_ready1, 1)
                elif kind == "var":
                    q = step[1]
                    dve.wait_ge(var_ready, q + 1)
                    nc.vector.tensor_scalar(ve1[:, :], tr[1][:, 0:8], EPS, None, ALU.add).then_inc(ve_ready, 1)
                elif kind == "spread":
                    q = step[1]
                    l = q // 2
                    normed(q)
                    if q == 2 * DEPTH:
                        nc.vector.tensor_scalar(y2[:, :], y_[:, :], vec[:, V_LNL:V_LNL + 1], vec[:, V_LNL + 1:V_LNL + 2],
                                                ALU.mult, ALU.add).then_inc(yn_ready, 1)
                    elif q % 2 == 0:
                        C, Sn = TAB[l % 2][:, 0, :], TAB[l % 2][:, 1, :]
                        step_done(nc.vector.tensor_scalar(z_[:, :], y_[:, :], vec[:, V_LN1 + l:V_LN1 + l + 1],
                                                          vec[:, V_LN1 + 4 + l:V_LN1 + 5 + l], ALU.mult, ALU.add))
                        dve.wait_ge(tz_ready, l + 1)
                        step_done(nc.vector.scalar_tensor_tensor(out=y2[:, :], in0=tz[:, :], scalar=1.0, in1=z_[:, :],
                                                                 op0=ALU.add, op1=ALU.mult))
                        dve.wait_ge(tab_step, 37 * (l + 1))
                        nc.vector.tensor_tensor(xc[:, :], y2[:, :], C, ALU.mult).then_inc(conv_step, 1)
                        steps[0] += 1
                        if l == 0:
                            dve.wait_ge(decay_ready, 1)
                        r = decay[:, l:l + 1].broadcast_to([P, S])
                        dve.wait_ge(conv_step, steps[0])
                        nc.vector.tensor_tensor_scan(w_[:, :], r, xc[:, :], init[:, 0, l:l + 1], ALU.mult, ALU.add).then_inc(conv_step, 1)
                        dve.wait_ge(im_ready, 2 * l + 1)
                        nc.vector.tensor_tensor_scan(v_[:, :], r, xs[:, :], init[:, 1, l:l + 1], ALU.mult, ALU.add).then_inc(v_ready, 1)
                        steps[0] += 1
                        dve.wait_ge(conv_step, steps[0])
                        step_done(nc.vector.tensor_tensor(xc[:, :], w_[:, :], C, ALU.mult))
                        dve.wait_ge(im_ready, 2 * l + 2)
                        step_done(nc.vector.tensor_tensor(w_[:, :], xc[:, :], xs[:, :], ALU.add))
                        nc.vector.scalar_tensor_tensor(out=h_[:, :], in0=w_[:, :], scalar=hscl[:, l:l + 1], in1=h_[:, :],
                                                       op0=ALU.mult, op1=ALU.add).then_inc(h_ready1, 1)
                    else:
                        nc.vector.tensor_scalar(y2[:, :], y_[:, :], vec[:, V_LN2 + l:V_LN2 + l + 1],
                                                vec[:, V_LN2 + 4 + l:V_LN2 + 5 + l], ALU.mult, ALU.add).then_inc(yn_ready, 1)
                        dve.wait_ge(h_ready1, q + 1)
                        nc.vector.tensor_scalar(hb_[:, :], h_[:, :], vec[:, V_B2 + l:V_B2 + l + 1], None, ALU.add).then_inc(hb_ready, 1)
                elif kind == "mlp":
                    q, fc = step[1:]
                    l = q // 2
                    for b in range(B):
                        n = 4 * l + 2 * fc + b
                        dve.wait_ge(mt_ready, n + 1)
                        dve.wait_ge(mz_ready, n + 1)
                        nc.vector.scalar_tensor_tensor(out=MU[2 * fc + b][:, :], in0=MT[b][:, :], scalar=1.0, in1=MZ[b][:, :],
                                                       op0=ALU.add, op1=ALU.mult).then_inc(mu_ready, 1)
                elif kind == "mlpout":
                    l = step[1] // 2
                    dve.wait_ge(o1_ready, l + 1)
                    dve.wait_ge(hb_ready, l + 1)
                    nc.vector.scalar_tensor_tensor(out=h_[:, :], in0=tr[1][:, :], scalar=0.5, in1=hb_[:, :],
                                                   op0=ALU.mult, op1=ALU.add).then_inc(h_ready1, 1)
            for n, t in enumerate(t for t in range(B * NT) if t not in LAST_BY_POOL):
                b, i = divmod(t, NT)
                dve.wait_ge(s1_free, t + 1)
                dve.wait_ge(*((bias1, 2 * NT) if b else (pre_ready, 3 * NT)))
                nc.vector.scalar_tensor_tensor(out=Ds[b][:, i, :], in0=Ds[b][:, i, :], scalar=scales[:, 1:2], in1=LAST_BANKS[t][:, :],
                                               op0=ALU.mult, op1=ALU.mult).then_inc(s1_ready, 1)
                dve.wait_ge(s1_ready, n + 1)
                nc.vector.tensor_tensor(X2[b][:, i, :], X2[b][:, i, :], Ds[b][:, i, :], ALU.add).then_inc(fin, 1)


S_COL = [0, 1, 3, 5, 6]


V_BIN, V_LN1, V_RE, V_IM, V_LRE, V_LIM, V_SCL, V_LN2, V_B2, V_LNL, NVEC = 0, 1, 9, 13, 17, 21, 25, 29, 37, 41, 43


def constants():
    half = D // 2
    inv_freq = (1.0 / np.float32(10000.0) ** (np.arange(half, dtype=np.float32) / np.float32(half))).astype(np.float32)
    ang = (np.arange(S, dtype=np.float32)[:, None] * inv_freq[None, :]).astype(np.float32)
    cos, sin = np.cos(ang).astype(np.float32), np.sin(ang).astype(np.float32)
    c2, s2 = np.concatenate([cos, cos], 1), np.concatenate([-sin, sin], 1)
    scale = np.float32(-0.25)
    rope = np.stack([c2 * scale, s2 * scale, c2, s2])
    rope = np.ascontiguousarray(rope.reshape(4, NT, P, D).transpose(2, 0, 1, 3))
    return {
        "ident": np.eye(P, dtype=np.float32),
        "rope": rope.astype(np.float32),
        "centre": np.kron(np.eye(B), np.eye(C1) - 1.0 / C1).astype(np.float32),
        "seq_mean": (np.kron(np.eye(B), np.ones((C1, 1))) / C1).astype(np.float32),
        "sel": np.stack([[np.repeat(np.arange(B) + 2 * t == r, C1) for t in range(NT)] for r in range(8)]).astype(np.float32),
        "zeros": np.zeros((HCOLS - HID1) * E, np.float32),
        "mask": np.concatenate([np.eye(P) * MASK_L, np.triu(np.ones((P, P)), 1) * MASK_R], 1).astype(np.float32),
    }


def layout(inputs):
    x = np.asarray(inputs["L0_attn_hidden_states"]).reshape(B, NT, P, E)
    w_qkv = np.asarray(inputs["L0_attn_qkv_w"])
    units = np.zeros((UNITS, P, 512), np.float32)
    for t in range(3):
        for kc in range(KC):
            units[U_QKV + 4 * t + kc] = w_qkv[kc * P:(kc + 1) * P, t * E:(t + 1) * E]
    for m, name in enumerate(("L0_ffn_W_gate", "L0_ffn_W_up")):
        w = np.asarray(inputs[name])
        pad = np.zeros((FC * P, E), np.float32)
        pad[:w.shape[0]] = w
        u = pad.reshape(FC, P, KC, P).transpose(0, 3, 2, 1)
        units[U_FFN + m:U_DOWN:2] = u.reshape(FC, P, 512)
    w = np.asarray(inputs["L0_ffn_W_down"])
    pad = np.zeros((FC * P, E), np.float32)
    pad[:w.shape[1]] = w.T
    units[U_DOWN:U_OUT] = pad.reshape(FC, P, E)
    units[U_OUT:] = np.asarray(inputs["L0_attn_out_w"]).reshape(KC, P, E)
    g = {k[8:]: np.asarray(v) for k, v in inputs.items() if k.startswith("L1_attn_")}
    v4 = [g[k].T for k in ("ln1_w", "ln1_b", "phz_re", "phz_im", "lc_re", "lc_im", "sc_lin", "ln2_w", "ln2_b", "b2")]
    vec = np.concatenate([g["bin"][:, None], *v4, g["lnl_w"][:, None], g["lnl_b"][:, None]], 1)
    win = np.zeros((P, KC, 192), np.float32)
    win[:, :, 64:128] = g["Win"].T.reshape(KC, P, C1).transpose(1, 0, 2)
    block1 = {
        "vec": np.concatenate([vec, vec], 0),
        "b1v": np.ascontiguousarray(g["b1"].reshape(DEPTH, 2, P).transpose(2, 0, 1).reshape(P, 2 * DEPTH)),
        "win": win,
        "w1T": np.concatenate([g["W1"].transpose(2, 0, 1)] * 2, 0),
        "w2T": np.ascontiguousarray(g["W2"].transpose(2, 0, 1).reshape(2, P, DEPTH, C1).transpose(1, 2, 0, 3)),
        "woT": np.concatenate([g["Wout"].T] * 2, 0),
        "bout": g["bout"],
        "tern_w": np.stack([np.asarray(inputs["L1_ffn_" + k]).transpose(0, 2, 1).reshape(P, FLAT) for k in ("w_gate", "w_up", "w_down")]),
    }
    return {
        **block1,
        "x": np.ascontiguousarray(x), "w0": units,
        "qk_bias": np.asarray(inputs["L0_attn_qkv_b"])[:2 * E],
        "v_bias": np.ascontiguousarray(np.asarray(inputs["L0_attn_qkv_b"])[2 * E:].reshape(KC, P).T),
        "out_b": np.asarray(inputs["L0_attn_out_b"]),
    }


def kernel(**inputs):
    import concourse.bacc as bacc
    from concourse.bass_utils import run_bass_kernel_spmd

    nc = bacc.Bacc("TRN2", target_bir_lowering=False, num_devices=1)
    arrays = {name: np.ascontiguousarray(a) for name, a in {**layout(inputs), **constants()}.items()}
    A = {name: nc.dram_tensor(name, a.shape, mybir.dt.from_np(a.dtype), kind="ExternalInput").ap() for name, a in arrays.items()}
    out = nc.dram_tensor("out", (B, NT, P, E), f32, kind="ExternalOutput").ap()
    program(nc, A, out)
    r = run_bass_kernel_spmd(nc, [arrays], core_ids=[0])
    return r.results[0]["out"].reshape(B, S, E)
```

```python
import numpy as np
import concourse.bass as bass
from concourse import mybir

f32 = mybir.dt.float32
f32r = mybir.dt.float32r
bf16 = mybir.dt.bfloat16
ALU = mybir.AluOpType
ACT = mybir.ActivationFunctionType
AX = mybir.AxisListType

P = 128
B, S, E, H = 2, 512, 512, 32
D = E // H
NT = S // P
KC = E // P
FC = 11
GROUPS = 8
PAIRS = 16
EPS = 1e-5
MASK_L, MASK_R = 163.0, 408.0

DEPTH, C1, F1 = 4, 64, 256
OCT, H8 = 8, 170
HID1 = OCT * H8


def oct_signs():
    s = np.zeros((8, 8, 8), np.float32)
    s[0, 0, 0] = 1.0
    for i in range(1, 8):
        s[0, i, i] = s[i, 0, i] = 1.0
        s[i, i, 0] = -1.0
    for a, b, c in [(1, 2, 3), (1, 4, 5), (1, 7, 6), (2, 4, 6), (2, 5, 7), (3, 4, 7), (3, 6, 5)]:
        for x, y, z in ((a, b, c), (b, c, a), (c, a, b)):
            s[x, y, z], s[y, x, z] = 1.0, -1.0
    return np.array([[s[i ^ k, i, k] for k in range(8)] for i in range(8)], np.float32)


S_BANKS = [[(0, 3, 0)], [(0, 2, 0), (0, 0, 384)], [(0, 1, 0), (1, 1, 256)], [(1, 3, 0)], [(1, 2, 0), (1, 0, 384)]]
T_BANKS = [[(0, 0, 0), (0, 0, 1), (0, 0, 2), (0, 0, 3)], [(0, 1, 1), (0, 1, 2), (0, 1, 3), (0, 3, 3)],
           [(0, 2, 2), (0, 2, 3), (1, 2, 2), (1, 2, 3)],
           [(1, 0, 0), (1, 0, 1), (1, 0, 2), (1, 0, 3)], [(1, 1, 1), (1, 1, 2), (1, 1, 3), (1, 3, 3)]]
T_BY_ACT = (0, 2, 3)
SLOTS = 5 * PAIRS + FC + 1
HEAD_UNITS = 2
TRIPLES = 2 * FC * KC


LAST_DOWN = 5 * PAIRS + FC
NORM_STATS, NORM_ROWS, NORM_TURN = 5 * PAIRS + 3, 5 * PAIRS + 5, 5 * PAIRS + 7


def p_off(qt):
    return P * qt * (qt + 1) // 2


def t_col(hh, kt):
    if kt == 2:
        return 2 * 512 + 256 * hh
    return (3 * hh + (kt > 0)) * 512 + (384 if kt == 3 else 0)


def triple_slot(k):
    return max(-1, (k - HEAD_UNITS * KC) * 5 * PAIRS // (TRIPLES - HEAD_UNITS * KC))


def triples_in(s):
    return [k for k in range(TRIPLES) if triple_slot(k) == s]


def ffn_units_after(s):
    return [k // KC for k in triples_in(s - 1) if k % KC == KC - 1 and k >= HEAD_UNITS * KC]


def down_in(s):
    f = s - (5 * PAIRS + 1)
    return f if 0 <= f < FC else None


def score_in(s):
    return (s // 5, s % 5) if s < 5 * PAIRS else None


def turn_in(s):
    j = s // 5 - 1
    return (j, s % 5) if 0 <= j < PAIRS else None


def stack_in(s):
    j, i = s // 5, s % 5
    return (j // 2 + 1, i) if j % 2 == 1 and i < 4 and j // 2 + 1 < GROUPS else None


def pv_in(s):
    j, i = s // 5, s % 5
    return ((j - 3) // 2, i) if j % 2 == 1 and 3 <= j <= 2 * GROUPS + 1 else None


def ctx_in(s):
    j, i = s // 5, s % 5
    g = (j - 4) // 2
    return g if j % 2 == 0 and j >= 4 and i == (1 if g < GROUPS - 1 else 0) and g < GROUPS else None


def turn_order():
    at = {}
    for i in range(4):
        at["stack", 0, i] = len(at)
    for s in range(SLOTS):
        if ctx_in(s) is not None:
            at["ctx", ctx_in(s)] = len(at)
        if stack_in(s):
            at["stack", *stack_in(s)] = len(at)
        if turn_in(s):
            at["p", *turn_in(s)] = len(at)
        if s == NORM_TURN:
            for kc in range(KC):
                at["xn", kc] = len(at)
        if s == LAST_DOWN:
            for kc in range(KC):
                at["ctxf", kc] = len(at)
    return at


TURN = turn_order()
TURNS = len(TURN)
assert TURNS % 2 == 0

U_QKV, U_FFN, U_DOWN, U_OUT = 0, 12, 12 + 2 * FC, 12 + 3 * FC
UNITS = U_OUT + KC
HI_BY_ACT = U_FFN + 4
ROPE_SPLITS = [[], [9], [10], [11], [12], [13], [14], []]
RAW, SPLIT = 4, 5


W_GATE, W_UP, W_DOWN = range(3)
FLAT = OCT * H8 * C1 // P
HCOLS = FC * P
SIGN = oct_signs()
LAYER = [("centre", 1), ("var", 3), ("rsT", 1), ("spread", 8), ("centre", 1), ("var", 3), ("rsT", 1), ("spread", 2),
         ("mlp", 1), ("mlp", 3), ("mlpout", 1)]
PRE, FIRST = 2, [("norm", 4), ("rows", 8), ("turn", 4)]


def items1():
    out = []
    for b in range(B):
        out += [("hid", b, f, m, half) for f in range(FC) for m in range(2) for half in range(2)]
        out += [("down", b, pr, f) for pr in range(2) for f in range(FC)]
    return out


def steps1():
    items = items1()
    seq, n = [], 0

    def take(k):
        nonlocal n
        for _ in range(k):
            if n < len(items):
                seq.append(("item", n, items[n]))
                n += 1

    take(PRE)
    for name, k in FIRST:
        seq.append((name,))
        take(k)
    seq.append(("proj",))
    take(1)
    for q in range(2 * DEPTH + 1):
        for name, k in (LAYER[0:4] if q % 2 == 0 else LAYER[4:]):
            if name == "mlp":
                fc = 0 if seq_count(seq, "mlp", q) == 0 else 1
                seq.append(("mlp", q, fc))
            else:
                seq.append((name, q))
            take(k)
    take(len(items))
    return seq


def seq_count(seq, name, q):
    return sum(1 for x in seq if x[0] == name and x[1] == q)


STEPS1 = steps1()
LAST_BY_POOL = (1, 3, 6)
ADD_BIAS = {("hid", 1, 2 * i + 2, 1, 1): i for i in range(NT)}
DOWN_HI = [min(5 * PAIRS - 3 + n, LAST_DOWN) for n in range(FC + KC)]
CONV_FIRST = 1
AHEAD, HS = 4, 4
TD_PART = 6


def down_number(b, pr, f):
    return FC * (2 * b + pr) + f


def program(nc, A, out):
    at = [0]

    def sb(name, shape, dt, offset=None):
        size = int(np.prod(shape[1:])) * (2 if dt == bf16 else 4)
        if offset is None:
            offset = at[0]
            at[0] += (size + 31) // 32 * 32
        return nc.alloc_sbuf_tensor_at(name, shape, dt, offset=BASE + offset)

    BASE = (nc.sbuf_base + 31) // 32 * 32

    ident = sb("ident", [P, P], f32)
    maskL = sb("maskL", [P, P], bf16)
    maskR = sb("maskR", [P, P], bf16)
    rope = sb("rope", [P, 4, NT, D], f32)
    centre_m = sb("centre_m", [P, P], f32)
    seq_mean = sb("seq_mean", [P, B], f32)
    o_bias = at[0]
    qkv_bias = sb("qkv_bias", [P, 2 * E], f32)
    at[0] += E * 4
    out_bias = sb("out_bias", [P, E], f32)
    v_bias = sb("v_bias", [P, KC], f32)
    half = sb("half", [P, 8], f32)
    vec = sb("vec", [P, NVEC], f32)
    b1v = sb("b1v", [P, 2 * DEPTH], f32)
    hb1v = sb("hb1v", [P, 2 * DEPTH], f32)
    hln = sb("hln", [P, 8], f32)
    hscl = sb("hscl", [P, 4], f32)
    init = sb("init", [P, 2, 4], f32)
    polar_v = sb("polar_v", [P, 10, 4], f32)
    decay = sb("decay", [P, 4], f32)
    abs_sums = sb("abs_sums", [P, 3], f32)
    theta = sb("theta", [P, 2, 3], f32)
    scales = sb("scales", [P, 4], f32)
    X = sb("X", [P, NT, E], f32)
    o_xn = at[0]
    xn_hi = sb("xn_hi", [P, KC, S], f32r)
    xn_lo = sb("xn_lo", [P, KC, S], f32r)
    o_qk = at[0]
    qk_rows = [sb(f"qk_rows{t}", [P, GROUPS, NT, 64], f32) for t in range(2)]
    stack_rows = [sb(f"stack_rows{t}", [P, 16, 64], f32r) for t in range(2)]
    V = sb("V", [P, NT, H * 32], f32)
    ctx_rows = sb("ctx_rows", [P, NT, E], f32)
    o_stack = at[0]
    q_stack = [sb(f"q_stack{n}", [P, 2, S], f32r) for n in range(2)]
    k_stack = [sb(f"k_stack{n}", [P, 2, S], f32r) for n in range(2)]
    o_p = at[0]
    probs = [sb(f"probs{n}", [P, 2, 1280], f32) for n in range(2)]
    o_pt = at[0]
    probs_T = [sb(f"probs_T{n}", [P, 2560], f32) for n in range(3)]
    o_h = at[0]
    hidden_T = sb("hidden_T", [P, FC, S], f32)
    o_work = at[0]
    ctx_sums = sb("ctx_sums", [P, 512], f32)
    raw = [sb(f"raw{n}", [P, 512], f32) for n in range(RAW)]
    w_hi = [sb(f"w_hi{n}", [P, 512], f32r) for n in range(SPLIT)]
    w_lo = [sb(f"w_lo{n}", [P, 512], f32r) for n in range(SPLIT)]
    gate_tanh = sb("gate_tanh", [P, 512], f32)
    gate_silu = sb("gate_silu", [P, 512], f32)
    at[0] += 2048
    row_min = sb("row_min", [P, 2, 8], f32)
    stat = sb("stat", [P, NT, 6], f32)
    mean_var = sb("mean_var", [P, NT, 2], f32)
    var_eps0 = sb("var_eps0", [P, NT], f32)
    rstd = sb("rstd", [P, NT], f32)
    rinv = sb("rinv", [P, 16], f32)
    assert BASE + at[0] <= nc.sbuf_usable_end, at[0]
    xn_first = sb("xn_first", [P, NT, E], f32, offset=o_h)
    xn_later = [sb(f"xn_later{b}", [P, NT, E], f32, offset=o_pt + 10240 * ((PAIRS * (b + 1) - 3) % 3)) for b in range(B)]
    x_next = sb("x_next", [P, NT, E], f32, offset=o_stack + 8192)
    qk_biased = [sb(f"qk_biased{n}", [P, E], f32, offset=o_h + 8192 + 2048 * n) for n in range(2)]
    by_cos = [sb(f"by_cos{n}", [P, E], f32, offset=o_h + 12288 + 2048 * n) for n in range(2)]
    down_tanh = [sb(f"down_tanh{n}", [P, E], f32, offset=o_h + 2048 * n) for n in range(NT)]
    gate4 = [sb(f"gate4{n}", [P, E], f32, offset=o_stack + 2048 * n) for n in range(NT)]
    by_sin = sb("by_sin", [P, E], f32, offset=o_h + 16384)
    hsh = [sb(f"hsh{n}", [P, S], f32r, offset=o_stack + 4096 * n) for n in range(2)]
    hsl = [sb(f"hsl{n}", [P, S], f32r, offset=o_stack + 4096 * n + 2048) for n in range(2)]
    ctx_hi = sb("ctx_hi", [P, KC, S], f32r, offset=o_p)
    ctx_lo = sb("ctx_lo", [P, KC, S], f32r, offset=o_p + 8192)

    tern_w = [sb(f"tern_w{w}", [P, FLAT], f32, offset=o_p + 2720 * w) for w in range(3)]
    tern_over = [sb(f"tern_over{w}", [P, FLAT], f32, offset=o_p + 2720 * (3 + w)) for w in range(3)]
    tern_pos = [sb(f"tern_pos{w}", [P, FLAT], f32r, offset=o_p + 2720 * (9 + w)) for w in range(3)]
    tern_neg = [sb(f"tern_neg{w}", [P, FLAT], f32r, offset=o_p + 2720 * (12 + w)) for w in range(3)]
    gate_w1 = sb("gate_w1", [P, KC, HCOLS], f32r, offset=o_qk)
    up_w1 = sb("up_w1", [P, KC, HCOLS], f32r, offset=o_qk + 22528)
    down_w1 = sb("down_w1", [P, FC, E], f32r, offset=o_h)
    hidden1_T = sb("hidden1_T", [P, FC, S], f32, offset=o_pt)
    w1T = sb("w1T", [P, DEPTH, F1], f32, offset=o_pt + 22528)
    biased = sb("biased", [P, E], f32, offset=o_pt + 28672)
    w2T = sb("w2T", [P, DEPTH, 2, C1], f32, offset=o_pt + 22528 + 4096)
    x2_first = sb("x2_first", [P, NT, E], f32, offset=o_stack)
    rotation = [sb(f"rotation{n}", [P, 2, S], f32, offset=o_stack + 8192 + 4096 * n) for n in range(2)]
    xm_hi = sb("xm_hi", [P, KC, S], f32r, offset=o_p)
    xm_lo = sb("xm_lo", [P, KC, S], f32r, offset=o_p + 8192)
    tab_a = sb("tab_a", [P, 2, 256], f32, offset=o_p + 16384)
    tab_b = sb("tab_b", [P, 2, 256], f32, offset=o_p + 16384 + 2048)
    woT = sb("woT", [P, E], f32, offset=o_bias)
    bout = sb("bout", [P, E], f32, offset=o_bias + 2048)
    sel = sb("sel", [8, NT, P], f32, offset=o_bias + 4096)
    gate1 = [sb(f"gate1{b}", [P, NT, E], f32, offset=(o_xn, o_p)[b]) for b in range(B)]
    wk = [sb(f"wk{n}", [P, S], f32, offset=o_work + 2048 * n) for n in range(12)]
    t1 = [sb(f"t1_{n}", [P, S], f32, offset=(o_work + 24576, o_qk + 45056)[n]) for n in range(2)]
    ab1 = [sb(f"ab1_{n}", [P, S], f32, offset=(o_bias + 6144, o_qk + 47104)[n]) for n in range(2)]
    xn_last = sb("xn_last", [P, NT, E], f32, offset=o_work)
    h_rows, h_with_b2, squares, centred, unit_rows, in_tanh, in_affine, act_rows, re_rows, im_rows, re_state, im_state = wk
    hsH = [sb(f"hsH{n}", [P, 2 * P], f32r, offset=o_work + 26624 + 2048 * n) for n in range(HS)]
    hsL = [sb(f"hsL{n}", [P, 2 * P], f32r, offset=o_work + 26624 + 2048 * n + 1024) for n in range(HS)]
    var_eps = sb("var_eps", [P, 8], f32, offset=o_work + 34816)
    inv_std = sb("inv_std", [P, 8], f32, offset=o_work + 34816 + 32)
    inv_std_T = sb("inv_std_T", [8, P], f32, offset=o_work + 34816 + 64)
    winR = sb("winR", [P, KC, 192], f32, offset=o_work + 12288)
    winH = sb("winH", [P, KC, 192], f32r, offset=o_work + 12288 + 3072)
    winL = sb("winL", [P, KC, 192], f32r, offset=o_work + 12288 + 6144)
    XN1 = [(xn_hi, xn_lo), (xm_hi, xm_lo)]
    X2 = [x2_first, X]
    NORM = [(X, xn_first, XN1[0]), (x_next, xn_later[0], XN1[0]), (x_next, xn_later[1], XN1[0]), (X, xn_last, XN1[1])]

    def bank(name):
        return nc.alloc_psum_tensor(name, [P, 512], f32)

    score_ps = [bank(f"score_ps{n}") for n in range(3)]
    turn_ps = [bank(f"turn_ps{n}") for n in range(2)]
    ctx_ps = bank("ctx_ps")
    proj_ps = [bank(f"proj_ps{n}") for n in range(2)]
    down_ps = [score_ps[0], score_ps[1], score_ps[2], proj_ps[0]]
    QKV_BANKS = [[proj_ps[0], score_ps[0], score_ps[1], score_ps[2]], [proj_ps[1], ctx_ps, turn_ps[0], turn_ps[1]]]
    out_ps = [proj_ps[1], ctx_ps, turn_ps[0], turn_ps[1]]
    OUT_TILES = (3, 0, 1, 2)
    hid1_ps = [proj_ps[0], proj_ps[1], score_ps[2], ctx_ps]
    down1_ps = [[score_ps[2], ctx_ps], [proj_ps[0], proj_ps[1]]]
    last_s = [t1[0], t1[1], biased]
    LAST_BANKS = [score_ps[0], score_ps[1], turn_ps[0], turn_ps[1], score_ps[2], ctx_ps, proj_ps[0], proj_ps[1]]
    mlp_tanh, mlp_biased = [in_tanh, in_affine], [unit_rows, centred]
    mlp_silu = [re_state, im_state, re_rows, im_rows]

    def sem(name):
        return nc.alloc_semaphore(name)

    const_in = sem("const_in")
    x_in = [sem(f"x_in{t}") for t in range(NT)]
    ident_in = sem("ident_in")
    qkv_used = sem("qkv_used")
    gate4_ready = sem("gate4_ready")
    bias_step = sem("bias_step")
    mask_ready = sem("mask_ready")
    x2_stored = sem("x2_stored")
    raw_in = [sem(f"raw_in{n}") for n in range(RAW)]
    hi_done = sem("hi_done")
    unit_ready = sem("unit_ready")
    down_used = sem("down_used")
    ones_set = sem("ones_set")
    stats = sem("stats")
    mv_ready = sem("mv_ready")
    eps_added = sem("eps_added")
    rstd_ready = sem("rstd_ready")
    xn_ready = sem("xn_ready")
    turned = sem("turned")
    turn_free = [sem(f"turn_free{n}") for n in range(2)]
    xh_ready = sem("xh_ready")
    proj_done = sem("proj_done")
    proj_free = sem("proj_free")
    r1_ready = sem("r1_ready")
    r2_ready = sem("r2_ready")
    qk_ready = sem("qk_ready")
    ts_hi = sem("ts_hi")
    ts_ready = sem("ts_ready")
    score_half = sem("score_half")
    score_done = sem("score_done")
    min_ready = sem("min_ready")
    probs_ready = sem("probs_ready")
    pv_done = sem("pv_done")
    ctx_copied = sem("ctx_copied")
    rinv_ready = sem("rinv_ready")
    tanh_ready = sem("tanh_ready")
    hs_hi = sem("hs_hi")
    hs_ready = sem("hs_ready")
    ct_hi = sem("ct_hi")
    out_done = sem("out_done")
    down_tanh_ready = sem("down_tanh_ready")
    combined = sem("combined")
    out_stored = sem("out_stored")
    wc_in = sem("wc_in")
    asum_ready = sem("asum_ready")
    tot_ready = sem("tot_ready")
    theta_ready = sem("theta_ready")
    tern_a = sem("tern_a")
    wp_ready = sem("wp_ready")
    tern_ready = sem("tern_ready")
    tern_stored = sem("tern_stored")
    small_in = sem("small_in")
    small1_in = sem("small1_in")
    x20_in = sem("x20_in")
    xb_in = sem("xb_in")
    arranged = sem("arranged")
    out_used = sem("out_used")
    win_in = sem("win_in")
    win_hi = sem("win_hi")
    win_ready = sem("win_ready")
    tg_in = sem("tg_in")
    tu_in = sem("tu_in")
    td_in = [sem(f"td_in{n}") for n in range(2)]
    vecs_ready = sem("vecs_ready")
    ph_step = sem("ph_step")
    polar_ready = sem("polar_ready")
    decay_ready = sem("decay_ready")
    tab_step = sem("tab_step")
    input_proj_done = sem("input_proj_done")
    h_ready = sem("h_ready")
    ctr_ready = sem("ctr_ready")
    sq_ready = sem("sq_ready")
    centred_ready = sem("centred_ready")
    var_ready = sem("var_ready")
    ve_ready = sem("ve_ready")
    rs_ready = sem("rs_ready")
    rst_ready = sem("rst_ready")
    rt_ready = sem("rt_ready")
    spread_done = sem("spread_done")
    y_ready = sem("y_ready")
    tz_ready = sem("tz_ready")
    conv_step = sem("conv_step")
    im_ready = sem("im_ready")
    im_state_ready = sem("im_state_ready")
    v_written = sem("v_written")
    yn_ready = sem("yn_ready")
    mlp_ready = sem("mlp_ready")
    mt_ready = sem("mt_ready")
    mz_ready = sem("mz_ready")
    mu_ready = sem("mu_ready")
    o1_ready = sem("o1_ready")
    hb_ready = sem("hb_ready")
    hid1_done = sem("hid1_done")
    hid1_free = sem("hid1_free")
    t1_ready = sem("t1_ready")
    hs1_hi = sem("hs1_hi")
    hs1_ready = sem("hs1_ready")
    down1_used = sem("down1_used")
    down1_tanh = sem("down1_tanh")
    gate1_ready = sem("gate1_ready")
    s1_ready = sem("s1_ready")
    last_proj_done = sem("last_proj_done")
    fin = sem("fin")
    fin_pool = sem("fin_pool")
    s1_scaled = sem("s1_scaled")
    pool_gated = sem("pool_gated")
    pre_ready = sem("pre_ready")
    bias1 = sem("bias1")
    scale_ready = sem("scale_ready")

    x_dram, w_dram, outb_d = A["x"], A["w0"], A["out_b"]
    x2_d = nc.dram_tensor("x2_scratch", (B, NT, P, E), f32, kind="Internal").ap()

    tern_d = [nc.dram_tensor(f"tern{w}", (2, P * FLAT), f32, kind="Internal").ap() for w in range(3)]

    arr_d = [nc.dram_tensor(f"arranged{w}", shape, f32, kind="Internal").ap() for w, shape in
             enumerate(((E, HCOLS), (E, HCOLS), (HCOLS, E)))]

    def block_of(w, i, k, rows, width):
        return (0 if SIGN[i, k] > 0 else P * FLAT) + (i ^ k) * rows * width

    def arrangement():
        out = []
        for w in (W_GATE, W_UP, W_DOWN):
            rows, width = (C1, H8) if w != W_DOWN else (H8, C1)
            pitch = OCT * width if w == W_DOWN else HCOLS
            for i in range(OCT):
                for k in range(0, OCT, 2):
                    o0, o1 = (block_of(w, i, k + x, rows, width) for x in range(2))
                    src = bass.AP(tensor=tern_d[w].tensor, offset=o0, ap=[[width, rows], [o1 - o0, 2], [1, width]])
                    dst = bass.AP(tensor=arr_d[w].tensor, offset=i * rows * pitch + k * width,
                                  ap=[[pitch, rows], [width, 2], [1, width]])
                    out.append((dst, src))
            if w == W_DOWN:
                out.append((arr_d[w][HID1:, :], A["zeros"].rearrange("(p n) -> p n", n=E)))
            else:
                out.append((arr_d[w][:, HID1:], A["zeros"].rearrange("(p n) -> p n", p=E)))
        return out

    ARRANGE = arrangement()

    def wide(ap, n):
        return ap.unsqueeze(1).broadcast_to([P, n, ap.shape[-1]])

    def F32(t):
        return t.bitcast(f32)

    FU, FV = 12 + 2 * FC, 8 + 2 * FC

    def unit_free(n):
        b, u = divmod(n, UNITS)
        if u < U_FFN:
            return (qkv_used, 3 * (3 * b + u // KC) + u % KC + 1) if u % KC < KC - 1 else (proj_done, FU * b + u + 1)
        if u < U_DOWN:
            return proj_done, FU * b + 12 + u - U_FFN + 1
        if u < U_OUT:
            return down_used, FC * b + u - U_DOWN + 1
        return out_used, KC * b + u - U_OUT + 1

    def hi_by_act(n):
        u = n % UNITS
        return u < HI_BY_ACT or u >= U_DOWN

    def copied(b, key):
        n = use(b, key)
        return turn_free[n % 2], n // 2 + 1

    def stacked(t, g):
        src = qk_rows[t][:, g, :, :].rearrange("p t (h d) -> p (t h) d", d=D).unsqueeze(2).broadcast_to([P, 16, 2, D])
        dst = stack_rows[t][:, :, :].rearrange("p n (a c d) -> p n a c d", a=2, c=2)
        return (src, dst[:, :, :, 0, :], dst[:, :, :, 1, :]) if t == 0 else (src, dst[:, :, 0, :, :], dst[:, :, 1, :, :])

    def norm_use(k, kc):
        return kc if k == 0 else use(k - 1, ("xn", kc)) if k <= B else KC + TURNS * B + kc

    def use(b, key):
        return KC + TURNS * b + TURN[key]

    def hidden(b, w):
        return proj_free, FV * b + 8 + w + 1

    with nc.Block() as block:

        @block.sync
        def _(sp):
            for t in range(NT):
                sp.dma_start(X[:, t, :], x_dram[0, t]).then_inc(x_in[t], 16)
                if t == 0:
                    sp.dma_start(ident[:, :], A["ident"]).then_inc(ident_in, 16)
            copies = list(ARRANGE)
            for b in range(B):
                for u in range(UNITS):
                    n = b * UNITS + u
                    if n >= RAW:
                        sp.wait_ge(unit_ready, n - RAW + 1)
                    sp.dma_start(raw[n % RAW][:, :], w_dram[u]).then_inc(raw_in[n % RAW], 16)
                    if b == 0 and u == RAW - 1:
                        sp.dma_start(qkv_bias[:, :], A["qk_bias"].partition_broadcast(P)).then_inc(const_in, 16)
                        for dst, src in ((rope[:, :, :, :], A["rope"]), (gate_tanh[:, 0:2 * P], A["mask"]), (v_bias[:, :], A["v_bias"]),
                                         (out_bias[:, :], outb_d.partition_broadcast(P))):
                            sp.dma_start(dst, src).then_inc(const_in, 16)
                        for w in range(3):
                            sp.dma_start(tern_w[w][:, :], A["tern_w"][w]).then_inc(wc_in, 16)
                        for dst, src in ((centre_m[:, :], A["centre"]), (seq_mean[:, :], A["seq_mean"]), (vec[:, :], A["vec"]),
                                         (b1v[:, :], A["b1v"])):
                            sp.dma_start(dst, src).then_inc(small_in, 16)
                    if b == 0 and U_FFN + 5 <= u < U_DOWN:
                        if u == U_FFN + 5:
                            sp.wait_ge(tern_stored, 96)
                        for _ in range(6):
                            if copies:
                                sp.dma_start(*copies.pop(0)).then_inc(arranged, 16)
                    if b == 1 and u == 8:
                        sp.wait_ge(combined, 2 * NT)
                        sp.dma_start(x2_d[0].rearrange("t p e -> p t e"), X[:, :, :]).then_inc(x2_stored, 16)
                    if b == 1 and u == U_FFN:
                        sp.wait_ge(x2_stored, 16)
                        for t in range(NT):
                            sp.dma_start(X[:, t, :], x_dram[1, t]).then_inc(x_in[t], 16)
            assert not copies
            sp.wait_ge(arranged, 16 * len(ARRANGE))
            sp.wait_ge(out_used, KC * B)
            sp.dma_start(winR[:, :, :], A["win"]).then_inc(win_in, 16)
            sp.wait_ge(combined, 2 * NT * B)
            sp.dma_start(x2_first[:, :, :], x2_d[0].rearrange("t p e -> p t e")).then_inc(x20_in, 16)
            down_rows = arr_d[W_DOWN].rearrange("(c p) e -> p c e", p=P)
            sp.dma_start(F32(down_w1[:, :TD_PART, :]), down_rows[:, :TD_PART, :]).then_inc(td_in[0], 16)
            sp.dma_start(F32(down_w1[:, TD_PART:, :]), down_rows[:, TD_PART:, :]).then_inc(td_in[1], 16)
            for t in range(B * NT):
                b, i = divmod(t, NT)
                sp.wait_ge(*((fin_pool, LAST_BY_POOL.index(t) + 1) if t in LAST_BY_POOL else
                             (fin, t + 1 - sum(1 for x in LAST_BY_POOL if x < t))))
                sp.dma_start(out[b, i], X2[b][:, i, :]).then_inc(out_stored, 16)
            sp.wait_ge(out_stored, 16 * B * NT)

        @block.gpsimd
        def _(pool):
            nc.gpsimd.memset(half[:, :], -0.5).then_inc(ones_set, 1)
            nc.gpsimd.memset(V[:, :, :], 1.0).then_inc(ones_set, 1)

            def split(n):
                if not hi_by_act(n):
                    pool.wait_ge(raw_in[n % RAW], 16 * (n // RAW + 1))
                    if n >= SPLIT:
                        pool.wait_ge(*unit_free(n - SPLIT))
                    nc.gpsimd.tensor_scalar(w_hi[n % SPLIT][:, :], raw[n % RAW][:, :], 1.0, 0.0, ALU.mult, ALU.add).then_inc(hi_done, 1)
                pool.wait_ge(hi_done, n + 1)
                nc.gpsimd.tensor_tensor(w_lo[n % SPLIT][:, :], raw[n % RAW][:, :], F32(w_hi[n % SPLIT][:, :]),
                                        ALU.subtract).then_inc(unit_ready, 1)

            def rope_cos(b, t, i):
                r = 8 * b + 4 * t + i
                pool.wait_ge(proj_free, FV * b + 4 * t + i + 1)
                if r >= 2:
                    pool.wait_ge(qk_ready, r - 1)
                if r == 0:
                    pool.wait_ge(const_in, 80)
                nc.gpsimd.tensor_tensor(by_cos[r % 2][:, :].rearrange("p (h d) -> p h d", d=D),
                                        qk_biased[r % 2][:, :].rearrange("p (h d) -> p h d", d=D),
                                        wide(rope[:, 2 * t, i, :], H), ALU.mult).then_inc(r1_ready, 1)

            def stack(b, g):
                for t in range(2):
                    n = 2 * (GROUPS * b + g) + t
                    if n >= 2:
                        b0, g0 = divmod(GROUPS * b + g - 1, GROUPS)
                        pool.wait_ge(turned, use(b0, ("stack", g0, 2 * t + 1)) + 1)
                    src, hi, lo = stacked(t, g)
                    if g:
                        nc.gpsimd.tensor_scalar(hi, src, 1.0, 0.0, ALU.mult, ALU.add).then_inc(ts_hi, 1)
                    pool.wait_ge(ts_hi, n + 1)
                    nc.gpsimd.tensor_tensor(lo, src, F32(hi), ALU.subtract).then_inc(ts_ready, 1)

            def polar():
                mult, add, sub = ALU.mult, ALU.add, ALU.subtract
                pool.wait_ge(small_in, 64)
                re, im = vec[:, V_RE:V_RE + 4], vec[:, V_IM:V_IM + 4]
                steps = [0]

                def step(ins):
                    steps[0] += 1
                    ins.then_inc(ph_step, 1)
                    pool.wait_ge(ph_step, steps[0])

                t = [polar_v[:, n, :] for n in range(10)]
                step(nc.gpsimd.tensor_tensor(t[0], re, re, mult))
                step(nc.gpsimd.tensor_tensor(t[1], im, im, mult))
                step(nc.gpsimd.tensor_tensor(t[0], t[0], t[1], add))
                step(nc.gpsimd.tensor_scalar(t[1], t[0], 1e-37, 1e38, ALU.max, ALU.min))
                step(nc.gpsimd.tensor_tensor(t[2], t[1], half[:, 0:4], ALU.pow))
                step(nc.gpsimd.tensor_tensor(t[3], t[1], t[2], mult))
                step(nc.gpsimd.tensor_tensor(t[3], t[3], t[2], mult))
                step(nc.gpsimd.tensor_scalar(t[3], t[3], -0.5, 1.5, mult, add))
                step(nc.gpsimd.tensor_tensor(t[2], t[2], t[3], mult))
                step(nc.gpsimd.tensor_tensor(t[7], t[0], t[2], mult))
                step(nc.gpsimd.tensor_scalar(t[8], t[0], 1e-37, 1.0, ALU.is_lt, mult))
                step(nc.gpsimd.tensor_scalar(t[9], t[8], -1.0, 1.0, mult, add))
                step(nc.gpsimd.tensor_tensor(t[2], t[2], t[9], mult))
                step(nc.gpsimd.tensor_tensor(t[4], re, t[2], mult))
                step(nc.gpsimd.tensor_tensor(t[4], t[4], t[8], add))
                nc.gpsimd.tensor_tensor(t[5], im, t[2], mult).then_inc(polar_ready, 1)
                pool.wait_ge(polar_ready, 1)

            def norm_rstd(k):
                pool.wait_ge(mv_ready, NT * (k + 1))
                nc.gpsimd.tensor_scalar(var_eps0[:, :], mean_var[:, :, 1], EPS, 1.0, ALU.add, ALU.mult).then_inc(eps_added, 1)
                pool.wait_ge(eps_added, k + 1)
                nc.gpsimd.tensor_tensor(rstd[:, :], var_eps0[:, :], half[:, 0:NT], ALU.pow).then_inc(rstd_ready, 1)

            pool.wait_ge(ones_set, 2)
            norm_rstd(0)
            for b in range(B):
                u0 = UNITS * b
                for n in range(0, 9):
                    split(u0 + n)
                for t in range(2):
                    for i in range(NT):
                        rope_cos(b, t, i)
                        for n in ROPE_SPLITS[4 * t + i]:
                            split(u0 + n)
                pool.wait_ge(qk_ready, 8 * (b + 1))
                stack(b, 0)
                done = U_FFN + HEAD_UNITS + 1
                for j in range(PAIRS):
                    upto = min(U_DOWN, U_FFN + HEAD_UNITS + (5 * (j + 1) + KC - 1) // KC + 1)
                    for n in range(done, upto):
                        split(u0 + n)
                    done = max(done, upto)
                    if j % 2 == 0 and j // 2 + 1 < GROUPS:
                        stack(b, j // 2 + 1)
                for n in range(done, UNITS):
                    if n == U_DOWN + 8:
                        norm_rstd(b + 1)
                    split(u0 + n)
                if b == 0:
                    polar()
            mult, add, sub = ALU.mult, ALU.add, ALU.subtract
            def table_start(l):
                if l >= 2:
                    pool.wait_ge(h_ready, 1 + 2 * (l - 2) + 1)
                nc.gpsimd.tensor_scalar(rotation[l % 2][:, :, 0], polar_v[:, 4:6, l], 1.0, 0.0, mult, add).then_inc(tab_step, 1)

            def table_double(l, e):
                m, T = 1 << e, rotation[l % 2]
                base = l * (1 + 4 * 9) + 1 + 4 * e
                pool.wait_ge(tab_step, base)
                nc.gpsimd.tensor_scalar(tab_a[:, :, 0:m], T[:, :, 0:m], T[:, 0, m - 1:m], 1.0, mult, mult).then_inc(tab_step, 1)
                nc.gpsimd.tensor_scalar(tab_b[:, :, 0:m], T[:, :, 0:m], T[:, 1, m - 1:m], 1.0, mult, mult).then_inc(tab_step, 1)
                pool.wait_ge(tab_step, base + 2)
                nc.gpsimd.tensor_tensor(T[:, 0, m:2 * m], tab_a[:, 0, 0:m], tab_b[:, 1, 0:m], sub).then_inc(tab_step, 1)
                nc.gpsimd.tensor_tensor(T[:, 1, m:2 * m], tab_b[:, 0, 0:m], tab_a[:, 1, 0:m], add).then_inc(tab_step, 1)

            pool.wait_ge(turned, use(B - 1, ("p", PAIRS - 1, 4)) + 1)
            table_start(0)
            for e in range(9):
                table_double(0, e)
            pool.wait_ge(win_in, 16)
            nc.gpsimd.tensor_scalar(winH[:, :, :], winR[:, :, :], 1.0, 0.0, mult, add).then_inc(win_hi, 1)
            pool.wait_ge(win_hi, 1)
            nc.gpsimd.tensor_tensor(winL[:, :, :], winR[:, :, :], F32(winH[:, :, :]), sub).then_inc(win_ready, 1)
            def add_bias(t):
                b, i = divmod(t, NT)
                pool.wait_ge(gate1_ready, t + 1)
                if t == 0:
                    pool.wait_ge(x20_in, 16)
                if t:
                    pool.wait_ge(pre_ready, 3 * t)
                nc.gpsimd.tensor_scalar(biased[:, :], gate1[b][:, i, :], scales[:, 1:2], 1.0, mult, mult).then_inc(pre_ready, 1)
                pool.wait_ge(pre_ready, 3 * t + 1)
                nc.gpsimd.tensor_tensor(biased[:, :], biased[:, :], bout[:, :], mult).then_inc(pre_ready, 1)
                pool.wait_ge(pre_ready, 3 * t + 2)
                nc.gpsimd.tensor_tensor(X2[b][:, i, :], X2[b][:, i, :], biased[:, :], add).then_inc(pre_ready, 1)

            todo = []
            for x in range(1, 2):
                todo += [(x, -1)] + [(x, e) for e in range(9)]
            for n_step, step in enumerate(STEPS1):
                if step[0] == "item":
                    _, n, it = step
                    nxt = items1()[n + AHEAD] if n + AHEAD < len(items1()) else None
                    if nxt and nxt[0] == "down":
                        _, b, pr, f = nxt
                        d = down_number(b, pr, f)
                        pool.wait_ge(hs1_hi, d + 1)
                        nc.gpsimd.tensor_tensor(hsL[d % HS][:, :], hidden1_T[:, f, 256 * pr:256 * pr + 256], F32(hsH[d % HS][:, :]),
                                                sub).then_inc(hs1_ready, 1)
                    if it in ADD_BIAS:
                        add_bias(ADD_BIAS[it])
                    if todo:
                        l, e = todo.pop(0)
                        table_start(l) if e < 0 else table_double(l, e)
                elif step[0] == "norm":
                    norm_rstd(3)
                elif step[0] == "var":
                    q = step[1]
                    pool.wait_ge(ve_ready, q + 1)
                    nc.gpsimd.tensor_tensor(inv_std[:, :], var_eps[:, :], half[:, :], ALU.pow).then_inc(rs_ready, 1)
                elif step[0] == "spread" and step[1] % 2 == 0 and step[1] < 2 * DEPTH:
                    l = step[1] // 2
                    pool.wait_ge(tab_step, 37 * (l + 1))
                    pool.wait_ge(conv_step, CONV_FIRST + 6 * l + 2)
                    nc.gpsimd.tensor_tensor(im_rows[:, :], act_rows[:, :], rotation[l % 2][:, 1, :], mult).then_inc(im_ready, 1)
                    pool.wait_ge(im_state_ready, l + 1)
                    nc.gpsimd.tensor_tensor(im_rows[:, :], im_state[:, :], rotation[l % 2][:, 1, :], mult).then_inc(im_ready, 1)
                elif step[0] == "centre" and step[1] % 2 == 1 and step[1] // 2 + 2 < DEPTH:
                    l = step[1] // 2 + 2
                    todo += [(l, -1)] + [(l, e) for e in range(9)]

            for n, t in enumerate(LAST_BY_POOL):
                b, i = divmod(t, NT)
                pool.wait_ge(s1_scaled, n + 1)
                nc.gpsimd.tensor_tensor(last_s[n][:, :], last_s[n][:, :], gate1[b][:, i, :], mult).then_inc(pool_gated, 1)
                pool.wait_ge(pool_gated, n + 1)
                pool.wait_ge(*((bias1, 2 * NT) if b else (pre_ready, 3 * NT)))
                nc.gpsimd.tensor_tensor(X2[b][:, i, :], X2[b][:, i, :], last_s[n][:, :], add).then_inc(fin_pool, 1)

        @block.tensor
        def _(pe):
            def turn(b, key, blocks):
                n = use(b, key)
                if n >= 2:
                    pe.wait_ge(turn_free[n % 2], n // 2)
                for c, src in enumerate(blocks):
                    m = nc.tensor.transpose(turn_ps[n % 2][:, c * P:(c + 1) * P], src, ident[:, :])
                m.then_inc(turned, 1)

            def passes(acc, lh, ll, rh, rl, first, last):
                nc.tensor.matmul(acc, lh, rh, start=first, stop=False)
                nc.tensor.matmul(acc, ll, rh, start=False, stop=False)
                return nc.tensor.matmul(acc, lh, rl, start=False, stop=last)

            def unit(b, u):
                n = UNITS * b + u
                return w_hi[n % SPLIT], w_lo[n % SPLIT]

            def stack_turn(b, g, i):
                t, p = divmod(i, 2)
                pe.wait_ge(ts_ready, 2 * (GROUPS * b + g) + t + 1)
                turn(b, ("stack", g, i), [F32(stack_rows[t][:, 4 * c + 2 * p:4 * c + 2 * p + 2, :].rearrange("p n c -> p (n c)"))
                                          for c in range(NT)])

            def score(acc, q, k, j, hh, qt, c):
                rows, w = slice(64 * hh, 64 * hh + 64), P * (qt + 1)
                nc.tensor.matmul(acc[:, c:c + w], q[rows, j % 2, qt * P:(qt + 1) * P], k[rows, j % 2, 0:w], start=True, stop=False)
                return nc.tensor.matmul(acc[:, c + w - P:c + w], maskL[:, :], maskR[:, :], start=False, stop=True)

            pe.wait_ge(ident_in, 16)

            def norm_turn(k):
                pe.wait_ge(xn_ready, NT * (k + 1))
                for kc in range(KC):
                    n = norm_use(k, kc)
                    if n >= 2:
                        pe.wait_ge(turn_free[n % 2], n // 2)
                    for t in range(NT):
                        m = nc.tensor.transpose(turn_ps[n % 2][:, t * P:(t + 1) * P], NORM[k][1][:, t, kc * P:(kc + 1) * P], ident[:, :])
                    m.then_inc(turned, 1)

            def ffn_triple(b, triple):
                w, kc = divmod(triple, KC)
                if kc == 0:
                    pe.wait_ge(unit_ready, UNITS * b + U_FFN + w + 1)
                    pe.wait_ge(*((v_written, NT * b + 1) if w == 0 else (proj_free, FV * b + (5 if w == 1 else 8 + w - 1))))
                wh, wl = unit(b, U_FFN + w)
                c = slice(kc * P, (kc + 1) * P)
                m = passes(proj_ps[w % 2][:, :], wh[:, c], wl[:, c], xn_hi[:, kc, :], xn_lo[:, kc, :], kc == 0, kc == KC - 1)
                if kc == KC - 1:
                    m.then_inc(proj_done, 1)

            norm_turn(0)
            for b in range(B):
                f0 = FV * b
                for t in range(3):
                    for kc in range(KC):
                        pe.wait_ge(unit_ready, UNITS * b + U_QKV + 4 * t + kc + 1)
                        if t == 0:
                            n0 = norm_use(b, kc)
                            pe.wait_ge(turn_free[n0 % 2], n0 // 2 + 1)
                        wh, wl = unit(b, U_QKV + 4 * t + kc)
                        if b == 0 and t == 0 and kc == KC - 2:
                            pe.wait_ge(ones_set, 2)
                            pe.wait_ge(asum_ready, 3)
                            nc.tensor.matmul(ctx_ps[:, 0:3], V[:, 0, 0:P], abs_sums[:, :], start=True, stop=True).then_inc(tot_ready, 1)
                        for i in range(NT):
                            if kc == 0 and t == 0 and b:
                                pe.wait_ge(gate4_ready, NT * b)
                            elif kc == 0 and t == 1:
                                if b:
                                    pe.wait_ge(combined, 2 * NT * (b - 1) + NT)
                                elif i == 1:
                                    pe.wait_ge(theta_ready, 2)
                            elif kc == 0 and t == 2:
                                pe.wait_ge(proj_free, f0 + i + 1)
                            c = slice(i * P, (i + 1) * P)
                            m = passes(QKV_BANKS[t % 2][i][:, :], xn_hi[:, kc, c], xn_lo[:, kc, c], wh[:, :], wl[:, :], kc == 0, kc == KC - 1)
                            if kc == KC - 1:
                                m.then_inc(proj_done, 1)
                        if kc < KC - 1:
                            m.then_inc(qkv_used, 1)
                for triple in triples_in(-1):
                    ffn_triple(b, triple)
                pe.wait_ge(proj_free, f0 + 8)
                for i in range(4):
                    stack_turn(b, 0, i)
                for s in range(SLOTS):
                    if score_in(s):
                        j, i = score_in(s)
                        g, n = j // 2, 5 * PAIRS * b + s
                        if n == 0:
                            pe.wait_ge(mask_ready, 2)
                        if s == 0:
                            pe.wait_ge(v_written, NT * (b + 1))
                        if i == 0:
                            for x in range(4):
                                pe.wait_ge(*copied(b, ("stack", g, x)))
                        if n >= 3:
                            pe.wait_ge(probs_ready, n - 2)
                        q, k = q_stack[g % 2], k_stack[g % 2]
                        for hh, qt, c in S_BANKS[i][:1 if i == 2 else 2]:
                            m = score(score_ps[n % 3], q, k, j, hh, qt, c)
                        m.then_inc(score_half if i == 2 else score_done, 1)
                    if ctx_in(s) is not None:
                        g = ctx_in(s)
                        pe.wait_ge(ctx_copied, GROUPS * b + g + 1)
                        turn(b, ("ctx", g), [ctx_sums[:, t * P:(t + 1) * P] for t in range(NT)])
                    for triple in triples_in(s):
                        ffn_triple(b, triple)
                    if score_in(s) and s % 5 == 2:
                        pe.wait_ge(score_half, PAIRS * b + j + 1)
                        score(score_ps[n % 3], q, k, j, *S_BANKS[2][1]).then_inc(score_done, 1)
                    if stack_in(s):
                        stack_turn(b, *stack_in(s))
                    if s == LAST_DOWN:
                        for kc in range(2):
                            turn(b, ("ctxf", kc), [ctx_rows[:, t, kc * P:(kc + 1) * P] for t in range(NT)])
                    if down_in(s) is not None:
                        f = down_in(s)
                        pe.wait_ge(hs_ready, FC * b + f + 1)
                        pe.wait_ge(unit_ready, UNITS * b + U_DOWN + f + 1)
                        if f == 0:
                            pe.wait_ge(probs_ready, 5 * PAIRS * (b + 1))
                            pe.wait_ge(proj_free, f0 + FV)
                        wh, wl = unit(b, U_DOWN + f)
                        for t in range(NT):
                            c = slice(t * P, (t + 1) * P)
                            m = passes(down_ps[t][:, :], hsh[f % 2][:, c], hsl[f % 2][:, c], wh[:, :], wl[:, :], f == 0, f == FC - 1)
                        m.then_inc(down_used, 1)
                    if s == LAST_DOWN:
                        for kc in range(2, KC):
                            turn(b, ("ctxf", kc), [ctx_rows[:, t, kc * P:(kc + 1) * P] for t in range(NT)])
                    if turn_in(s):
                        j, i = turn_in(s)
                        pe.wait_ge(probs_ready, 5 * PAIRS * b + 5 * j + (3 if i < 2 else 5))
                        turn(b, ("p", j, i), [probs[j % 2][:, hh, p_off(qt) + kt * P:p_off(qt) + kt * P + P] for hh, kt, qt in T_BANKS[i]])
                    if pv_in(s) and pv_in(s)[1] < NT:
                        g, kt = pv_in(s)
                        gp = PAIRS * b + 2 * g
                        if kt == 0:
                            for x in range(5):
                                pe.wait_ge(*copied(b, ("p", 2 * g + 1, x)))
                            pe.wait_ge(v_written, NT * (b + 1))
                            if GROUPS * b + g:
                                pe.wait_ge(ctx_copied, GROUPS * b + g)
                        for h in range(4):
                            c = t_col(h % 2, kt)
                            m = nc.tensor.matmul(ctx_ps[32 * h:32 * h + 32, kt * P:S], V[:, kt, (4 * g + h) * 32:(4 * g + h + 1) * 32],
                                                 probs_T[(gp + h // 2) % 3][:, c:c + S - kt * P], start=kt == 0, stop=kt == NT - 1,
                                                 skip_group_check=True)
                        if kt == NT - 1:
                            m.then_inc(pv_done, 1)
                    if s == NORM_TURN:
                        norm_turn(b + 1)
                for kc in range(KC):
                    pe.wait_ge(*copied(b, ("ctxf", kc)))
                    pe.wait_ge(unit_ready, UNITS * b + U_OUT + kc + 1)
                    wh, wl = unit(b, U_OUT + kc)
                    for x, i in enumerate(OUT_TILES):
                        if kc == 0 and x == 2:
                            pe.wait_ge(*copied(b, ("ctxf", KC - 2)))
                            pe.wait_ge(*copied(b, ("ctxf", KC - 1)))
                        c = slice(i * P, (i + 1) * P)
                        m = passes(out_ps[x][:, :], ctx_hi[:, kc, c], ctx_lo[:, kc, c], wh[:, :], wl[:, :], kc == 0, kc == KC - 1)
                        if x == NT - 1:
                            m.then_inc(out_used, 1)
                        elif kc == KC - 1:
                            m.then_inc(out_done, 1)

            def hidden_item(n, b, f, mm, halfway):
                u = 2 * (FC * b + f) + mm
                if halfway == 0:
                    if b and f < 2:
                        pe.wait_ge(gate1_ready, NT * (b - 1) + 2 * f + mm + 1)
                    elif u >= 4:
                        pe.wait_ge(hid1_free, u - 3)
                    elif u >= 2:
                        pe.wait_ge(combined, 2 * NT * (B - 1) + NT)
                    elif mm == 0:
                        pe.wait_ge(gate4_ready, NT * B)
                    else:
                        pe.wait_ge(combined, 2 * NT * (B - 1) + NT)
                    if b == 0 and f == 0:
                        pe.wait_ge((tg_in, tu_in)[mm], 16 * KC)
                    if f == 0 and mm == 0:
                        for x in range(2):
                            last = norm_use(B + b, 2 + x)
                            pe.wait_ge(turn_free[last % 2], last // 2 + 1)
                T, (xh, xl) = (gate_w1, up_w1)[mm], XN1[b]
                for kc in range(2 * halfway, 2 * halfway + 2):
                    lhs = T[:, kc, f * P:(f + 1) * P]
                    nc.tensor.matmul(hid1_ps[u % 4][:, :], lhs, xh[:, kc, :], start=kc == 0, stop=False)
                    m = nc.tensor.matmul(hid1_ps[u % 4][:, :], lhs, xl[:, kc, :], start=False, stop=kc == KC - 1)
                if halfway:
                    m.then_inc(hid1_done, 1)

            def down_item(b, pr, f):
                d = down_number(b, pr, f)
                if d in (0, TD_PART):
                    pe.wait_ge(td_in[d > 0], 16)
                if f == 0:
                    pe.wait_ge(hid1_free, 2 * FC * (b + 1))
                pe.wait_ge(hs1_ready, d + 1)
                for t in range(2):
                    c = slice(t * P, (t + 1) * P)
                    nc.tensor.matmul(down1_ps[pr][t][:, :], hsH[d % HS][:, c], down_w1[:, f, :], start=f == 0, stop=False)
                    m = nc.tensor.matmul(down1_ps[pr][t][:, :], hsL[d % HS][:, c], down_w1[:, f, :], start=False, stop=f == FC - 1)
                m.then_inc(down1_used, 1)

            for step in STEPS1:
                kind = step[0]
                if kind == "item":
                    it = step[2]
                    if it[0] == "hid":
                        hidden_item(step[1], *it[1:])
                    else:
                        down_item(*it[1:])
                elif kind == "turn":
                    pe.wait_ge(combined, 2 * NT * (B - 1) + NT)
                    norm_turn(3)
                elif kind == "proj":
                    pe.wait_ge(win_ready, 1)
                    pe.wait_ge(combined, 2 * NT * B)
                    for x in range(2):
                        last = norm_use(3, 2 + x)
                        pe.wait_ge(turn_free[last % 2], last // 2 + 1)
                    for b in range(B):
                        cols = slice(64 * (1 - b), 64 * (1 - b) + P)
                        for kc in range(KC):
                            xh, xl = XN1[b]
                            m = passes(score_ps[0][:, :], winH[:, kc, cols], winL[:, kc, cols], xh[:, kc, :], xl[:, kc, :],
                                       b == 0 and kc == 0, b == 1 and kc == KC - 1)
                    m.then_inc(input_proj_done, 1)
                elif kind == "centre":
                    q = step[1]
                    pe.wait_ge(h_ready, q + 1)
                    nc.tensor.matmul(score_ps[0][:, :], centre_m[:, :], h_rows[:, :], start=True, stop=True).then_inc(ctr_ready, 1)
                elif kind == "var":
                    q = step[1]
                    pe.wait_ge(sq_ready, q + 1)
                    for t in range(NT):
                        m = nc.tensor.matmul(turn_ps[1][:, 2 * t:2 * t + 2], squares[:, t * P:(t + 1) * P], seq_mean[:, :], start=True, stop=True)
                    m.then_inc(var_ready, 1)
                elif kind == "rsT":
                    q = step[1]
                    pe.wait_ge(rs_ready, q + 1)
                    nc.tensor.transpose(turn_ps[1][0:8, P:2 * P], inv_std[:, :], ident[:, :]).then_inc(rst_ready, 1)
                elif kind == "spread":
                    q = step[1]
                    pe.wait_ge(rt_ready, q + 1)
                    if q == 0:
                        pe.wait_ge(small1_in, 80)
                    for t in range(NT):
                        m = nc.tensor.matmul(turn_ps[0][:, t * P:(t + 1) * P], sel[:, t, :], inv_std_T[:, :], start=True, stop=True)
                    m.then_inc(spread_done, 1)
                elif kind == "mlp":
                    q, fc = step[1:]
                    l = q // 2
                    pe.wait_ge(yn_ready, l + 1)
                    for b in range(B):
                        n = 4 * l + 2 * fc + b
                        if b == 0:
                            pe.wait_ge(centred_ready, q + 1)
                        if fc:
                            pe.wait_ge(mz_ready, n - 1)
                        rows = slice(64 * b, 64 * b + 64)
                        nc.tensor.matmul(score_ps[b][:, :], w1T[rows, l, fc * P:(fc + 1) * P], act_rows[rows, :], start=True, stop=True)\
                            .then_inc(mlp_ready, 1)
                elif kind == "mlpout":
                    l = step[1] // 2
                    pe.wait_ge(mu_ready, 4 * (l + 1))
                    for fc in range(2):
                        for b in range(B):
                            m = nc.tensor.matmul(turn_ps[1][64 * b:64 * b + 64, :], w2T[:, l, fc, :], mlp_silu[2 * fc + b][:, :],
                                                 start=fc == 0, stop=fc == 1, skip_group_check=True)
                    m.then_inc(o1_ready, 1)
            pe.wait_ge(yn_ready, DEPTH + 1)
            pe.wait_ge(mz_ready, 4 * DEPTH)
            for t in range(B * NT):
                b, i = divmod(t, NT)
                if t >= NT:
                    pe.wait_ge(gate1_ready, 2 * NT)
                rows = slice(64 * b, 64 * b + 64)
                nc.tensor.matmul(LAST_BANKS[t][:, :], act_rows[rows, i * P:(i + 1) * P], woT[rows, :], start=True, stop=True).then_inc(last_proj_done, 1)

        @block.scalar
        def _(act):
            def copy_out(n, dst):
                act.wait_ge(turned, n + 1)
                return nc.scalar.activation(dst, turn_ps[n % 2][:, :], ACT.Copy)

            def stack_out(b, g, i):
                t, p = divmod(i, 2)
                n = use(b, ("stack", g, i))
                copy_out(n, (q_stack, k_stack)[t][g % 2][:, p, :]).then_inc(turn_free[n % 2], 1)

            def load_rows(w, T, done, chunks):
                for kc in chunks:
                    act.dma_start(F32(T[:, kc, :]), arr_d[w][kc * P:(kc + 1) * P, :]).then_inc(done, 16)

            def magnitudes():
                act.wait_ge(wc_in, 48)
                for w in range(3):
                    nc.scalar.activation(tern_over[w][:, :], tern_w[w][:, :], ACT.Abs, accum_out=abs_sums[:, w:w + 1]).then_inc(asum_ready, 1)
            def norm_hi(k):
                for kc in range(KC):
                    copy_out(norm_use(k, kc), NORM[k][2][0][:, kc, :]).then_inc(xh_ready, 1)

            def split_hi(n):
                act.wait_ge(raw_in[n % RAW], 16 * (n // RAW + 1))
                if n >= SPLIT:
                    act.wait_ge(*unit_free(n - SPLIT))
                act.wait_ge(hi_done, n)
                nc.scalar.activation(w_hi[n % SPLIT][:, :], raw[n % RAW][:, :], ACT.Copy).then_inc(hi_done, 1)

            def ffn_tanh(b, w):
                if w % 2 == 0:
                    n = FC * b + w // 2
                    act.wait_ge(proj_done, FU * b + 12 + w + 1)
                    if n:
                        act.wait_ge(*(hidden(b, w - 2) if w else hidden(b - 1, 2 * FC - 2)))
                    else:
                        act.wait_ge(mask_ready, 2)
                    nc.scalar.activation(gate_tanh[:, :], proj_ps[0][:, :], ACT.Tanh, scale=0.5).then_inc(tanh_ready, 1)

            def stack_hi(b, t):
                act.wait_ge(qk_ready, 8 * (b + 1))
                n = 2 * GROUPS * b + t
                if b:
                    act.wait_ge(turned, use(b - 1, ("stack", GROUPS - 1, 2 * t + 1)) + 1)
                act.wait_ge(ts_hi, n)
                src, hi, _ = stacked(t, 0)
                nc.scalar.activation(hi, src, ACT.Copy).then_inc(ts_hi, 1)

            for u in range(2):
                split_hi(u)
            norm_hi(0)
            for u in range(2, RAW):
                split_hi(u)
            magnitudes()
            for b in range(B):
                for u in range(5 if b else RAW, HI_BY_ACT):
                    split_hi(UNITS * b + u)
                    if b == 0 and u == 10:
                        for w in range(3):
                            act.wait_ge(tern_ready, w + 1)
                            nc.scalar.activation(tern_pos[w][:, :], F32(tern_neg[w][:, :]), ACT.Copy, scale=-1.0).then_inc(wp_ready, 1)
                            act.wait_ge(wp_ready, w + 1)
                            for x, src in enumerate((tern_pos[w], tern_neg[w])):
                                act.dma_start(tern_d[w][x].rearrange("(p n) -> p n", p=P), F32(src[:, :])).then_inc(tern_stored, 16)
                for i in range(NT):
                    act.wait_ge(proj_done, FU * b + 9 + i)
                    if b == 0 and i == 0:
                        act.wait_ge(ones_set, 2)
                    nc.scalar.activation(V[:, i, :].rearrange("p (h c) -> p h c", c=32)[:, :, 0:D],
                                         QKV_BANKS[0][i][:, :].rearrange("p (h d) -> p h d", d=D), ACT.Copy).then_inc(v_written, 1)
                for t in range(2):
                    stack_hi(b, t)
                ffn_tanh(b, 0)
                for i in (0, 2):
                    stack_out(b, 0, i)
                if b == 0:
                    act.wait_ge(tern_stored, 96)
                for s in range(SLOTS):
                    if score_in(s):
                        j, i = score_in(s)
                        n = 5 * PAIRS * b + s
                        if i == 0 and j >= 2:
                            act.wait_ge(turned, use(b, ("p", j - 2, 4)) + 1)
                        act.wait_ge(min_ready, n + 1)
                        for x, (hh, qt, c) in enumerate(S_BANKS[i]):
                            w = P * (qt + 1)
                            e = nc.scalar.activation(probs[j % 2][:, hh, p_off(qt):p_off(qt) + w], score_ps[n % 3][:, c:c + w], ACT.Exp,
                                                     bias=row_min[:, j % 2, S_COL[i] + x:S_COL[i] + x + 1], scale=-1.0)
                        e.then_inc(probs_ready, 1)
                    for w in ffn_units_after(s):
                        ffn_tanh(b, w)
                    if stack_in(s) and stack_in(s)[1] % 2 == 0:
                        stack_out(b, *stack_in(s))
                    if down_in(s + 1) is not None:
                        f = down_in(s + 1)
                        act.wait_ge(*hidden(b, 2 * f + 1))
                        if f >= 2:
                            act.wait_ge(down_used, FC * b + f - 1)
                        nc.scalar.activation(hsh[f % 2][:, :], hidden_T[:, f, :], ACT.Copy).then_inc(hs_hi, 1)
                    for u in range(U_DOWN, UNITS):
                        if s == DOWN_HI[u - U_DOWN]:
                            split_hi(UNITS * b + u)
                    if turn_in(s) and turn_in(s)[1] in T_BY_ACT:
                        j, i = turn_in(s)
                        gp = PAIRS * b + j
                        if i == 0 and gp >= 3:
                            act.wait_ge(pv_done, (gp - 3) // 2 + 1)
                        n = use(b, ("p", j, i))
                        copy_out(n, probs_T[gp % 3][:, 512 * i:512 * i + 512]).then_inc(turn_free[n % 2], 1)
                    if pv_in(s) and pv_in(s)[1] == NT:
                        g = pv_in(s)[0]
                        act.wait_ge(pv_done, GROUPS * b + g + 1)
                        if g:
                            act.wait_ge(turned, use(b, ("ctx", g - 1)) + 1)
                        nc.scalar.activation(ctx_sums[:, :], ctx_ps[:, :], ACT.Copy).then_inc(ctx_copied, 1)
                    if s == 5 * PAIRS:
                        if b:
                            act.wait_ge(x2_stored, 16)
                        act.dma_start(x_next[:, :, :], (x2_d[0] if b else x_dram[1]).rearrange("t p e -> p t e")).then_inc(xb_in, 16)
                    if s == NORM_TURN:
                        norm_hi(b + 1)
                    if b == B - 1 and s == LAST_DOWN - 1:
                        load_rows(W_UP, up_w1, tu_in, range(KC - 1))
                        for dst, src in ((w1T[:, :, :], A["w1T"]), (w2T[:, :, :, :], A["w2T"]), (woT[:, :], A["woT"]),
                                         (sel[:, :, :], A["sel"]), (bout[:, :], A["bout"].partition_broadcast(P))):
                            act.dma_start(dst, src).then_inc(small1_in, 16)
                    if s == LAST_DOWN:
                        for kc in range(KC):
                            n = use(b, ("ctxf", kc))
                            act.wait_ge(turned, n + 1)
                            nc.scalar.activation(ctx_hi[:, kc, :], turn_ps[n % 2][:, :], ACT.Identity, bias=v_bias[:, kc:kc + 1]).then_inc(ct_hi, 1)
                    if b == B - 1 and s == 5 * PAIRS:
                        act.wait_ge(*copied(b, ("stack", GROUPS - 1, 3)))
                        act.wait_ge(arranged, 16 * len(ARRANGE))
                        load_rows(W_GATE, gate_w1, tg_in, range(KC))
                if b == B - 1:
                    act.wait_ge(turned, use(b, ("ctxf", KC - 1)) + 1)
                    load_rows(W_UP, up_w1, tu_in, [KC - 1])
                if b < B - 1:
                    split_hi(UNITS * (b + 1))
                act.wait_ge(down_used, FC * (b + 1))
                for i in OUT_TILES:
                    nc.scalar.activation(down_tanh[i][:, :], down_ps[i][:, :], ACT.Tanh, scale=0.25).then_inc(down_tanh_ready, 1)
                if b < B - 1:
                    for u in range(1, 5):
                        split_hi(UNITS * (b + 1) + u)
                if b == 0:
                    act.wait_ge(polar_ready, 1)
                    nc.scalar.activation(decay[:, :], polar_v[:, 7, :], ACT.Tanh).then_inc(decay_ready, 1)

            for step in STEPS1:
                kind = step[0]
                if kind == "item":
                    _, n, it = step
                    if it[0] == "hid" and it[3] == 0 and it[4] == 1:
                        _, b, f, _, _ = it
                        act.wait_ge(hid1_done, 2 * (FC * b + f) + 1)
                        n1 = FC * b + f
                        if n1 >= 2:
                            act.wait_ge(hid1_free, 2 * n1 - 3)
                        if b and f < 2:
                            act.wait_ge(gate1_ready, NT * b - 1 + f)
                        nc.scalar.activation(t1[f % 2][:, :], hid1_ps[2 * n1 % 4][:, :], ACT.Tanh, scale=scales[:, 0:1]).then_inc(t1_ready, 1)
                    nxt = items1()[n + AHEAD] if n + AHEAD < len(items1()) else None
                    if nxt and nxt[0] == "down":
                        _, b, pr, f = nxt
                        d = down_number(b, pr, f)
                        act.wait_ge(hid1_free, 2 * (FC * b + f) + 2)
                        if d >= HS:
                            act.wait_ge(down1_used, d - HS + 1)
                        nc.scalar.activation(hsH[d % HS][:, :], hidden1_T[:, f, 256 * pr:256 * pr + 256], ACT.Copy).then_inc(hs1_hi, 1)
                    if it[0] == "down" and it[3] == FC - 1:
                        _, b, pr, f = it
                        act.wait_ge(down1_used, down_number(b, pr, f) + 1)
                        for t in range(2):
                            n = 2 * (2 * b + pr) + t
                            act.wait_ge(hid1_free, 2 * FC * (b + 1))
                            if n >= 2:
                                act.wait_ge(gate1_ready, n - 1)
                            nc.scalar.activation(t1[t][:, :], down1_ps[pr][t][:, :], ACT.Tanh, scale=scales[:, 1:2]).then_inc(down1_tanh, 1)
                elif kind == "turn":
                    act.wait_ge(out_used, KC * B)
                    norm_hi(3)
                elif kind == "centre":
                    q = step[1]
                    act.wait_ge(ctr_ready, q + 1)
                    nc.scalar.activation(squares[:, :], score_ps[0][:, :], ACT.Square).then_inc(sq_ready, 1)
                    nc.scalar.activation(centred[:, :], score_ps[0][:, :], ACT.Copy).then_inc(centred_ready, 1)
                elif kind == "rsT":
                    q = step[1]
                    act.wait_ge(rst_ready, q + 1)
                    nc.scalar.activation(inv_std_T[:, :], turn_ps[1][0:8, P:2 * P], ACT.Copy).then_inc(rt_ready, 1)
                elif kind == "spread" and step[1] % 2 == 0 and step[1] < 2 * DEPTH:
                    q = step[1]
                    l = q // 2
                    act.wait_ge(y_ready, q + 1)
                    if q == 0:
                        act.wait_ge(vecs_ready, 4)
                    nc.scalar.activation(in_tanh[:, :], unit_rows[:, :], ACT.Tanh, bias=hln[:, 4 + l:5 + l], scale=hln[:, l:l + 1]).then_inc(tz_ready, 1)
                elif kind == "mlp":
                    q, fc = step[1:]
                    l = q // 2
                    for b in range(B):
                        n = 4 * l + 2 * fc + b
                        act.wait_ge(mlp_ready, n + 1)
                        if n >= 2:
                            act.wait_ge(mu_ready, n - 1)
                        c = 2 * l + fc
                        nc.scalar.activation(mlp_tanh[b][:, :], score_ps[b][:, :], ACT.Tanh, bias=hb1v[:, c:c + 1], scale=0.5).then_inc(mt_ready, 1)
                        nc.scalar.activation(mlp_biased[b][:, :], score_ps[b][:, :], ACT.Identity, bias=b1v[:, c:c + 1]).then_inc(mz_ready, 1)

            for n, t in enumerate(LAST_BY_POOL):
                act.wait_ge(last_proj_done, t + 1)
                act.wait_ge(gate1_ready, 2 * NT)
                if n == 0:
                    act.wait_ge(pre_ready, 3 * NT)
                nc.scalar.activation(last_s[n][:, :], LAST_BANKS[t][:, :], ACT.Copy, scale=scales[:, 1:2]).then_inc(s1_scaled, 1)

        @block.vector
        def _(dve):
            def minus_hi(n, dst, hi):
                nc.vector.tensor_tensor(dst, turn_ps[n % 2][:, :], F32(hi), ALU.subtract).then_inc(turn_free[n % 2], 1)

            def stack_out(b, g, i):
                t, p = divmod(i, 2)
                n = use(b, ("stack", g, i))
                dve.wait_ge(turned, n + 1)
                nc.vector.tensor_copy((q_stack, k_stack)[t][g % 2][:, p, :], turn_ps[n % 2][:, :]).then_inc(turn_free[n % 2], 1)

            def norm_stats(k):
                if k in (1, 2):
                    dve.wait_ge(xb_in, 16 * k)
                if k:
                    dve.wait_ge(xn_ready, NT * k)
                for t in range(NT):
                    if k == 0:
                        dve.wait_ge(x_in[t], 16)
                    nc.vector.bn_stats(stat[:, t, :], NORM[k][0][:, t, :]).then_inc(stats, 1)
                for t in range(NT):
                    dve.wait_ge(stats, NT * k + t + 1)
                    nc.vector.bn_aggr(mean_var[:, t, :], stat[:, t, :]).then_inc(mv_ready, 1)

            def norm_rows(k):
                dve.wait_ge(mv_ready, NT * (k + 1))
                dve.wait_ge(rstd_ready, k + 1)
                for t in range(NT):
                    nc.vector.tensor_scalar(NORM[k][1][:, t, :], NORM[k][0][:, t, :], mean_var[:, t, 0:1], rstd[:, t:t + 1],
                                            ALU.subtract, ALU.mult).then_inc(xn_ready, 1)

            def norm_lo(k):
                for kc in range(KC):
                    dve.wait_ge(xh_ready, KC * k + kc + 1)
                    minus_hi(norm_use(k, kc), NORM[k][2][1][:, kc, :], NORM[k][2][0][:, kc, :])

            def ffn_out(b, w):
                n = FC * b + w // 2
                dve.wait_ge(proj_done, FU * b + 12 + w + 1)
                if w % 2 == 0:
                    dve.wait_ge(tanh_ready, n + 1)
                    if n:
                        dve.wait_ge(*(hidden(b, w - 1) if w else hidden(b - 1, 2 * FC - 1)))
                    nc.vector.scalar_tensor_tensor(out=gate_silu[:, :], in0=gate_tanh[:, :], scalar=1.0, in1=proj_ps[0][:, :],
                                                   op0=ALU.add, op1=ALU.mult).then_inc(proj_free, 1)
                else:
                    dve.wait_ge(*hidden(b, w - 1))
                    nc.vector.tensor_tensor(hidden_T[:, w // 2, :], gate_silu[:, :], proj_ps[1][:, :], ALU.mult)\
                        .then_inc(proj_free, 1)

            def qk_bias(b, t, i):
                n, r = 4 * t + i, 8 * b + 4 * t + i
                dve.wait_ge(proj_done, FU * b + n + 1)
                if r >= 2:
                    dve.wait_ge(r1_ready, r - 1)
                    dve.wait_ge(r2_ready, 2 * (r - 1))
                nc.vector.tensor_tensor(qk_biased[r % 2][:, :], QKV_BANKS[t][i][:, :], qkv_bias[:, t * E:(t + 1) * E], ALU.add)\
                    .then_inc(proj_free, 1)

            def qk_turned_part(b, t, i):
                r = 8 * b + 4 * t + i
                dve.wait_ge(proj_free, FV * b + 4 * t + i + 1)
                if r:
                    dve.wait_ge(qk_ready, r)
                x4 = qk_biased[r % 2][:, :].rearrange("p (h c d) -> p h c d", c=2, d=D // 2)
                y4 = by_sin[:, :].rearrange("p (h c d) -> p h c d", c=2, d=D // 2)
                for c in range(2):
                    nc.vector.tensor_tensor(y4[:, :, c, :], x4[:, :, 1 - c, :],
                                            wide(rope[:, 2 * t + 1, i, c * 8:c * 8 + 8], H), ALU.mult).then_inc(r2_ready, 1)

            def qk_add(b, t, i):
                r = 8 * b + 4 * t + i
                dve.wait_ge(r2_ready, 2 * (r + 1))
                dve.wait_ge(r1_ready, r + 1)
                nc.vector.tensor_tensor(qk_rows[t][:, :, i, :], by_cos[r % 2][:, :].rearrange("p (g c) -> p g c", c=64),
                                        by_sin[:, :].rearrange("p (g c) -> p g c", c=64), ALU.add).then_inc(qk_ready, 1)

            norm_stats(0)
            norm_rows(0)
            norm_lo(0)
            dve.wait_ge(const_in, 80)
            nc.vector.tensor_copy(maskL[:, :], gate_tanh[:, 0:P]).then_inc(mask_ready, 1)
            nc.vector.tensor_copy(maskR[:, :], gate_tanh[:, P:2 * P]).then_inc(mask_ready, 1)
            for b in range(B):
                if b == 0:
                    dve.wait_ge(tot_ready, 1)
                    mean = 1.0 / (OCT * H8 * C1)
                    nc.vector.tensor_scalar(theta[:, 0, :], ctx_ps[:, 0:3], mean, 0.5, ALU.mult, ALU.mult).then_inc(theta_ready, 1)
                    nc.vector.tensor_scalar(theta[:, 1, :], ctx_ps[:, 0:3], mean, -0.5, ALU.mult, ALU.mult).then_inc(theta_ready, 1)
                    dve.wait_ge(theta_ready, 2)
                    nc.vector.tensor_copy(scales[:, 0:1], theta[:, 0, 0:1]).then_inc(scale_ready, 1)
                    nc.vector.tensor_tensor(scales[:, 2:3], theta[:, 0, 0:1], theta[:, 0, 1:2], ALU.mult).then_inc(scale_ready, 1)
                    dve.wait_ge(scale_ready, 2)
                    nc.vector.tensor_scalar(scales[:, 1:2], scales[:, 2:3], theta[:, 0, 2:3], 2.0, ALU.mult, ALU.mult).then_inc(scale_ready, 1)
                    for w in range(3):
                        nc.vector.tensor_scalar(tern_over[w][:, :], tern_w[w][:, :], theta[:, 0, w:w + 1], None, ALU.is_gt).then_inc(tern_a, 1)
                        dve.wait_ge(tern_a, w + 1)
                        nc.vector.scalar_tensor_tensor(out=tern_neg[w][:, :], in0=tern_w[w][:, :], scalar=theta[:, 1, w:w + 1], in1=tern_over[w][:, :],
                                                       op0=ALU.is_lt, op1=ALU.subtract).then_inc(tern_ready, 1)
                for t in range(2):
                    qk_bias(b, t, 0)
                    for i in range(NT):
                        qk_turned_part(b, t, i)
                        if i + 1 < NT:
                            qk_bias(b, t, i + 1)
                        qk_add(b, t, i)
                ffn_out(b, 0)
                ffn_out(b, 1)
                for i in (1, 3):
                    stack_out(b, 0, i)
                for s in range(SLOTS):
                    if score_in(s):
                        j, i = score_in(s)
                        n = 5 * PAIRS * b + s
                        dve.wait_ge(score_done, n + 1)
                        col = S_COL[i]
                        if i == 2:
                            m = nc.vector.tensor_reduce(row_min[:, j % 2, col:col + 2], score_ps[n % 3][:, :].rearrange("p (a c) -> p a c", a=2),
                                                        AX.X, ALU.min)
                        else:
                            for x, (hh, qt, c) in enumerate(S_BANKS[i]):
                                m = nc.vector.tensor_reduce(row_min[:, j % 2, col + x:col + x + 1], score_ps[n % 3][:, c:c + P * (qt + 1)],
                                                            AX.X, ALU.min)
                        m.then_inc(min_ready, 1)
                    if ctx_in(s) is not None:
                        g = ctx_in(s)
                        n = use(b, ("ctx", g))
                        dve.wait_ge(turned, n + 1)
                        c3 = turn_ps[n % 2][:, :].rearrange("p (n c) -> p n c", c=32)
                        if g:
                            dve.wait_ge(*copied(b, ("ctx", g - 1)))
                        nc.vector.reciprocal(rinv[:, :], c3[:, :, D]).then_inc(rinv_ready, 1)
                        dve.wait_ge(rinv_ready, GROUPS * b + g + 1)
                        nc.vector.tensor_tensor(ctx_rows[:, :, g * 64:(g + 1) * 64].rearrange("p t (h d) -> p t h d", d=D),
                                                c3[:, :, 0:D].rearrange("p (t h) d -> p t h d", t=NT),
                                                rinv[:, :].rearrange("p (t h) -> p t h", t=NT).unsqueeze(3).broadcast_to([P, NT, 4, D]),
                                                ALU.mult).then_inc(turn_free[n % 2], 1)
                    for w in ffn_units_after(s):
                        ffn_out(b, w)
                    if stack_in(s) and stack_in(s)[1] % 2 == 1:
                        stack_out(b, *stack_in(s))
                    if down_in(s + 1) is not None:
                        f = down_in(s + 1)
                        dve.wait_ge(hs_hi, FC * b + f + 1)
                        nc.vector.tensor_tensor(hsl[f % 2][:, :], hidden_T[:, f, :], F32(hsh[f % 2][:, :]), ALU.subtract).then_inc(hs_ready, 1)
                    if turn_in(s) and turn_in(s)[1] not in T_BY_ACT:
                        j, i = turn_in(s)
                        gp = PAIRS * b + j
                        if i == 1 and gp == 0:
                            dve.wait_ge(tern_stored, 96)
                        if i == 1 and gp >= 3:
                            dve.wait_ge(pv_done, (gp - 3) // 2 + 1)
                        n = use(b, ("p", j, i))
                        dve.wait_ge(turned, n + 1)
                        nc.vector.tensor_copy(probs_T[gp % 3][:, 512 * i:512 * i + 512], turn_ps[n % 2][:, :])\
                            .then_inc(turn_free[n % 2], 1)
                    if s == NORM_STATS:
                        norm_stats(b + 1)
                    if s == NORM_ROWS:
                        norm_rows(b + 1)
                    if s == NORM_TURN:
                        norm_lo(b + 1)
                    if s == LAST_DOWN:
                        for kc in range(KC):
                            dve.wait_ge(ct_hi, KC * b + kc + 1)
                            n = use(b, ("ctxf", kc))
                            nc.vector.scalar_tensor_tensor(out=ctx_lo[:, kc, :], in0=turn_ps[n % 2][:, :], scalar=v_bias[:, kc:kc + 1],
                                                           in1=F32(ctx_hi[:, kc, :]), op0=ALU.add, op1=ALU.subtract).then_inc(turn_free[n % 2], 1)
                for t in range(NT):
                    dve.wait_ge(x_in[t], 16 * (b + 1))
                for x, i in enumerate(OUT_TILES):
                    n = NT * b + x
                    dve.wait_ge(down_tanh_ready, n + 1)
                    nc.vector.scalar_tensor_tensor(out=gate4[i][:, :], in0=down_tanh[i][:, :], scalar=1.0, in1=down_ps[i][:, :],
                                                   op0=ALU.add, op1=ALU.mult).then_inc(gate4_ready, 1)
                for x, i in enumerate(OUT_TILES):
                    n = NT * b + x
                    dve.wait_ge(gate4_ready, n + 1)
                    nc.vector.tensor_tensor(down_tanh[i][:, :], gate4[i][:, :], out_bias[:, :], ALU.mult).then_inc(bias_step, 1)
                for x, i in enumerate(OUT_TILES):
                    n = NT * b + x
                    dve.wait_ge(bias_step, 2 * NT * b + x + 1)
                    nc.vector.scalar_tensor_tensor(out=X[:, i, :], in0=down_tanh[i][:, :], scalar=0.25, in1=X[:, i, :],
                                                   op0=ALU.mult, op1=ALU.add).then_inc(bias_step, 1)
                for x, i in enumerate(OUT_TILES):
                    dve.wait_ge(*((out_done, (NT - 1) * b + x + 1) if x < NT - 1 else (out_used, KC * (b + 1))))
                    nc.vector.tensor_tensor(gate4[i][:, :], gate4[i][:, :], out_ps[x][:, :], ALU.mult).then_inc(combined, 1)
                for x, i in enumerate(OUT_TILES):
                    dve.wait_ge(combined, 2 * NT * b + x + 1)
                    dve.wait_ge(bias_step, 2 * NT * b + NT + x + 1)
                    nc.vector.scalar_tensor_tensor(out=X[:, i, :], in0=gate4[i][:, :], scalar=0.25, in1=X[:, i, :],
                                                   op0=ALU.mult, op1=ALU.add).then_inc(combined, 1)

            steps = [0]

            def step_done(ins):
                steps[0] += 1
                ins.then_inc(conv_step, 1)
                dve.wait_ge(conv_step, steps[0])

            dve.wait_ge(combined, 2 * NT * B)
            nc.vector.tensor_scalar(hln[:, :], vec[:, V_LN1:V_LN1 + 8], 0.5, None, ALU.mult).then_inc(vecs_ready, 1)
            nc.vector.tensor_scalar(hscl[:, :], vec[:, V_SCL:V_SCL + 4], 0.5, None, ALU.mult).then_inc(vecs_ready, 1)
            nc.vector.tensor_scalar(init[:, 0, :], vec[:, V_LRE:V_LRE + 4], 2.0, None, ALU.mult).then_inc(vecs_ready, 1)
            nc.vector.tensor_scalar(hb1v[:, :], b1v[:, :], 0.5, None, ALU.mult).then_inc(vecs_ready, 1)
            step_done(nc.vector.tensor_scalar(init[:, 1, :], vec[:, V_LIM:V_LIM + 4], -2.0, None, ALU.mult))
            dve.wait_ge(vecs_ready, 4)

            def normed(q):
                dve.wait_ge(spread_done, q + 1)
                dve.wait_ge(centred_ready, q + 1)
                nc.vector.tensor_tensor(unit_rows[:, :], centred[:, :], turn_ps[0][:, :], ALU.mult).then_inc(y_ready, 1)
                dve.wait_ge(y_ready, q + 1)

            for step in STEPS1:
                kind = step[0]
                if kind == "item":
                    _, n, it = step
                    if it[0] == "hid" and it[4] == 1:
                        _, b, f, mm, _ = it
                        u = 2 * (FC * b + f) + mm
                        dve.wait_ge(hid1_done, u + 1)
                        if mm == 0:
                            dve.wait_ge(t1_ready, FC * b + f + 1)
                            if u:
                                dve.wait_ge(hid1_free, u)
                            nc.vector.scalar_tensor_tensor(out=ab1[f % 2][:, :], in0=t1[f % 2][:, :], scalar=1.0, in1=hid1_ps[u % 4][:, :],
                                                           op0=ALU.add, op1=ALU.mult).then_inc(hid1_free, 1)
                        else:
                            dve.wait_ge(hid1_free, u)
                            if b == 1:
                                dve.wait_ge(hs1_ready, FC + f + 1)
                            nc.vector.tensor_tensor(hidden1_T[:, f, :], ab1[f % 2][:, :], hid1_ps[u % 4][:, :], ALU.mult).then_inc(hid1_free, 1)
                    if it[0] == "down" and it[3] == FC - 1:
                        _, b, pr, f = it
                        for t in range(2):
                            n = 2 * (2 * b + pr) + t
                            dve.wait_ge(down1_tanh, n + 1)
                            if b == 1:
                                dve.wait_ge(input_proj_done, 1)
                            nc.vector.scalar_tensor_tensor(out=gate1[b][:, 2 * pr + t, :], in0=t1[t][:, :], scalar=1.0, in1=down1_ps[pr][t][:, :],
                                                           op0=ALU.add, op1=ALU.mult).then_inc(gate1_ready, 1)
                        for t in range(2 * b):
                            n = 2 * (2 * b + pr) + t
                            dve.wait_ge(gate1_ready, n + 1)
                            nc.vector.scalar_tensor_tensor(out=ab1[t][:, :], in0=gate1[b][:, 2 * pr + t, :], scalar=scales[:, 1:2],
                                                           in1=bout[:, :], op0=ALU.mult, op1=ALU.mult).then_inc(bias1, 1)
                        for t in range(2 * b):
                            dve.wait_ge(bias1, 4 * pr + t + 1)
                            nc.vector.tensor_tensor(X2[b][:, 2 * pr + t, :], X2[b][:, 2 * pr + t, :], ab1[t][:, :], ALU.add).then_inc(bias1, 1)
                elif kind == "norm":
                    norm_stats(3)
                elif kind == "rows":
                    norm_rows(3)
                elif kind == "turn":
                    norm_lo(3)
                elif kind == "proj":
                    dve.wait_ge(input_proj_done, 1)
                    nc.vector.tensor_scalar(h_rows[:, :], score_ps[0][:, :], vec[:, V_BIN:V_BIN + 1], None, ALU.add).then_inc(h_ready, 1)
                elif kind == "var":
                    q = step[1]
                    dve.wait_ge(var_ready, q + 1)
                    nc.vector.tensor_scalar(var_eps[:, :], turn_ps[1][:, 0:8], EPS, None, ALU.add).then_inc(ve_ready, 1)
                elif kind == "spread":
                    q = step[1]
                    l = q // 2
                    normed(q)
                    if q == 2 * DEPTH:
                        nc.vector.tensor_scalar(act_rows[:, :], unit_rows[:, :], vec[:, V_LNL:V_LNL + 1], vec[:, V_LNL + 1:V_LNL + 2],
                                                ALU.mult, ALU.add).then_inc(yn_ready, 1)
                    elif q % 2 == 0:
                        C, Sn = rotation[l % 2][:, 0, :], rotation[l % 2][:, 1, :]
                        step_done(nc.vector.tensor_scalar(in_affine[:, :], unit_rows[:, :], vec[:, V_LN1 + l:V_LN1 + l + 1],
                                                          vec[:, V_LN1 + 4 + l:V_LN1 + 5 + l], ALU.mult, ALU.add))
                        dve.wait_ge(tz_ready, l + 1)
                        step_done(nc.vector.scalar_tensor_tensor(out=act_rows[:, :], in0=in_tanh[:, :], scalar=1.0, in1=in_affine[:, :],
                                                                 op0=ALU.add, op1=ALU.mult))
                        dve.wait_ge(tab_step, 37 * (l + 1))
                        nc.vector.tensor_tensor(re_rows[:, :], act_rows[:, :], C, ALU.mult).then_inc(conv_step, 1)
                        steps[0] += 1
                        if l == 0:
                            dve.wait_ge(decay_ready, 1)
                        r = decay[:, l:l + 1].broadcast_to([P, S])
                        dve.wait_ge(conv_step, steps[0])
                        nc.vector.tensor_tensor_scan(re_state[:, :], r, re_rows[:, :], init[:, 0, l:l + 1], ALU.mult, ALU.add).then_inc(conv_step, 1)
                        dve.wait_ge(im_ready, 2 * l + 1)
                        nc.vector.tensor_tensor_scan(im_state[:, :], r, im_rows[:, :], init[:, 1, l:l + 1], ALU.mult, ALU.add).then_inc(im_state_ready, 1)
                        steps[0] += 1
                        dve.wait_ge(conv_step, steps[0])
                        step_done(nc.vector.tensor_tensor(re_rows[:, :], re_state[:, :], C, ALU.mult))
                        dve.wait_ge(im_ready, 2 * l + 2)
                        step_done(nc.vector.tensor_tensor(re_state[:, :], re_rows[:, :], im_rows[:, :], ALU.add))
                        nc.vector.scalar_tensor_tensor(out=h_rows[:, :], in0=re_state[:, :], scalar=hscl[:, l:l + 1], in1=h_rows[:, :],
                                                       op0=ALU.mult, op1=ALU.add).then_inc(h_ready, 1)
                    else:
                        nc.vector.tensor_scalar(act_rows[:, :], unit_rows[:, :], vec[:, V_LN2 + l:V_LN2 + l + 1],
                                                vec[:, V_LN2 + 4 + l:V_LN2 + 5 + l], ALU.mult, ALU.add).then_inc(yn_ready, 1)
                        dve.wait_ge(h_ready, q + 1)
                        nc.vector.tensor_scalar(h_with_b2[:, :], h_rows[:, :], vec[:, V_B2 + l:V_B2 + l + 1], None, ALU.add).then_inc(hb_ready, 1)
                elif kind == "mlp":
                    q, fc = step[1:]
                    l = q // 2
                    for b in range(B):
                        n = 4 * l + 2 * fc + b
                        dve.wait_ge(mt_ready, n + 1)
                        dve.wait_ge(mz_ready, n + 1)
                        nc.vector.scalar_tensor_tensor(out=mlp_silu[2 * fc + b][:, :], in0=mlp_tanh[b][:, :], scalar=1.0, in1=mlp_biased[b][:, :],
                                                       op0=ALU.add, op1=ALU.mult).then_inc(mu_ready, 1)
                elif kind == "mlpout":
                    l = step[1] // 2
                    dve.wait_ge(o1_ready, l + 1)
                    dve.wait_ge(hb_ready, l + 1)
                    nc.vector.scalar_tensor_tensor(out=h_rows[:, :], in0=turn_ps[1][:, :], scalar=0.5, in1=h_with_b2[:, :],
                                                   op0=ALU.mult, op1=ALU.add).then_inc(h_ready, 1)
            for n, t in enumerate(t for t in range(B * NT) if t not in LAST_BY_POOL):
                b, i = divmod(t, NT)
                dve.wait_ge(last_proj_done, t + 1)
                dve.wait_ge(*((bias1, 2 * NT) if b else (pre_ready, 3 * NT)))
                nc.vector.scalar_tensor_tensor(out=gate1[b][:, i, :], in0=gate1[b][:, i, :], scalar=scales[:, 1:2], in1=LAST_BANKS[t][:, :],
                                               op0=ALU.mult, op1=ALU.mult).then_inc(s1_ready, 1)
                dve.wait_ge(s1_ready, n + 1)
                nc.vector.tensor_tensor(X2[b][:, i, :], X2[b][:, i, :], gate1[b][:, i, :], ALU.add).then_inc(fin, 1)


S_COL = [0, 1, 3, 5, 6]


V_BIN, V_LN1, V_RE, V_IM, V_LRE, V_LIM, V_SCL, V_LN2, V_B2, V_LNL, NVEC = 0, 1, 9, 13, 17, 21, 25, 29, 37, 41, 43


def constants():
    half = D // 2
    inv_freq = (1.0 / np.float32(10000.0) ** (np.arange(half, dtype=np.float32) / np.float32(half))).astype(np.float32)
    ang = (np.arange(S, dtype=np.float32)[:, None] * inv_freq[None, :]).astype(np.float32)
    cos, sin = np.cos(ang).astype(np.float32), np.sin(ang).astype(np.float32)
    c2, s2 = np.concatenate([cos, cos], 1), np.concatenate([-sin, sin], 1)
    scale = np.float32(-0.25)
    rope = np.stack([c2 * scale, s2 * scale, c2, s2])
    rope = np.ascontiguousarray(rope.reshape(4, NT, P, D).transpose(2, 0, 1, 3))
    return {
        "ident": np.eye(P, dtype=np.float32),
        "rope": rope.astype(np.float32),
        "centre": np.kron(np.eye(B), np.eye(C1) - 1.0 / C1).astype(np.float32),
        "seq_mean": (np.kron(np.eye(B), np.ones((C1, 1))) / C1).astype(np.float32),
        "sel": np.stack([[np.repeat(np.arange(B) + 2 * t == r, C1) for t in range(NT)] for r in range(8)]).astype(np.float32),
        "zeros": np.zeros((HCOLS - HID1) * E, np.float32),
        "mask": np.concatenate([np.eye(P) * MASK_L, np.triu(np.ones((P, P)), 1) * MASK_R], 1).astype(np.float32),
    }


def layout(inputs):
    x = np.asarray(inputs["L0_attn_hidden_states"]).reshape(B, NT, P, E)
    w_qkv = np.asarray(inputs["L0_attn_qkv_w"])
    units = np.zeros((UNITS, P, 512), np.float32)
    for t in range(3):
        for kc in range(KC):
            units[U_QKV + 4 * t + kc] = w_qkv[kc * P:(kc + 1) * P, t * E:(t + 1) * E]
    for m, name in enumerate(("L0_ffn_W_gate", "L0_ffn_W_up")):
        w = np.asarray(inputs[name])
        pad = np.zeros((FC * P, E), np.float32)
        pad[:w.shape[0]] = w
        u = pad.reshape(FC, P, KC, P).transpose(0, 3, 2, 1)
        units[U_FFN + m:U_DOWN:2] = u.reshape(FC, P, 512)
    w = np.asarray(inputs["L0_ffn_W_down"])
    pad = np.zeros((FC * P, E), np.float32)
    pad[:w.shape[1]] = w.T
    units[U_DOWN:U_OUT] = pad.reshape(FC, P, E)
    units[U_OUT:] = np.asarray(inputs["L0_attn_out_w"]).reshape(KC, P, E)
    g = {k[8:]: np.asarray(v) for k, v in inputs.items() if k.startswith("L1_attn_")}
    v4 = [g[k].T for k in ("ln1_w", "ln1_b", "phz_re", "phz_im", "lc_re", "lc_im", "sc_lin", "ln2_w", "ln2_b", "b2")]
    vec = np.concatenate([g["bin"][:, None], *v4, g["lnl_w"][:, None], g["lnl_b"][:, None]], 1)
    win = np.zeros((P, KC, 192), np.float32)
    win[:, :, 64:128] = g["Win"].T.reshape(KC, P, C1).transpose(1, 0, 2)
    block1 = {
        "vec": np.concatenate([vec, vec], 0),
        "b1v": np.ascontiguousarray(g["b1"].reshape(DEPTH, 2, P).transpose(2, 0, 1).reshape(P, 2 * DEPTH)),
        "win": win,
        "w1T": np.concatenate([g["W1"].transpose(2, 0, 1)] * 2, 0),
        "w2T": np.ascontiguousarray(g["W2"].transpose(2, 0, 1).reshape(2, P, DEPTH, C1).transpose(1, 2, 0, 3)),
        "woT": np.concatenate([g["Wout"].T] * 2, 0),
        "bout": g["bout"],
        "tern_w": np.stack([np.asarray(inputs["L1_ffn_" + k]).transpose(0, 2, 1).reshape(P, FLAT) for k in ("w_gate", "w_up", "w_down")]),
    }
    return {
        **block1,
        "x": np.ascontiguousarray(x), "w0": units,
        "qk_bias": np.asarray(inputs["L0_attn_qkv_b"])[:2 * E],
        "v_bias": np.ascontiguousarray(np.asarray(inputs["L0_attn_qkv_b"])[2 * E:].reshape(KC, P).T),
        "out_b": np.asarray(inputs["L0_attn_out_b"]),
    }


def kernel(**inputs):
    import concourse.bacc as bacc
    from concourse.bass_utils import run_bass_kernel_spmd

    nc = bacc.Bacc("TRN2", target_bir_lowering=False, num_devices=1)
    arrays = {name: np.ascontiguousarray(a) for name, a in {**layout(inputs), **constants()}.items()}
    A = {name: nc.dram_tensor(name, a.shape, mybir.dt.from_np(a.dtype), kind="ExternalInput").ap() for name, a in arrays.items()}
    out = nc.dram_tensor("out", (B, NT, P, E), f32, kind="ExternalOutput").ap()
    program(nc, A, out)
    r = run_bass_kernel_spmd(nc, [arrays], core_ids=[0])
    return r.results[0]["out"].reshape(B, S, E)
```
